# Optimizing a Trainium2 kernel written in Bass

```python
import numpy as np
import jax
import jax.numpy as jnp

def _softmax(x, axis=-1):
    return jax.nn.softmax(x, axis=axis)

def _gelu(x):
    return jax.nn.gelu(x, approximate=True)

def _silu(x):
    return jax.nn.silu(x)

def _sigmoid(x):
    return jax.nn.sigmoid(x)

def _layernorm(x, axis=-1, eps=1e-05):
    m = jnp.mean(x, axis=axis, keepdims=True)
    v = jnp.var(x, axis=axis, keepdims=True)
    return (x - m) / jnp.sqrt(v + eps)

def _scatter_add(tgt, idx, src, axis=0):
    return tgt.at[idx].add(src)

def _segment_sum(src, seg, n):
    return jax.ops.segment_sum(src, seg, n)
kernel_name = 'mk_seq_postln_d2_jaxref_r8_355587'

def setup_inputs(seed: int=0):
    np.random.seed(seed)
    _w = jnp.asarray

    def _L0_attn_setup():
        import jax, jax.numpy as jnp
        import numpy as np
        D_MODEL = 128
        D_STATE = 128
        D_CONV = 4
        EXPAND = 2
        HEADDIM = 64
        D_INNER = D_MODEL * EXPAND
        NHEADS = D_INNER // HEADDIM
        CONV_DIM = D_INNER + 2 * D_STATE
        D_IN_PROJ = 2 * D_INNER + 2 * D_STATE + NHEADS
        POOL = 50
        SDIM = 64
        HEAD_DIM_RET = SDIM // 4
        TAU1 = 0.5
        TAU2 = 0.3
        HID = D_MODEL // 4
        B = 4
        T = 256
        EPS = 1e-05

        def _rmsnorm(x, w):
            return x * jax.lax.rsqrt(jnp.mean(x * x, axis=-1, keepdims=True) + EPS) * w

        def _mamba2(x, in_w, conv_w, conv_b, dt_bias, A_log, D_param, gnorm_w, out_w):
            Bn, Tn, _ = x.shape
            zxbcdt = x @ in_w.T
            z = zxbcdt[..., :D_INNER]
            xBC = zxbcdt[..., D_INNER:D_INNER + CONV_DIM]
            dt = zxbcdt[..., D_INNER + CONV_DIM:]
            xp = jnp.pad(jnp.transpose(xBC, (0, 2, 1)), ((0, 0), (0, 0), (D_CONV - 1, 0)))
            conv = jax.lax.conv_general_dilated(xp, conv_w[:, None, :], (1,), 'VALID', dimension_numbers=('NCH', 'OIH', 'NCH'), feature_group_count=CONV_DIM)
            xBC = jax.nn.silu(jnp.transpose(conv, (0, 2, 1)) + conv_b)
            xs = xBC[..., :D_INNER].reshape(Bn, Tn, NHEADS, HEADDIM)
            Bm = xBC[..., D_INNER:D_INNER + D_STATE]
            Cm = xBC[..., D_INNER + D_STATE:]
            dt = jax.nn.softplus(dt + dt_bias)
            A = -jnp.exp(A_log)
            dA = jnp.exp(dt * A)
            dtx = dt[..., None] * xs

            def step(h, inp):
                dA_t, dtx_t, B_t, C_t = inp
                h = h * dA_t[:, :, None, None] + dtx_t[..., None] * B_t[:, None, None, :]
                y = jnp.einsum('bhpn,bn->bhp', h, C_t)
                return (h, y)
            tm = lambda a: jnp.moveaxis(a, 1, 0)
            h0 = jnp.zeros((Bn, NHEADS, HEADDIM, D_STATE), x.dtype)
            _, ys = jax.lax.scan(step, h0, (tm(dA), tm(dtx), tm(Bm), tm(Cm)))
            y = jnp.moveaxis(ys, 0, 1) + D_param[None, None, :, None] * xs
            y = y.reshape(Bn, Tn, D_INNER)
            y = _rmsnorm(y * jax.nn.silu(z), gnorm_w)
            return y @ out_w.T

        def _update_memory(tokens, imp, summ_w, pool, prio, counts):
            Bn, Tn, Dm = tokens.shape
            S = min(Tn, POOL)
            order = jnp.argsort(-imp, axis=1)[:, :S]
            s_imp = jnp.take_along_axis(imp, order, axis=1)
            s_tok = jnp.take_along_axis(tokens, order[..., None], axis=1)
            s_sum = s_tok @ summ_w.T
            s_mask = s_imp > TAU1
            ar = jnp.arange(Bn)

            def body(carry, inp):
                pool, prio, counts = carry
                hi, si, ss = inp
                add = hi & (counts < POOL)
                idx = jnp.minimum(counts, POOL - 1)
                pool = pool.at[ar, idx].set(jnp.where(add[:, None], ss, pool[ar, idx]))
                prio = prio.at[ar, idx].set(jnp.where(add, si, prio[ar, idx]))
                counts = counts + add.astype(counts.dtype)
                repl = hi & (counts >= POOL)
                mi = jnp.argmin(prio, axis=1)
                should = repl & (si > prio[ar, mi])
                pool = pool.at[ar, mi].set(jnp.where(should[:, None], ss, pool[ar, mi]))
                prio = prio.at[ar, mi].set(jnp.where(should, si, prio[ar, mi]))
                return ((pool, prio, counts), None)
            xs = (jnp.moveaxis(s_mask, 1, 0), jnp.moveaxis(s_imp, 1, 0), jnp.moveaxis(s_sum, 1, 0))
            (pool, prio, counts), _ = jax.lax.scan(body, (pool, prio, counts), xs)
            return (pool, prio, counts)
        key = jax.random.key(seed)
        ks = jax.random.split(key, 16)

        def w(k, shape, fan_in):
            return jax.random.normal(k, shape, dtype=jnp.float32) / np.float32(np.sqrt(fan_in))
        inp = {}
        inp['x'] = jax.random.normal(ks[0], (B, T, D_MODEL), dtype=jnp.float32)
        inp['norm_w'] = jnp.ones((D_MODEL,), jnp.float32)
        inp['in_w'] = w(ks[1], (D_IN_PROJ, D_MODEL), D_MODEL)
        inp['conv_w'] = w(ks[2], (CONV_DIM, D_CONV), D_CONV)
        inp['conv_b'] = jnp.zeros((CONV_DIM,), jnp.float32)
        inp['dt_bias'] = jnp.log(jnp.expm1(jax.random.uniform(ks[3], (NHEADS,), minval=0.001, maxval=0.1))).astype(jnp.float32)
        inp['A_log'] = jnp.log(jax.random.uniform(ks[4], (NHEADS,), minval=1.0, maxval=16.0)).astype(jnp.float32)
        inp['D_param'] = jnp.ones((NHEADS,), jnp.float32)
        inp['gnorm_w'] = jnp.ones((D_INNER,), jnp.float32)
        inp['out_w'] = w(ks[5], (D_MODEL, D_INNER), D_INNER)
        inp['scorer_w1'] = w(ks[6], (HID, D_MODEL), D_MODEL)
        inp['scorer_w2'] = w(ks[7], (1, HID), HID)
        inp['summ_w'] = w(ks[8], (SDIM, D_MODEL), D_MODEL)
        inp['q_w'] = w(ks[9], (SDIM, D_MODEL), D_MODEL)
        inp['k_w'] = w(ks[10], (SDIM, SDIM), SDIM)
        inp['v_w'] = w(ks[11], (D_MODEL, SDIM), SDIM)
        inp['gate_w'] = w(ks[12], (D_MODEL, 2 * D_MODEL), 2 * D_MODEL)
        return inp
    _L0_attn_in = _L0_attn_setup()

    def _L0_ffn_setup():
        import jax, jax.numpy as jnp
        import numpy as np
        H = 128
        I = 256
        E = 8
        B, S = (2, 512)
        EPS = 1e-05
        INIT = 0.02

        def _layernorm(x, w, b):
            mu = jnp.mean(x, axis=-1, keepdims=True)
            var = jnp.mean(jnp.square(x - mu), axis=-1, keepdims=True)
            return (x - mu) * jax.lax.rsqrt(var + EPS) * w + b
        key = jax.random.key(seed)
        ks = jax.random.split(key, 9)
        return {'hidden_states': jax.random.normal(ks[0], (B, S, H), jnp.float32), 'ln_w': jnp.ones((H,), jnp.float32), 'ln_b': jnp.zeros((H,), jnp.float32), 'router_w': jax.random.normal(ks[1], (H, E), jnp.float32) * INIT, 'gate_w': jax.random.normal(ks[2], (E, H, I), jnp.float32) * INIT, 'up_w': jax.random.normal(ks[3], (E, H, I), jnp.float32) * INIT, 'down_w': jax.random.normal(ks[4], (E, I, H), jnp.float32) * INIT, 'sh_gate': jax.random.normal(ks[5], (H, I), jnp.float32) * INIT, 'sh_up': jax.random.normal(ks[6], (H, I), jnp.float32) * INIT, 'sh_down': jax.random.normal(ks[7], (I, H), jnp.float32) * INIT}
    _L0_ffn_in = _L0_ffn_setup()

    def _L1_attn_setup():
        import jax, jax.numpy as jnp
        import numpy as np
        import math
        NUM_HEADS = 16

        def get_slopes(n):

            def pow2(n):
                start = 2 ** (-2 ** (-(math.log2(n) - 3)))
                return [start * start ** i for i in range(n)]
            if math.log2(n).is_integer():
                return pow2(n)
            c = 2 ** math.floor(math.log2(n))
            return pow2(c) + get_slopes(2 * c)[0::2][:n - c]
        key = jax.random.key(seed)
        ks = jax.random.split(key, 5)
        B, T, C = (2, 256, 128)
        return {'x': jax.random.normal(ks[0], (B, T, C), dtype=jnp.float32), 'W_qkv': jax.random.normal(ks[1], (C, 3 * C), dtype=jnp.float32) * 0.02, 'b_qkv': jax.random.normal(ks[2], (3 * C,), dtype=jnp.float32) * 0.02, 'W_proj': jax.random.normal(ks[3], (C, C), dtype=jnp.float32) * 0.02, 'b_proj': jax.random.normal(ks[4], (C,), dtype=jnp.float32) * 0.02}
    _L1_attn_in = _L1_attn_setup()

    def _L1_ffn_setup():
        import jax, jax.numpy as jnp
        import numpy as np
        TOP_K = 2
        E = 8
        D = 128
        F = 256
        B, S = (2, 128)
        key = jax.random.key(seed)
        ks = jax.random.split(key, 8)
        sc = 0.02
        return {'x_bsD': jax.random.normal(ks[0], (B, S, D), dtype=jnp.float32), 'router_DE': jax.random.normal(ks[1], (D, E), dtype=jnp.float32) * sc, 'w_in_shared_FD': jax.random.normal(ks[2], (F, D), dtype=jnp.float32) * sc, 'w_out_shared_DF': jax.random.normal(ks[3], (D, F), dtype=jnp.float32) * sc, 'w_swiglu_FD': jax.random.normal(ks[4], (F, D), dtype=jnp.float32) * sc, 'w_in_eDF': jax.random.normal(ks[5], (E, D, F), dtype=jnp.float32) * sc, 'w_swiglu_eDF': jax.random.normal(ks[6], (E, D, F), dtype=jnp.float32) * sc, 'w_out_eFD': jax.random.normal(ks[7], (E, F, D), dtype=jnp.float32) * sc}
    _L1_ffn_in = _L1_ffn_setup()
    _d = {'L0_attn_x': _L0_attn_in['x'], 'L0_attn_norm_w': _L0_attn_in['norm_w'], 'L0_attn_in_w': _L0_attn_in['in_w'], 'L0_attn_conv_w': _L0_attn_in['conv_w'], 'L0_attn_conv_b': _L0_attn_in['conv_b'], 'L0_attn_dt_bias': _L0_attn_in['dt_bias'], 'L0_attn_A_log': _L0_attn_in['A_log'], 'L0_attn_D_param': _L0_attn_in['D_param'], 'L0_attn_gnorm_w': _L0_attn_in['gnorm_w'], 'L0_attn_out_w': _L0_attn_in['out_w'], 'L0_attn_scorer_w1': _L0_attn_in['scorer_w1'], 'L0_attn_scorer_w2': _L0_attn_in['scorer_w2'], 'L0_attn_summ_w': _L0_attn_in['summ_w'], 'L0_attn_q_w': _L0_attn_in['q_w'], 'L0_attn_k_w': _L0_attn_in['k_w'], 'L0_attn_v_w': _L0_attn_in['v_w'], 'L0_attn_gate_w': _L0_attn_in['gate_w'], 'L0_ffn_ln_w': _L0_ffn_in['ln_w'], 'L0_ffn_ln_b': _L0_ffn_in['ln_b'], 'L0_ffn_router_w': _L0_ffn_in['router_w'], 'L0_ffn_gate_w': _L0_ffn_in['gate_w'], 'L0_ffn_up_w': _L0_ffn_in['up_w'], 'L0_ffn_down_w': _L0_ffn_in['down_w'], 'L0_ffn_sh_gate': _L0_ffn_in['sh_gate'], 'L0_ffn_sh_up': _L0_ffn_in['sh_up'], 'L0_ffn_sh_down': _L0_ffn_in['sh_down'], 'L1_attn_W_qkv': _L1_attn_in['W_qkv'], 'L1_attn_b_qkv': _L1_attn_in['b_qkv'], 'L1_attn_W_proj': _L1_attn_in['W_proj'], 'L1_attn_b_proj': _L1_attn_in['b_proj'], 'L1_ffn_router_DE': _L1_ffn_in['router_DE'], 'L1_ffn_w_in_shared_FD': _L1_ffn_in['w_in_shared_FD'], 'L1_ffn_w_out_shared_DF': _L1_ffn_in['w_out_shared_DF'], 'L1_ffn_w_swiglu_FD': _L1_ffn_in['w_swiglu_FD'], 'L1_ffn_w_in_eDF': _L1_ffn_in['w_in_eDF'], 'L1_ffn_w_swiglu_eDF': _L1_ffn_in['w_swiglu_eDF'], 'L1_ffn_w_out_eFD': _L1_ffn_in['w_out_eFD']}
    _x0 = _d['L0_attn_x']
    _d['L0_attn_x'] = jax.random.normal(jax.random.fold_in(jax.random.key(seed), 1), (16, 256, 128), dtype=_x0.dtype)
    del _x0
    return _d

def reference(L0_attn_x, L0_attn_norm_w, L0_attn_in_w, L0_attn_conv_w, L0_attn_conv_b, L0_attn_dt_bias, L0_attn_A_log, L0_attn_D_param, L0_attn_gnorm_w, L0_attn_out_w, L0_attn_scorer_w1, L0_attn_scorer_w2, L0_attn_summ_w, L0_attn_q_w, L0_attn_k_w, L0_attn_v_w, L0_attn_gate_w, L0_ffn_ln_w, L0_ffn_ln_b, L0_ffn_router_w, L0_ffn_gate_w, L0_ffn_up_w, L0_ffn_down_w, L0_ffn_sh_gate, L0_ffn_sh_up, L0_ffn_sh_down, L1_attn_W_qkv, L1_attn_b_qkv, L1_attn_W_proj, L1_attn_b_proj, L1_ffn_router_DE, L1_ffn_w_in_shared_FD, L1_ffn_w_out_shared_DF, L1_ffn_w_swiglu_FD, L1_ffn_w_in_eDF, L1_ffn_w_swiglu_eDF, L1_ffn_w_out_eFD):

    def _L0_attn_ref(x, norm_w, in_w, conv_w, conv_b, dt_bias, A_log, D_param, gnorm_w, out_w, scorer_w1, scorer_w2, summ_w, q_w, k_w, v_w, gate_w):
        import jax, jax.numpy as jnp
        import numpy as np
        D_MODEL = 128
        D_STATE = 128
        D_CONV = 4
        EXPAND = 2
        HEADDIM = 64
        D_INNER = D_MODEL * EXPAND
        NHEADS = D_INNER // HEADDIM
        CONV_DIM = D_INNER + 2 * D_STATE
        D_IN_PROJ = 2 * D_INNER + 2 * D_STATE + NHEADS
        POOL = 50
        SDIM = 64
        HEAD_DIM_RET = SDIM // 4
        TAU1 = 0.5
        TAU2 = 0.3
        HID = D_MODEL // 4
        B = 4
        T = 256
        EPS = 1e-05

        def _rmsnorm(x, w):
            return x * jax.lax.rsqrt(jnp.mean(x * x, axis=-1, keepdims=True) + EPS) * w

        def _mamba2(x, in_w, conv_w, conv_b, dt_bias, A_log, D_param, gnorm_w, out_w):
            Bn, Tn, _ = x.shape
            zxbcdt = x @ in_w.T
            z = zxbcdt[..., :D_INNER]
            xBC = zxbcdt[..., D_INNER:D_INNER + CONV_DIM]
            dt = zxbcdt[..., D_INNER + CONV_DIM:]
            xp = jnp.pad(jnp.transpose(xBC, (0, 2, 1)), ((0, 0), (0, 0), (D_CONV - 1, 0)))
            conv = jax.lax.conv_general_dilated(xp, conv_w[:, None, :], (1,), 'VALID', dimension_numbers=('NCH', 'OIH', 'NCH'), feature_group_count=CONV_DIM)
            xBC = jax.nn.silu(jnp.transpose(conv, (0, 2, 1)) + conv_b)
            xs = xBC[..., :D_INNER].reshape(Bn, Tn, NHEADS, HEADDIM)
            Bm = xBC[..., D_INNER:D_INNER + D_STATE]
            Cm = xBC[..., D_INNER + D_STATE:]
            dt = jax.nn.softplus(dt + dt_bias)
            A = -jnp.exp(A_log)
            dA = jnp.exp(dt * A)
            dtx = dt[..., None] * xs

            def step(h, inp):
                dA_t, dtx_t, B_t, C_t = inp
                h = h * dA_t[:, :, None, None] + dtx_t[..., None] * B_t[:, None, None, :]
                y = jnp.einsum('bhpn,bn->bhp', h, C_t)
                return (h, y)
            tm = lambda a: jnp.moveaxis(a, 1, 0)
            h0 = jnp.zeros((Bn, NHEADS, HEADDIM, D_STATE), x.dtype)
            _, ys = jax.lax.scan(step, h0, (tm(dA), tm(dtx), tm(Bm), tm(Cm)))
            y = jnp.moveaxis(ys, 0, 1) + D_param[None, None, :, None] * xs
            y = y.reshape(Bn, Tn, D_INNER)
            y = _rmsnorm(y * jax.nn.silu(z), gnorm_w)
            return y @ out_w.T

        def _update_memory(tokens, imp, summ_w, pool, prio, counts):
            Bn, Tn, Dm = tokens.shape
            S = min(Tn, POOL)
            order = jnp.argsort(-imp, axis=1)[:, :S]
            s_imp = jnp.take_along_axis(imp, order, axis=1)
            s_tok = jnp.take_along_axis(tokens, order[..., None], axis=1)
            s_sum = s_tok @ summ_w.T
            s_mask = s_imp > TAU1
            ar = jnp.arange(Bn)

            def body(carry, inp):
                pool, prio, counts = carry
                hi, si, ss = inp
                add = hi & (counts < POOL)
                idx = jnp.minimum(counts, POOL - 1)
                pool = pool.at[ar, idx].set(jnp.where(add[:, None], ss, pool[ar, idx]))
                prio = prio.at[ar, idx].set(jnp.where(add, si, prio[ar, idx]))
                counts = counts + add.astype(counts.dtype)
                repl = hi & (counts >= POOL)
                mi = jnp.argmin(prio, axis=1)
                should = repl & (si > prio[ar, mi])
                pool = pool.at[ar, mi].set(jnp.where(should[:, None], ss, pool[ar, mi]))
                prio = prio.at[ar, mi].set(jnp.where(should, si, prio[ar, mi]))
                return ((pool, prio, counts), None)
            xs = (jnp.moveaxis(s_mask, 1, 0), jnp.moveaxis(s_imp, 1, 0), jnp.moveaxis(s_sum, 1, 0))
            (pool, prio, counts), _ = jax.lax.scan(body, (pool, prio, counts), xs)
            return (pool, prio, counts)
        residual = x
        xn = _rmsnorm(x, norm_w)
        y = _mamba2(xn, in_w, conv_w, conv_b, dt_bias, A_log, D_param, gnorm_w, out_w)
        h = jax.nn.relu(y @ scorer_w1.T)
        scores = jax.nn.sigmoid((h @ scorer_w2.T)[..., 0])
        Bn = x.shape[0]
        pool = jnp.zeros((Bn, POOL, SDIM), x.dtype)
        prio = jnp.zeros((Bn, POOL), x.dtype)
        counts = jnp.zeros((Bn,), jnp.int32)
        pool, prio, counts = _update_memory(y, scores, summ_w, pool, prio, counts)
        mean_score = jnp.mean(scores, axis=1)
        retrieve_mask = (mean_score > TAU2) & (counts > 0)
        memory_mask = jnp.arange(POOL)[None, :] < counts[:, None]
        q = y @ q_w.T
        k = pool @ k_w.T
        v = pool @ v_w.T
        scale = np.float32(1.0 / np.sqrt(HEAD_DIM_RET))
        logits = jnp.einsum('btd,bpd->btp', q, k) * scale
        logits = jnp.where(memory_mask[:, None, :], logits, jnp.float32(-1000000000.0))
        attn = jax.nn.softmax(logits, axis=-1)
        retrieved = jnp.einsum('btp,bpd->btd', attn, v)
        gate = jax.nn.sigmoid(jnp.concatenate([y, retrieved], axis=-1) @ gate_w.T)
        y = y + gate * retrieved * retrieve_mask[:, None, None].astype(y.dtype)
        return residual + y

    def _L0_ffn_ref(hidden_states, ln_w, ln_b, router_w, gate_w, up_w, down_w, sh_gate, sh_up, sh_down):
        import jax, jax.numpy as jnp
        import numpy as np
        H = 128
        I = 256
        E = 8
        B, S = (2, 512)
        EPS = 1e-05
        INIT = 0.02

        def _layernorm(x, w, b):
            mu = jnp.mean(x, axis=-1, keepdims=True)
            var = jnp.mean(jnp.square(x - mu), axis=-1, keepdims=True)
            return (x - mu) * jax.lax.rsqrt(var + EPS) * w + b
        b, s, h = hidden_states.shape
        normed = _layernorm(hidden_states, ln_w, ln_b)
        xf = normed.reshape(-1, h)
        logits = xf @ router_w
        top_idx = jnp.argmax(logits, axis=-1)
        top_score = jax.nn.sigmoid(jnp.max(logits, axis=-1))

        def body(acc, ew):
            g, u, d, e = ew
            w = jnp.where(top_idx == e, top_score, 0.0)[:, None]
            xe = xf * w
            hmid = jax.nn.silu(xe @ g) * (xe @ u)
            return (acc + hmid @ d, None)
        routed, _ = jax.lax.scan(body, jnp.zeros_like(xf), (gate_w, up_w, down_w, jnp.arange(E)))
        shared = jax.nn.silu(xf @ sh_gate) * (xf @ sh_up) @ sh_down
        moe_out = (routed + shared).reshape(b, s, h)
        return hidden_states + moe_out

    def _L1_attn_ref(x, W_qkv, b_qkv, W_proj, b_proj):
        import jax, jax.numpy as jnp
        import numpy as np
        import math
        NUM_HEADS = 16

        def get_slopes(n):

            def pow2(n):
                start = 2 ** (-2 ** (-(math.log2(n) - 3)))
                return [start * start ** i for i in range(n)]
            if math.log2(n).is_integer():
                return pow2(n)
            c = 2 ** math.floor(math.log2(n))
            return pow2(c) + get_slopes(2 * c)[0::2][:n - c]
        B, T, C = x.shape
        H = NUM_HEADS
        D = C // H
        qkv = x @ W_qkv + b_qkv
        q, k, v = jnp.split(qkv, 3, axis=-1)
        q = q.reshape(B, T, H, D).transpose(0, 2, 1, 3)
        k = k.reshape(B, T, H, D).transpose(0, 2, 1, 3)
        v = v.reshape(B, T, H, D).transpose(0, 2, 1, 3)
        slopes = jnp.asarray(get_slopes(H), dtype=jnp.float32)
        idx = jnp.arange(T)
        alibi = jnp.minimum(idx[None, :] - idx[:, None], 0).astype(jnp.float32)
        bias = slopes[:, None, None] * alibi
        scale = 1.0 / math.sqrt(D)
        scores = jnp.einsum('bhtd,bhsd->bhts', q, k) * scale + bias[None]
        w = jax.nn.softmax(scores, axis=-1)
        y = jnp.einsum('bhts,bhsd->bhtd', w, v)
        y = y.transpose(0, 2, 1, 3).reshape(B, T, C)
        return y @ W_proj + b_proj

    def _L1_ffn_ref(x_bsD, router_DE, w_in_shared_FD, w_out_shared_DF, w_swiglu_FD, w_in_eDF, w_swiglu_eDF, w_out_eFD):
        import jax, jax.numpy as jnp
        import numpy as np
        TOP_K = 2
        E = 8
        D = 128
        F = 256
        B, S = (2, 128)
        b, s, d = x_bsD.shape
        x_aD = x_bsD.reshape(-1, d)
        a = x_aD.shape[0]
        scores_aE = x_aD @ router_DE
        topv_aK, topi_aK = jax.lax.top_k(scores_aE, TOP_K)
        masked_aE = jnp.full_like(scores_aE, -jnp.inf)
        masked_aE = masked_aE.at[jnp.arange(a)[:, None], topi_aK].set(topv_aK)
        gates_Ea = jax.nn.sigmoid(masked_aE.astype(jnp.float32)).astype(x_aD.dtype).T
        routed_in_EaD = x_aD[None, :, :] * gates_Ea[:, :, None]
        routed_in_EaD = jax.lax.stop_gradient(routed_in_EaD)
        mid_EaF = jnp.einsum('ead,edf->eaf', routed_in_EaD, w_in_eDF)
        sw_EaF = jnp.einsum('ead,edf->eaf', routed_in_EaD, w_swiglu_eDF)
        h_EaF = jax.nn.silu(mid_EaF) * sw_EaF
        out_EaD = jnp.einsum('eaf,efd->ead', h_EaF, w_out_eFD)
        shared_aF = jax.nn.silu(x_aD @ w_in_shared_FD.T) * (x_aD @ w_swiglu_FD.T)
        shared_out_aD = jax.lax.stop_gradient(shared_aF @ w_out_shared_DF.T)
        out_aD = shared_out_aD + jnp.sum(out_EaD, axis=0)
        return out_aD.reshape(b, s, d)
    x = L0_attn_x
    x = _layernorm(x + _L0_attn_ref(x, L0_attn_norm_w, L0_attn_in_w, L0_attn_conv_w, L0_attn_conv_b, L0_attn_dt_bias, L0_attn_A_log, L0_attn_D_param, L0_attn_gnorm_w, L0_attn_out_w, L0_attn_scorer_w1, L0_attn_scorer_w2, L0_attn_summ_w, L0_attn_q_w, L0_attn_k_w, L0_attn_v_w, L0_attn_gate_w), axis=-1)
    x = _layernorm(x + _L0_ffn_ref(x, L0_ffn_ln_w, L0_ffn_ln_b, L0_ffn_router_w, L0_ffn_gate_w, L0_ffn_up_w, L0_ffn_down_w, L0_ffn_sh_gate, L0_ffn_sh_up, L0_ffn_sh_down), axis=-1)
    x = _layernorm(x + _L1_attn_ref(x, L1_attn_W_qkv, L1_attn_b_qkv, L1_attn_W_proj, L1_attn_b_proj), axis=-1)
    x = _layernorm(x + _L1_ffn_ref(x, L1_ffn_router_DE, L1_ffn_w_in_shared_FD, L1_ffn_w_out_shared_DF, L1_ffn_w_swiglu_FD, L1_ffn_w_in_eDF, L1_ffn_w_swiglu_eDF, L1_ffn_w_out_eFD), axis=-1)
    return x

_drawn_inputs = setup_inputs


def setup_inputs(seed=0):
    import zlib

    import numpy as np

    out = dict(_drawn_inputs(seed))
    spreads = {'L0_attn_norm_w': (1.0, 0.2),
     'L0_attn_conv_b': (0.0, 0.1),
     'L0_attn_D_param': (1.0, 0.2),
     'L0_attn_gnorm_w': (1.0, 0.2),
     'L0_ffn_ln_w': (1.0, 0.6),
     'L0_ffn_ln_b': (0.0, 0.8)}
    factors = {'L0_ffn_router_w': 8.0,
     'L0_ffn_gate_w': 8.0,
     'L0_ffn_up_w': 8.0,
     'L0_ffn_down_w': 8.0,
     'L0_ffn_sh_gate': 8.0,
     'L0_ffn_sh_up': 8.0,
     'L0_ffn_sh_down': 8.0,
     'L1_attn_W_qkv': 7.396,
     'L1_attn_b_qkv': 8.0,
     'L1_attn_W_proj': 6.739,
     'L1_attn_b_proj': 2.782,
     'L1_ffn_router_DE': 8.0,
     'L1_ffn_w_in_shared_FD': 6.846,
     'L1_ffn_w_out_shared_DF': 6.765,
     'L1_ffn_w_swiglu_FD': 6.801,
     'L1_ffn_w_in_eDF': 8.0,
     'L1_ffn_w_swiglu_eDF': 8.0,
     'L1_ffn_w_out_eFD': 8.0}
    for name, (base, spread) in spreads.items():
        noise = np.random.default_rng([zlib.crc32(name.encode()), seed]).standard_normal(out[name].shape)
        drawn = base * np.exp(spread * noise) if base else spread * noise
        out[name] = jnp.asarray(drawn.astype(out[name].dtype))
    for name, factor in factors.items():
        out[name] = (out[name] * factor).astype(out[name].dtype)
    return out
```

```python
import numpy as np
import concourse.bass as bass
from concourse import mybir
from contextlib import ExitStack

F32 = mybir.dt.float32
BF16 = mybir.dt.bfloat16
ALU = mybir.AluOpType
ACT = mybir.ActivationFunctionType
AX_X = mybir.AxisListType.X

P = 128
B, T, D = 16, 256, 128
NT = B * T // P
TT = T // P
EPS = 1e-5
MH, MP = 4, 64
DI = MH * MP
TAPS = 4
POOL = 50
SLOTS = 2
TURNS = B // SLOTS
UNITS = B * T // 512
NE = 8
FF = 256
TILES = 40
BIG = 1.0e30
U32 = mybir.dt.uint32


def columns(table):
    at, out = 0, {}
    for name, width in table:
        out[name] = (at, at + width)
        at += width
    return out, at


CONST, CONST_W = columns([("ident", P), ("tri", P), ("ones", P), ("later", P), ("earlier", TT * T),
                          ("ones2", NE * NT), ("ahead", P), ("eight", NE), ("m128", NT), ("tile", TILES), ("slot", POOL), ("sel", TURNS * MH)])
WA, WA_W = columns([("inw", 768), ("dtw", MH), ("normw", 1), ("convw", 16), ("convb", 4), ("dtb", MH),
                    ("alog", MH), ("dpar", 2), ("gnorm", 2), ("outw", 2 * D), ("w1", 32), ("w2", 1), ("tapbc", 4 * 2 * P), ("summ", D),
                    ("qw", D), ("kwt", 64), ("vwt", D), ("g1", D), ("g2", D)])
WF, WF_W = columns([("router0", NE), ("router1", NE), ("lnw", D), ("lnb", D)])


class Links:

    def __init__(self, engine, sem, total=0, turn=0):
        self.engine, self.sem, self.base, self.total, self.n = engine, sem, turn * total, total, 0

    def __call__(self, ins):
        self.n += 1
        ins.then_inc(self.sem, 1)
        self.engine.wait_ge(self.sem, self.base + self.n)

    def close(self):
        assert self.n == self.total, f"links in the body: {self.n}, not {self.total}"


class Kept:

    def c(self, name):
        a, z = CONST[name]
        return self.C[:, a:z]

    def w(self, name):
        a, z = WA[name]
        return self.W[:, a:z]

    def cf(self, name):
        a, z = WF[name]
        return self.F[:, a:z]


def alone(engine):
    engine.nop(nofuse=True)


def spread(ap, n):
    return ap.unsqueeze(2).broadcast_to((ap.shape[0], ap.shape[1], n))


def prepare(nc, sb, ps, sem, dram, k):
    XN4 = sb("XN4", [P, SLOTS, 4, D])
    XNS = sb("XNS", [P, SLOTS, 4 * P])
    SQ = sb("SQ", [P, SLOTS, 4, D])
    MS = sb("MS", [P, SLOTS, 4])
    RS = sb("RS", [P, SLOTS, 4])
    MK = sb("MK", [64, D])
    VWT = sb("VWT", [P, D])
    DTR, RAW, E, U, DLT, LNU, LA = (sb(n, [P, NT, MH]) for n in ("DTR", "RAW", "E", "U", "DLT", "LNU", "LA"))
    LA2 = sb("LA2", [P, TT, B, MH])
    CUM = sb("CUM", [P, TT, B * MH])
    PARTS = sb("PARTS", [P, SLOTS, TT, 96], BF16)
    IDB = k.IDB
    psb = ps[:].bitcast(BF16)

    s_x, s_c, s_wa = sem("x_loaded"), sem("const_loaded"), sem("wa_loaded")
    s_pow = sem("power_set")
    s_idb = sem("bf16_consts")
    s_mk, s_mkc = sem("mk"), sem("mk_copied")
    s_prod, s_prodc = sem("products"), sem("products_copied")
    s_link = sem("dve_links")
    s_ms = [sem(f"mean_square{p}") for p in range(SLOTS)]
    s_rs = [sem(f"rstd{p}") for p in range(SLOTS)]
    s_xn = [sem(f"xn{p}") for p in range(SLOTS)]
    s_tr = [sem(f"xn_transposed{p}") for p in range(SLOTS)]
    s_ev = [sem(f"xn_evacuated{p}") for p in range(SLOTS)]
    s_cp = [sem(f"xn_kept{p}") for p in range(SLOTS)]
    s_dt = [sem(f"dt_raw{p}") for p in range(SLOTS)]
    s_dtc = [sem(f"dt_copied{p}") for p in range(SLOTS)]
    s_sp = sem("softplus_act")
    s_abs = sem("abs_done")
    s_spd = sem("softplus_dve")
    s_cum = sem("cumulated")
    s_parts = sem("parts_split")
    s_cumt = sem("parts_transposed")
    s_done = sem("parts_kept")

    X, C, W = k.X, k.C, k.W
    with nc.Block() as block:
        @block.sync
        def _(sp):
            sp.dma_start(C[:], dram["const"]).then_inc(s_c, 16)
            sp.dma_start(X[:, 0:16], dram["x"][0:8].rearrange("b (t p) d -> p (b t) d", p=P)).then_inc(s_x, 16)
            sp.dma_start(W[:], dram["wa"]).then_inc(s_wa, 16)
            sp.dma_start(X[:, 16:32], dram["x"][8:16].rearrange("b (t p) d -> p (b t) d", p=P)).then_inc(s_x, 16)

        @block.gpsimd
        def _(pool):
            nc.gpsimd.memset(k.POWER[:], -0.5).then_inc(s_pow, 1)
            pool.wait_ge(s_pow, 1)
            with pool.Fori(0, UNITS // SLOTS) as j:
                for p in range(SLOTS):
                    pool.wait_ge(s_ms[p], j + 1)
                    pool.wait_ge(s_xn[p], j)
                    nc.gpsimd.tensor_tensor(RS[:, p], MS[:, p], k.POWER[:, 0:4], ALU.pow).then_inc(s_rs[p], 1)
                for p in range(SLOTS):
                    pool.wait_ge(s_ev[p], j + 1)
                    nc.gpsimd.tensor_copy(k.XNT[:, bass.ds((UNITS // 2 * p + j) * 512, 512)], XNS[:, p]).then_inc(s_cp[p], 1)

        @block.vector
        def _(dve):
            link = Links(dve, s_link)
            dve.wait_ge(s_c, 16)
            nc.vector.tensor_copy(IDB[:], k.c("ident"))
            nc.vector.tensor_copy(k.LATER[:], k.c("later"))
            link(nc.vector.tensor_copy(k.SEL[:], k.c("sel")[0:96].unsqueeze(2).broadcast_to((96, TURNS * MH, T))))
            dve.wait_ge(s_wa, 16)
            nc.vector.tensor_scalar(k.w("inw")[:, 0:DI], k.w("inw")[:, 0:DI], 0.5, None, ALU.mult)
            nc.vector.tensor_scalar(k.w("convw"), k.w("convw"), 0.5, None, ALU.mult)
            nc.vector.tensor_scalar(k.w("convb"), k.w("convb"), 0.5, None, ALU.mult)
            for tap in range(TAPS):
                w = k.w("tapbc")[:, 2 * P * tap:2 * P * tap + 2 * P]
                nc.vector.scalar_tensor_tensor(w, w, 0.5, k.w("inw")[:, 4 * P:6 * P], ALU.mult, ALU.mult)
            for ct in range(2):
                o = k.w("outw")[:, ct * D:(ct + 1) * D]
                last = nc.vector.tensor_scalar(o, o, k.w("gnorm")[:, ct:ct + 1], None, ALU.mult)
            link(last)
            dve.wait_ge(s_mk, 1)
            nc.vector.tensor_copy(MK[:], ps[0:64, 1024:1152]).then_inc(s_mkc, 1)
            nc.vector.tensor_copy(VWT[:], ps[:, 1536:1664]).then_inc(s_mkc, 1)
            dve.wait_ge(s_prod, 1)
            nc.vector.tensor_copy(k.AT[:], ps[:, 2048:2176])
            link(nc.vector.tensor_copy(k.VV[:], ps[:, 2560:2816]))
            dve.wait_ge(s_x, 32)
            with dve.Fori(0, UNITS // SLOTS) as j:
                ln = Links(dve, s_link, 2 * SLOTS, j)
                ln.base = ln.base + link.n
                for p in range(SLOTS):
                    xu = X[:, bass.ds((UNITS // 2 * p + j) * 4, 4), :]
                    dve.wait_ge(s_xn[p], j)
                    ln(nc.vector.tensor_tensor(SQ[:, p], xu, xu, ALU.mult))
                    ln(nc.vector.tensor_reduce(MS[:, p], SQ[:, p], AX_X, ALU.add))
                    nc.vector.tensor_scalar(MS[:, p], MS[:, p], 1.0 / D, EPS, ALU.mult, ALU.add).then_inc(s_ms[p], 1)
                for p in range(SLOTS):
                    xu = X[:, bass.ds((UNITS // 2 * p + j) * 4, 4), :]
                    dve.wait_ge(s_rs[p], j + 1)
                    dve.wait_ge(s_tr[p], j)
                    nc.vector.tensor_tensor(XN4[:, p], xu, spread(RS[:, p], D), ALU.mult).then_inc(s_xn[p], 1)
                for p in range(SLOTS):
                    dve.wait_ge(s_dt[p], j + 1)
                    nc.vector.tensor_copy(DTR[:, bass.ds((UNITS // 2 * p + j) * 4, 4), :],
                                          ps[:, 1024 + 512 * p:1040 + 512 * p].rearrange("p (t h) -> p t h", h=MH)
                                          ).then_inc(s_dtc[p], 1)
                ln.close()
            link.n += (UNITS // SLOTS) * 2 * SLOTS
            for p in range(SLOTS):
                dve.wait_ge(s_dtc[p], UNITS // SLOTS)
            nc.vector.tensor_tensor(RAW[:], DTR[:], k.w("dtb").unsqueeze(1).broadcast_to((P, NT, MH)),
                                    ALU.add).then_inc(s_spd, 1)
            dve.wait_ge(s_sp, 2)
            nc.vector.tensor_scalar(U[:], E[:], 1.0, None, ALU.add).then_inc(s_spd, 1)
            dve.wait_ge(s_spd, 2)
            link(nc.vector.tensor_scalar(DLT[:], U[:], 1.0, None, ALU.subtract))
            link(nc.vector.tensor_tensor(DLT[:], E[:], DLT[:], ALU.subtract))
            link(nc.vector.reciprocal(E[:], U[:]))
            link(nc.vector.tensor_tensor(DLT[:], DLT[:], E[:], ALU.mult))
            link(nc.vector.scalar_tensor_tensor(DLT[:], RAW[:], 0.0, DLT[:], ALU.max, ALU.add))
            dve.wait_ge(s_sp, 3)
            link(nc.vector.tensor_tensor(k.DT[:], DLT[:], LNU[:], ALU.add))
            link(nc.vector.scalar_tensor_tensor(LA[:], k.DT[:], -1.0,
                                                k.w("alog").unsqueeze(1).broadcast_to((P, NT, MH)),
                                                ALU.mult, ALU.mult))
            nc.vector.tensor_copy(LA2[:], LA[:].rearrange("p (b t) h -> p t b h", t=TT)).then_inc(s_spd, 1)
            dve.wait_ge(s_cum, 1)
            link(nc.vector.tensor_copy(CUM[:], ps[:, 0:TT * B * MH].rearrange("p (t c) -> p t c", t=TT)))
            for part in range(3):
                for t in range(TT):
                    for h2 in range(SLOTS):
                        last = nc.vector.tensor_copy(
                            PARTS[:, h2, t].rearrange("p (b c h) -> p b c h", c=3, h=MH)[:, :, part, :],
                            CUM[:, t, h2 * 32:h2 * 32 + 32].rearrange("p (b h) -> p b h", h=MH))
                if part < 2:
                    link(last)
                    for t in range(TT):
                        for h2 in range(SLOTS):
                            c = CUM[:, t, h2 * 32:h2 * 32 + 32].rearrange("p (b h) -> p b h", h=MH)
                            last = nc.vector.tensor_tensor(
                                c, c, PARTS[:, h2, t].rearrange("p (b c h) -> p b c h", c=3, h=MH)[:, :, part, :],
                                ALU.subtract)
                    link(last)
                else:
                    last.then_inc(s_parts, 1)
            dve.wait_ge(s_cumt, 1)
            for h2 in range(SLOTS):
                o = psb[0:96, h2 * 1024:h2 * 1024 + TT * P].rearrange("p (t c) -> p t c", t=TT)
                nc.vector.tensor_copy(k.CUMT[:, h2], o)
                last = nc.vector.tensor_scalar(k.NCUMT[:, h2], o, -1.0, None, ALU.mult)
            last.then_inc(s_done, 1)
            dve.wait_ge(s_done, 1)

        @block.scalar
        def _(act):
            with act.Fori(0, UNITS // SLOTS) as j:
                for p in range(SLOTS):
                    act.wait_ge(s_tr[p], j + 1)
                    act.wait_ge(s_cp[p], j)
                    act.wait_ge(s_dt[p], j)
                    nc.scalar.activation(XNS[:, p], ps[:, 512 * p:512 * p + 512], ACT.Copy,
                                         scale=k.w("normw")).then_inc(s_ev[p], 1)
            act.wait_ge(s_wa, 16)
            act.wait_ge(s_spd, 1)
            nc.scalar.activation(k.w("alog"), k.w("alog"), ACT.Exp).then_inc(s_sp, 1)
            nc.scalar.activation(E[:], RAW[:], ACT.Abs).then_inc(s_abs, 1)
            act.wait_ge(s_abs, 1)
            nc.scalar.activation(E[:], E[:], ACT.Exp, scale=-1.0).then_inc(s_sp, 1)
            act.wait_ge(s_spd, 2)
            nc.scalar.activation(LNU[:], U[:], ACT.Ln).then_inc(s_sp, 1)

        @block.tensor
        def _(pe):
            pe.wait_ge(s_c, 16)
            pe.wait_ge(s_wa, 16)
            pe.wait_ge(s_link, 2)
            nc.tensor.matmul(ps[0:64, 1024:1152], k.w("kwt")[0:64], k.w("summ")[0:64], start=True, stop=True)
            nc.tensor.matmul(ps[:, 1536:1664], k.w("vwt")[0:64], k.w("summ")[0:64], start=True,
                             stop=True).then_inc(s_mk, 1)
            pe.wait_ge(s_mkc, 2)
            nc.tensor.matmul(ps[:, 2048:2176], MK[:], k.w("qw")[0:64], start=True, stop=True)
            nc.tensor.matmul(ps[:, 2560:2688], k.w("summ")[0:64], k.w("vwt")[0:64], start=True, stop=True)
            nc.tensor.matmul(ps[:, 2688:2816], VWT[:], k.w("g2"), start=True, stop=True).then_inc(s_prod, 1)
            with pe.Fori(0, UNITS // SLOTS) as j:
                for p in range(SLOTS):
                    pe.wait_ge(s_xn[p], j + 1)
                    pe.wait_ge(s_ev[p], j)
                    for t in range(4):
                        last = nc.tensor.transpose(ps[:, 512 * p + 128 * t:512 * p + 128 * t + 128], XN4[:, p, t, :],
                                                   k.c("ident"))
                    last.then_inc(s_tr[p], 1)
                for p in range(SLOTS):
                    pe.wait_ge(s_ev[p], j + 1)
                    pe.wait_ge(s_dtc[p], j)
                    for t in range(4):
                        last = nc.tensor.matmul(ps[:, 1024 + 512 * p + 4 * t:1028 + 512 * p + 4 * t],
                                                XNS[:, p, P * t:P * t + P], k.w("dtw"), start=True, stop=True)
                    last.then_inc(s_dt[p], 1)
            pe.wait_ge(s_spd, 3)
            nc.tensor.matmul(ps[:, 0:64], k.c("tri"), LA2[:, 0], start=True, stop=True)
            nc.tensor.matmul(ps[:, 64:128], k.c("tri"), LA2[:, 1], start=True, stop=False)
            nc.tensor.matmul(ps[:, 64:128], k.c("ones"), LA2[:, 0], start=False, stop=True).then_inc(s_cum, 1)
            pe.wait_ge(s_parts, 1)
            for h2 in range(SLOTS):
                for t in range(TT):
                    last = nc.tensor.transpose(psb[0:96, h2 * 1024 + t * P:h2 * 1024 + t * P + P], PARTS[:, h2, t],
                                               IDB[:])
            last.then_inc(s_cumt, 1)


def mamba(nc, sb, ps, sem, k):
    PAD = TAPS - 1
    CB = sb("CB", [P, SLOTS, 2, PAD + T])
    TH = sb("TH", [P, SLOTS, 4 * T])
    ZZ = sb("ZZ", [P, SLOTS, 2 * T])
    CV = sb("CV", [P, SLOTS, 4, T])
    XS = sb("XS", [P, SLOTS, 4, T])
    EX = sb("EX", [P, SLOTS, MH, T + P])
    DTX = sb("DTX", [P, SLOTS, TT * MH, MP])
    YG = sb("YG", [P, SLOTS, 2, T])
    YSQ = sb("YSQ", [P, SLOTS, 2, T])
    MS = sb("MSY", [P, SLOTS, TT])
    RS = sb("RSY", [P, SLOTS, TT])
    YO = sb("YO", [P, SLOTS, TT, D])
    YT = sb("YT", [P, SLOTS, T])
    HT = sb("HT", [32, SLOTS, T])
    W2 = sb("W2", [32, P])
    SC = sb("SC", [P, SLOTS, T])
    SCC = sb("SCC", [P, SLOTS, TT])
    MEAN = sb("MEAN", [P, SLOTS])
    JUNK = sb("JUNK", [P, SLOTS, TT, T])
    JUNK2 = sb("JUNK2", [P, SLOTS, TT, T])
    RANK = sb("RANK", [P, SLOTS, 2 * TT])
    HIGH = sb("HIGH", [P, SLOTS, TT])
    PICK = sb("PICK", [P, SLOTS, TT, POOL])
    YSEL = sb("YSEL", [P, SLOTS, POOL])
    EMPTY = sb("EMPTY", [1, SLOTS, POOL])
    KA = sb("KA", [P, SLOTS, POOL])
    VSEL = sb("VSEL", [P, SLOTS, 2 * D])
    LG = sb("LG", [P, SLOTS, TT, POOL])
    MX = sb("MX", [P, SLOTS, TT])
    SM = sb("SM", [P, SLOTS, TT])
    PRT = sb("PRT", [P, SLOTS, T])
    TG = sb("TG", [P, SLOTS, TT, D])
    GR = sb("GR", [P, SLOTS, TT, D])
    WX = sb("WX", [P, SLOTS, TT, D])
    BN = sb("BN", [P, SLOTS, TT, 6])
    MV = sb("MV", [P, SLOTS, TT, 2])
    X, C, psb = k.X, k.C, ps[:].bitcast(BF16)

    def two(name):
        return [sem(f"{name}{p}") for p in range(SLOTS)]

    s_zero, s_w2 = sem("zeroed"), sem("w2_spread")
    s_link = sem("mamba_dve_links")
    s_in, s_inz, s_cb, s_thz, s_zz = two("in_proj"), two("z_proj"), two("conv_in"), two("tanh_z"), two("silu_z")
    s_cvx, s_inbc, s_thx, s_thb, s_xs, s_bc = two("conv_x"), two("bc_psum"), two("tanh_x"), two("tanh_bc"), two("xs"), two("bc")
    s_g, s_xt, s_dec, s_ex, s_m, s_dtx = two("g"), two("x_tokens"), two("decay"), two("decay_exp"), two("m"), two("dtx")
    s_y, s_yd, s_yg, s_sq, s_yo, s_ms, s_rs = two("y"), two("y_d"), two("y_gated"), two("y_sq"), two("y_out"), two("y_ms"), two("y_rs")
    s_yoc, s_ytp, s_yt, s_hp, s_ht, s_zsp, s_tsc = two("yo_kept"), two("yt_psum"), two("yt"), two("h_psum"), two("ht"), two("score_psum"), two("score_tanh")
    s_sc, s_sct, s_pick, s_self, s_ysel, s_kv, s_ka, s_vs = two("scores"), two("scores_turned"), two("picked"), two("sel_psum"), two("ysel"), two("kv_psum"), two("ka"), two("vsel")
    s_lg, s_sub, s_ep, s_pr, s_prt, s_prc = two("logits"), two("logits_less_max"), two("exps"), two("probs"), two("probs_turned"), two("prt")
    s_rg, s_tg, s_gr, s_wx, s_var, s_lrs, s_res = two("retrieved"), two("gate_tanh"), two("gated"), two("x2_y"), two("variance"), two("ln_rstd"), two("x_written")

    def bank(p, n, a=0, z=512):
        return ps[:, (4 * p + n) * 512 + a:(4 * p + n) * 512 + z]

    LINKS_DVE = 2 * 15
    slots = range(SLOTS)
    with nc.Block() as block:
        @block.gpsimd
        def _(pool):
            for t in (CB, VSEL, PRT):
                last = nc.gpsimd.memset(t[:], 0.0)
            last.then_inc(s_zero, 1)
            with pool.Fori(0, TURNS) as j:
                def power(p):
                    pool.wait_ge(s_ms[p], j + 1)
                    nc.gpsimd.tensor_tensor(RS[:, p], MS[:, p], k.POWER[:, 0:TT], ALU.pow).then_inc(s_rs[p], 1)

                def ln_power(p):
                    pool.wait_ge(s_var[p], j + 1)
                    nc.gpsimd.tensor_tensor(MV[:, p, :, 1:2], MV[:, p, :, 1:2],
                                            k.POWER[:, 0:TT].unsqueeze(2), ALU.pow).then_inc(s_lrs[p], 1)

                for step in (power, ln_power):
                    for p in slots:
                        step(p)

        @block.vector
        def _(dve):
            dve.wait_ge(s_zero, 1)
            nc.vector.tensor_copy(W2[:], k.w("w2")[0:32].broadcast_to((32, P))).then_inc(s_w2, 1)
            with dve.Fori(0, TURNS) as j:
                link = Links(dve, s_link, LINKS_DVE, j)
                n = j + 1

                def silu_z(p):
                    dve.wait_ge(s_thz[p], n)
                    nc.vector.scalar_tensor_tensor(ZZ[:, p], TH[:, p, 0:2 * T], 1.0, bank(p, 2), ALU.add,
                                                   ALU.mult).then_inc(s_zz[p], 1)

                def conv(p):
                    dve.wait_ge(s_cb[p], n)
                    for ct in (0, 1):
                        w, b = k.w("convw")[:, 4 * ct:4 * ct + 4], k.w("convb")[:, ct:ct + 1]
                        last = nc.vector.tensor_scalar(CV[:, p, ct], CB[:, p, ct, 0:T], w[:, 0:1], b, ALU.mult, ALU.add)
                    link(last)
                    for tap in range(1, TAPS):
                        for ct in (0, 1):
                            w = k.w("convw")[:, 4 * ct + tap:4 * ct + tap + 1]
                            last = nc.vector.scalar_tensor_tensor(CV[:, p, ct], CB[:, p, ct, tap:tap + T], w,
                                                                  CV[:, p, ct], ALU.mult, ALU.add)
                        if tap < TAPS - 1:
                            link(last)
                    last.then_inc(s_cvx[p], 1)

                def silu_x(p):
                    dve.wait_ge(s_thx[p], n)
                    nc.vector.scalar_tensor_tensor(XS[:, p, 0:2], TH[:, p, 0:2 * T].rearrange("p (c t) -> p c t", t=T), 1.0,
                                                   CV[:, p, 0:2], ALU.add, ALU.mult).then_inc(s_xs[p], 1)

                def silu_bc(p):
                    dve.wait_ge(s_thb[p], n)
                    nc.vector.scalar_tensor_tensor(XS[:, p, 2:4], TH[:, p, 2 * T:4 * T].rearrange("p (c t) -> p c t", t=T), 1.0,
                                                   CV[:, p, 2:4], ALU.add, ALU.mult).then_inc(s_bc[p], 1)

                def dt_x(p):
                    dve.wait_ge(s_xt[p], n)
                    nc.vector.tensor_tensor(DTX[:, p], bank(p, 3).rearrange("p (a b) -> p a b", b=MP),
                                            spread(k.DT[:, bass.ds(16 * p + 2 * j, 2), :].rearrange("p t h -> p (t h)"), MP),
                                            ALU.mult).then_inc(s_dtx[p], 1)

                def mix(p):
                    dve.wait_ge(s_ex[p], 2 * n)
                    dve.wait_ge(s_g[p], n)
                    nc.vector.tensor_tensor(EX[:, p], EX[:, p], bank(p, 2, 0, T + P).unsqueeze(1).broadcast_to((P, MH, T + P)),
                                            ALU.mult).then_inc(s_m[p], 1)

                def gated_y(p):
                    dve.wait_ge(s_y[p], n)
                    for ct in range(2):
                        last = nc.vector.scalar_tensor_tensor(YG[:, p, ct], XS[:, p, ct], k.w("dpar")[:, ct:ct + 1],
                                                              bank(p, 0, ct * T, ct * T + T), ALU.mult, ALU.add)
                    link(last)
                    nc.vector.tensor_tensor(YG[:, p], YG[:, p], ZZ[:, p].rearrange("p (c t) -> p c t", t=T),
                                            ALU.mult).then_inc(s_yg[p], 1)

                def mean_square(p):
                    dve.wait_ge(s_yo[p], n)
                    nc.vector.tensor_scalar(MS[:, p], bank(p, 1, T, T + TT), 1.0 / DI, EPS, ALU.mult,
                                            ALU.add).then_inc(s_ms[p], 1)

                def scaled_y(p):
                    dve.wait_ge(s_rs[p], n)
                    nc.vector.tensor_tensor(YO[:, p], bank(p, 1, 0, T).rearrange("p (t d) -> p t d", d=D),
                                            spread(RS[:, p], D), ALU.mult).then_inc(s_yoc[p], 1)

                def scores(p):
                    dve.wait_ge(s_tsc[p], n)
                    nc.vector.tensor_scalar(SC[:, p], SC[:, p], 0.5, 0.5, ALU.mult, ALU.add).then_inc(s_sc[p], 1)
                    dve.wait_ge(s_sc[p], n)
                    link(nc.vector.tensor_reduce(MEAN[:, p:p + 1], SC[:, p], AX_X, ALU.add))
                    nc.vector.tensor_scalar(MEAN[:, p:p + 1], MEAN[:, p:p + 1], 1.0 / T, None, ALU.mult)

                def ranks(p):
                    dve.wait_ge(s_sct[p], n)
                    link(nc.vector.tensor_copy(SCC[:, p], bank(p, 0, T, T + TT)))
                    nc.vector.tensor_scalar(HIGH[:, p], SCC[:, p], 0.5, None, ALU.is_gt)
                    for t in range(TT):
                        nc.vector.tensor_scalar(JUNK[:, p, t], SC[:, p], SCC[:, p, t:t + 1], None, ALU.is_gt, ALU.add,
                                                accum_out=RANK[:, p, t:t + 1])
                        last = nc.vector.scalar_tensor_tensor(JUNK2[:, p, t], SC[:, p], SCC[:, p, t:t + 1],
                                                              k.c("earlier")[:, t * T:t * T + T], ALU.is_equal, ALU.mult,
                                                              accum_out=RANK[:, p, TT + t:TT + t + 1])
                    link(last)
                    link(nc.vector.tensor_tensor(RANK[:, p, 0:TT], RANK[:, p, 0:TT], RANK[:, p, TT:2 * TT], ALU.add))
                    for t in range(TT):
                        last = nc.vector.tensor_scalar(PICK[:, p, t], k.c("slot"), RANK[:, p, t:t + 1],
                                                       HIGH[:, p, t:t + 1], ALU.is_equal, ALU.mult)
                    last.then_inc(s_pick[p], 1)

                def empty(p):
                    dve.wait_ge(s_self[p], n)
                    nc.vector.tensor_scalar(EMPTY[:, p], bank(p, 1, 64, 64 + POOL)[0:1], 1.0, 4.0e9, ALU.subtract, ALU.mult)
                    nc.vector.tensor_copy(YSEL[:, p], bank(p, 1, 0, POOL)).then_inc(s_ysel[p], 1)

                def less_max(p):
                    dve.wait_ge(s_lg[p], n)
                    lg = bank(p, 0, 0, TT * POOL).rearrange("p (t s) -> p t s", s=POOL)
                    link(nc.vector.tensor_reduce(MX[:, p], lg, AX_X, ALU.max))
                    nc.vector.tensor_tensor(LG[:, p], lg, spread(MX[:, p], POOL), ALU.subtract).then_inc(s_sub[p], 1)

                def probs(p):
                    dve.wait_ge(s_ep[p], n)
                    link(nc.vector.tensor_reduce(SM[:, p], LG[:, p], AX_X, ALU.add))
                    link(nc.vector.reciprocal(SM[:, p], SM[:, p]))
                    nc.vector.tensor_tensor(LG[:, p], LG[:, p], spread(SM[:, p], POOL), ALU.mult).then_inc(s_pr[p], 1)

                def gate(p):
                    xs = X[:, bass.ds(16 * p + 2 * j, 2), :]
                    link(nc.vector.scalar_tensor_tensor(WX[:, p], xs, 2.0, YO[:, p], ALU.mult, ALU.add))
                    nc.vector.tensor_scalar(MEAN[:, p:p + 1], MEAN[:, p:p + 1], 0.3, 0.5, ALU.is_gt, ALU.mult)
                    dve.wait_ge(s_tg[p], n)
                    nc.vector.scalar_tensor_tensor(GR[:, p], TG[:, p], 1.0,
                                                   bank(p, 1).rearrange("p (t c) -> p t c", t=TT)[:, :, 0:D],
                                                   ALU.add, ALU.mult).then_inc(s_gr[p], 1)
                    dve.wait_ge(s_gr[p], n)
                    link(nc.vector.scalar_tensor_tensor(WX[:, p], GR[:, p], MEAN[:, p:p + 1], WX[:, p], ALU.mult, ALU.add))

                def stats(p):
                    for t in range(TT):
                        last = nc.vector.bn_stats(BN[:, p, t], WX[:, p, t])
                    link(last)
                    alone(dve)
                    for t in range(TT):
                        last = nc.vector.bn_aggr(MV[:, p, t], BN[:, p, t])
                    link(last)
                    nc.vector.tensor_scalar(MV[:, p, :, 1:2], MV[:, p, :, 1:2], EPS, None, ALU.add).then_inc(s_var[p], 1)

                def normed(p):
                    dve.wait_ge(s_lrs[p], n)
                    for t in range(TT):
                        last = nc.vector.tensor_scalar(X[:, bass.ds(16 * p + 2 * j + t, 1), :].rearrange("p a d -> p (a d)"),
                                                       WX[:, p, t], MV[:, p, t, 0:1], MV[:, p, t, 1:2],
                                                       ALU.subtract, ALU.mult)
                    last.then_inc(s_res[p], 1)

                for step in (silu_z, conv, silu_x, silu_bc, dt_x, mix, gated_y, mean_square, scaled_y, scores, ranks,
                             empty, less_max, probs, gate, stats, normed):
                    for p in slots:
                        step(p)
                link.close()

        @block.scalar
        def _(act):
            act.wait_ge(s_zero, 1)
            with act.Fori(0, TURNS) as j:
                n = j + 1

                def tanh_z(p):
                    act.wait_ge(s_inz[p], n)
                    act.wait_ge(s_res[p], j)
                    nc.scalar.activation(TH[:, p, 0:2 * T], bank(p, 2), ACT.Tanh).then_inc(s_thz[p], 1)

                def conv_in(p):
                    act.wait_ge(s_in[p], n)
                    nc.scalar.activation(CB[:, p, :, PAD:], bank(p, 0).rearrange("p (c t) -> p c t", t=T),
                                         ACT.Copy).then_inc(s_cb[p], 1)

                def tanh_x(p):
                    act.wait_ge(s_cvx[p], n)
                    act.wait_ge(s_zz[p], n)
                    nc.scalar.activation(TH[:, p, 0:2 * T].rearrange("p (c t) -> p c t", t=T), CV[:, p, 0:2],
                                         ACT.Tanh).then_inc(s_thx[p], 1)

                def tanh_bc(p):
                    act.wait_ge(s_inbc[p], n)
                    for i in range(2):
                        bias = k.w("convb")[:, 2 + i:3 + i]
                        nc.scalar.activation(CV[:, p, 2 + i], bank(p, 1, i * T, i * T + T), ACT.Identity, bias=bias)
                        last = nc.scalar.activation(TH[:, p, 2 * T + i * T:3 * T + i * T], bank(p, 1, i * T, i * T + T),
                                                    ACT.Tanh, bias=bias)
                    last.then_inc(s_thb[p], 1)

                def decays(i):
                    def step(p):
                        act.wait_ge(s_dec[p], 2 * j + i + 1)
                        nc.scalar.activation(EX[:, p, 2 * i:2 * i + 2],
                                             ps[:, 2048 * p:2048 * p + 1024].rearrange("p (h c) -> p h c", h=2)[:, :, 0:T + P],
                                             ACT.Exp).then_inc(s_ex[p], 1)
                    return step

                def squares(p):
                    act.wait_ge(s_yg[p], n)
                    nc.scalar.activation(YSQ[:, p], YG[:, p], ACT.Square).then_inc(s_sq[p], 1)

                def yt(p):
                    act.wait_ge(s_ytp[p], n)
                    nc.scalar.activation(YT[:, p], bank(p, 2, 0, T), ACT.Copy).then_inc(s_yt[p], 1)

                def relu(p):
                    act.wait_ge(s_hp[p], n)
                    nc.scalar.activation(HT[:, p], bank(p, 3, 0, T)[0:32], ACT.Relu).then_inc(s_ht[p], 1)

                def score(p):
                    act.wait_ge(s_zsp[p], n)
                    nc.scalar.activation(SC[:, p], bank(p, 0, 0, T), ACT.Tanh, scale=0.5).then_inc(s_tsc[p], 1)

                def kv(p):
                    act.wait_ge(s_kv[p], n)
                    nc.scalar.activation(KA[:, p], bank(p, 3, 256, 256 + POOL), ACT.Copy).then_inc(s_ka[p], 1)
                    nc.scalar.activation(VSEL[0:POOL, p], bank(p, 2, 256, 512)[0:POOL], ACT.Copy).then_inc(s_vs[p], 1)

                def exps(p):
                    act.wait_ge(s_sub[p], n)
                    nc.scalar.activation(LG[:, p], LG[:, p], ACT.Exp, scale=0.25).then_inc(s_ep[p], 1)

                def prt(p):
                    act.wait_ge(s_prt[p], n)
                    nc.scalar.activation(PRT[0:POOL, p], bank(p, 3, 0, T)[0:POOL], ACT.Copy).then_inc(s_prc[p], 1)

                def tanh_gate(p):
                    act.wait_ge(s_rg[p], n)
                    nc.scalar.activation(TG[:, p], bank(p, 1).rearrange("p (t c) -> p t c", t=TT)[:, :, D:2 * D],
                                         ACT.Tanh, scale=0.5).then_inc(s_tg[p], 1)

                for step in (tanh_z, conv_in, tanh_x, tanh_bc, decays(0), decays(1), squares, yt, relu, score, kv, exps,
                             prt, tanh_gate):
                    for p in slots:
                        step(p)

        @block.tensor
        def _(pe):
            pe.wait_ge(s_w2, 1)
            with pe.Fori(0, TURNS) as j:
                n = j + 1

                def in_proj(p):
                    pe.wait_ge(s_gr[p], j)
                    rhs = k.XNT[:, bass.ds((8 * p + j) * T, T)]
                    for i, ct in enumerate((0, 1)):
                        last = nc.tensor.matmul(bank(p, 2, i * T, i * T + T), k.w("inw")[:, ct * P:ct * P + P], rhs,
                                                start=True, stop=True)
                    last.then_inc(s_inz[p], 1)
                    for i, ct in enumerate((2, 3)):
                        last = nc.tensor.matmul(bank(p, 0, i * T, i * T + T), k.w("inw")[:, ct * P:ct * P + P],
                                                rhs, start=True, stop=True)
                    last.then_inc(s_in[p], 1)
                    for i in range(2):
                        for back in range(TAPS):
                            w = k.w("tapbc")[:, 2 * P * (TAPS - 1 - back) + i * P:2 * P * (TAPS - 1 - back) + i * P + P]
                            last = nc.tensor.matmul(bank(p, 1, i * T + back, i * T + T), w,
                                                    k.XNT[:, bass.ds((8 * p + j) * T, T - back)], start=(back == 0),
                                                    stop=(back == TAPS - 1))
                    last.then_inc(s_inbc[p], 1)

                def x_tokens(p):
                    pe.wait_ge(s_xs[p], n)
                    for t in range(TT):
                        for ct in range(2):
                            last = nc.tensor.transpose(bank(p, 3, (2 * t + ct) * P, (2 * t + ct) * P + P),
                                                       XS[:, p, ct, t * P:t * P + P], k.c("ident"))
                    last.then_inc(s_xt[p], 1)

                def b_c(p):
                    pe.wait_ge(s_bc[p], n)
                    pe.wait_ge(s_zz[p], n)
                    nc.tensor.matmul(bank(p, 2, 0, T), XS[:, p, 2, 0:P], XS[:, p, 3], start=True, stop=True)
                    nc.tensor.matmul(bank(p, 2, T, T + P), XS[:, p, 2, P:T], XS[:, p, 3, P:T], start=True,
                                     stop=True).then_inc(s_g[p], 1)

                def decay(i):
                    def step(p):
                        if i == 0:
                            pe.wait_ge(s_cb[p], n)
                            pe.wait_ge(s_thb[p], n)
                        else:
                            pe.wait_ge(s_ex[p], 2 * j + 1)
                        for h in (0, 1):
                            one = k.SEL[:, bass.ds(MH * j + 2 * i + h, 1), :].rearrange("p a c -> p (a c)")
                            for s in range(TT):
                                w = T - s * P
                                o = bank(p, h, s * T, s * T + w)
                                nc.tensor.matmul(o, one[:, 0:P], k.CUMT[:, p, s:].rearrange("p t c -> p (t c)"),
                                                 start=True, stop=False)
                                nc.tensor.matmul(o, k.NCUMT[:, p, s], one[:, 0:w], start=False, stop=False)
                                last = nc.tensor.matmul(o[:, 0:P], k.IDB[:], k.LATER[:], start=False, stop=True)
                        last.then_inc(s_dec[p], 1)
                    return step

                def scan(p):
                    pe.wait_ge(s_m[p], n)
                    pe.wait_ge(s_dtx[p], n)
                    for h in range(MH):
                        o = bank(p, 0, h // 2 * T, h // 2 * T + T)[MP * (h % 2):MP * (h % 2) + MP]
                        nc.tensor.matmul(o, DTX[:, p, h], EX[:, p, h, 0:T], start=True, stop=False)
                        last = nc.tensor.matmul(o[:, P:T], DTX[:, p, MH + h], EX[:, p, h, T:T + P], start=False, stop=True)
                    last.then_inc(s_y[p], 1)

                def out_proj(p):
                    pe.wait_ge(s_sq[p], n)
                    for t in range(TT):
                        for ct in range(2):
                            nc.tensor.matmul(bank(p, 1, t * D, t * D + D), YG[:, p, ct, t * P:t * P + P],
                                             k.w("outw")[:, ct * D:ct * D + D], start=(ct == 0), stop=(ct == 1))
                    for t in range(TT):
                        for ct in range(2):
                            last = nc.tensor.matmul(bank(p, 1, T + t, T + t + 1), YSQ[:, p, ct, t * P:t * P + P],
                                                    k.c("ones")[:, 0:1], start=(ct == 0), stop=(ct == 1))
                    last.then_inc(s_yo[p], 1)

                def y_turn(p):
                    pe.wait_ge(s_yoc[p], n)
                    for t in range(TT):
                        last = nc.tensor.transpose(bank(p, 2, t * P, t * P + P), YO[:, p, t], k.c("ident"))
                    last.then_inc(s_ytp[p], 1)

                def hidden(p):
                    pe.wait_ge(s_yt[p], n)
                    nc.tensor.matmul(bank(p, 3, 0, T)[0:32], k.w("w1"), YT[:, p], start=True, stop=True).then_inc(s_hp[p], 1)

                def score(p):
                    pe.wait_ge(s_ht[p], n)
                    nc.tensor.matmul(bank(p, 0, 0, T), W2[:], HT[:, p], start=True, stop=True).then_inc(s_zsp[p], 1)

                def score_turn(p):
                    pe.wait_ge(s_sc[p], n)
                    alone(pe)
                    for t in range(TT):
                        last = nc.tensor.transpose(bank(p, 0, T + t, T + t + 1), SC[0:1, p, t * P:t * P + P],
                                                   k.c("ident")[0:1, 0:1])
                    last.then_inc(s_sct[p], 1)

                def select(p):
                    pe.wait_ge(s_pick[p], n)
                    for t in range(TT):
                        nc.tensor.matmul(bank(p, 1, 0, POOL), YO[:, p, t], PICK[:, p, t], start=(t == 0), stop=(t == TT - 1))
                    for t in range(TT):
                        last = nc.tensor.matmul(bank(p, 1, 64, 64 + POOL)[0:1], k.c("ones")[:, 0:1], PICK[:, p, t],
                                                start=(t == 0), stop=(t == TT - 1))
                    last.then_inc(s_self[p], 1)

                def keys_values(p):
                    pe.wait_ge(s_ysel[p], n)
                    nc.tensor.matmul(bank(p, 3, 256, 256 + POOL), k.AT[:], YSEL[:, p], start=True, stop=True)
                    nc.tensor.matmul(bank(p, 2, 256, 512)[0:POOL], YSEL[:, p], k.VV[:], start=True,
                                     stop=True).then_inc(s_kv[p], 1)

                def logits(p):
                    pe.wait_ge(s_ka[p], n)
                    for t in range(TT):
                        o = bank(p, 0, t * POOL, t * POOL + POOL)
                        nc.tensor.matmul(o, YT[:, p, t * P:t * P + P], KA[:, p], start=True, stop=False)
                        last = nc.tensor.matmul(o, k.c("ones")[0:1], EMPTY[:, p], start=False, stop=True)
                    last.then_inc(s_lg[p], 1)

                def probs_turn(p):
                    pe.wait_ge(s_pr[p], n)
                    alone(pe)
                    for t in range(TT):
                        last = nc.tensor.transpose(bank(p, 3, t * P, t * P + P)[0:POOL], LG[:, p, t], k.c("ident"))
                    last.then_inc(s_prt[p], 1)

                def retrieve(p):
                    pe.wait_ge(s_prc[p], n)
                    pe.wait_ge(s_vs[p], n)
                    for t in range(TT):
                        o = bank(p, 1, t * 2 * D, (t + 1) * 2 * D)
                        nc.tensor.matmul(o, PRT[:, p, t * P:t * P + P], VSEL[:, p], start=True, stop=False)
                        last = nc.tensor.matmul(o[:, D:2 * D], YT[:, p, t * P:t * P + P], k.w("g1"), start=False, stop=True)
                    last.then_inc(s_rg[p], 1)

                for step in (in_proj, x_tokens, b_c, decay(0), decay(1), scan, out_proj, y_turn, hidden, score,
                             score_turn, select, keys_values, logits, probs_turn, retrieve):
                    for p in slots:
                        step(p)


def ffn_tokens(nc, sb, ps, sem, k, layer):
    norm = layer == 0
    X, XF = k.X, (k.XF if norm else k.X)
    router = k.cf("router0" if norm else "router1")
    BN = sb("BNF", [P, SLOTS, 4, 6])
    MV = sb("MVF", [P, SLOTS, 4, 2])
    XN = sb("XNF", [P, SLOTS, 4, D])
    XS4 = sb("XS4", [P, SLOTS, 4, D])
    XFS = sb("XFS", [P, SLOTS, 4 * P])

    def two(name):
        return [sem(f"{name}{p}") for p in range(SLOTS)]

    s_link = sem("token_links")
    s_var, s_rstd, s_xf = two("f_variance"), two("f_rstd"), two("f_tokens")
    s_xfk = two("f_tokens_kept")
    s_tr, s_ev, s_kept, s_lg, s_lgc = two("f_turned"), two("f_turned_kept"), two("f_turned_copied"), two("f_logits"), two("f_logits_kept")
    slots, turns = range(SLOTS), UNITS // SLOTS

    def tiles(p, j):
        return bass.ds((turns * p + j) * 4, 4)

    with nc.Block() as block:
        @block.gpsimd
        def _(pool):
            with pool.Fori(0, turns) as j:
                if norm:
                    for p in slots:
                        pool.wait_ge(s_var[p], j + 1)
                        nc.gpsimd.tensor_tensor(MV[:, p, :, 1:2], MV[:, p, :, 1:2], k.POWER[:, 0:4].unsqueeze(2),
                                                ALU.pow).then_inc(s_rstd[p], 1)
                    for p in slots:
                        pool.wait_ge(s_xf[p], j + 1)
                        nc.gpsimd.tensor_copy(XF[:, tiles(p, j), :], XS4[:, p]).then_inc(s_xfk[p], 1)
                else:
                    for p in slots:
                        pool.wait_ge(s_tr[p], j)
                        nc.gpsimd.tensor_copy(XS4[:, p], X[:, tiles(p, j), :]).then_inc(s_xf[p], 1)
                for p in slots:
                    pool.wait_ge(s_ev[p], j + 1)
                    nc.gpsimd.tensor_copy(k.XNT[:, bass.ds((turns * p + j) * 512, 512)], XFS[:, p]).then_inc(s_kept[p], 1)

        @block.vector
        def _(dve):
            with dve.Fori(0, turns) as j:
                link = Links(dve, s_link, 4 * SLOTS if norm else 0, j)
                if norm:
                    for p in slots:
                        dve.wait_ge(s_xf[p], j)
                        for t in range(4):
                            x = X[:, bass.ds((turns * p + j) * 4 + t, 1), :].rearrange("p a d -> p (a d)")
                            last = nc.vector.bn_stats(BN[:, p, t], x)
                        link(last)
                        alone(dve)
                        for t in range(4):
                            last = nc.vector.bn_aggr(MV[:, p, t], BN[:, p, t])
                        link(last)
                        nc.vector.tensor_scalar(MV[:, p, :, 1:2], MV[:, p, :, 1:2], EPS, None, ALU.add).then_inc(s_var[p], 1)
                    for p in slots:
                        dve.wait_ge(s_rstd[p], j + 1)
                        for t in range(4):
                            x = X[:, bass.ds((turns * p + j) * 4 + t, 1), :].rearrange("p a d -> p (a d)")
                            last = nc.vector.tensor_scalar(XN[:, p, t], x, MV[:, p, t, 0:1], MV[:, p, t, 1:2],
                                                           ALU.subtract, ALU.mult)
                        link(last)
                        link(nc.vector.tensor_tensor(XN[:, p], XN[:, p], k.cf("lnw").unsqueeze(1).broadcast_to((P, 4, D)),
                                                     ALU.mult))
                        dve.wait_ge(s_tr[p], j)
                        dve.wait_ge(s_xfk[p], j)
                        nc.vector.tensor_tensor(XS4[:, p], XN[:, p],
                                                k.cf("lnb").unsqueeze(1).broadcast_to((P, 4, D)), ALU.add).then_inc(s_xf[p], 1)
                for p in slots:
                    dve.wait_ge(s_lg[p], j + 1)
                    nc.vector.tensor_copy(k.LOG[:, :, tiles(p, j)],
                                          ps[:, 1024 + 512 * p:1056 + 512 * p].rearrange("p (n e) -> p e n", e=NE)
                                          ).then_inc(s_lgc[p], 1)
                link.close()

        @block.scalar
        def _(act):
            with act.Fori(0, turns) as j:
                for p in slots:
                    act.wait_ge(s_tr[p], j + 1)
                    act.wait_ge(s_kept[p], j)
                    act.wait_ge(s_lg[p], j)
                    nc.scalar.activation(XFS[:, p], ps[:, 512 * p:512 * p + 512], ACT.Copy).then_inc(s_ev[p], 1)

        @block.tensor
        def _(pe):
            with pe.Fori(0, turns) as j:
                for p in slots:
                    pe.wait_ge(s_xf[p], j + 1)
                    pe.wait_ge(s_ev[p], j)
                    for t in range(4):
                        last = nc.tensor.transpose(ps[:, 512 * p + P * t:512 * p + P * t + P], XS4[:, p, t], k.c("ident"))
                    last.then_inc(s_tr[p], 1)
                for p in slots:
                    pe.wait_ge(s_ev[p], j + 1)
                    pe.wait_ge(s_lgc[p], j)
                    for t in range(4):
                        last = nc.tensor.matmul(ps[:, 1024 + 512 * p + NE * t:1024 + 512 * p + NE * t + NE],
                                                XFS[:, p, P * t:P * t + P], router, start=True, stop=True)
                    last.then_inc(s_lg[p], 1)


def route(nc, sb, ps, sem, k, layer, choices):
    OH = [sb(f"OH{c}", [P, NE, NT]) for c in range(choices)]
    EQ = sb("EQ", [P, NE, NT])
    MX = [sb(f"MXR{c}", [P, NT]) for c in range(choices)]
    FI = sb("FI", [P, NT])
    CI = sb("CI", [P, NE, NT])
    ENDS, NTL, START, OFF, ZERO = (sb(n, [P, NE]) for n in ("ENDS", "NTL", "START", "OFF", "ZERO"))
    GT = sb("GT", [P, NE, NT])
    POSF = sb("POSF", [P, NE, NT])
    POS1 = sb("POS1", [P, NT])
    TE = sb("TE", [1, TILES, NE - 1])
    TEF = sb("TEF", [1, TILES])
    s_link, s_mx, s_sig, s_oh, s_cnt, s_done = (sem(n) for n in (
        "route_links", "best_logit", "route_tanh", "experts_marked", "counted", "routed"))
    with nc.Block() as block:
        @block.vector
        def _(dve):
            link = Links(dve, s_link)
            link(nc.vector.memset(ZERO[:], 0.0))
            rev = k.c("eight").unsqueeze(2).broadcast_to((P, NE, NT))
            for c in range(choices):
                nc.vector.tensor_reduce(MX[c][:], k.LOG[:].rearrange("p e n -> p n e"), AX_X, ALU.max).then_inc(s_mx, 1)
                dve.wait_ge(s_mx, c + 1)
                best = MX[c][:].unsqueeze(1).broadcast_to((P, NE, NT))
                link(nc.vector.tensor_tensor(EQ[:], k.LOG[:], best, ALU.is_equal))
                link(nc.vector.tensor_tensor(EQ[:], EQ[:], rev, ALU.mult))
                link(nc.vector.tensor_reduce(FI[:], EQ[:].rearrange("p e n -> p n e"), AX_X, ALU.max))
                nc.vector.tensor_tensor(OH[c][:], rev, FI[:].unsqueeze(1).broadcast_to((P, NE, NT)),
                                        ALU.is_equal).then_inc(s_oh, 1)
                if c + 1 < choices:
                    dve.wait_ge(s_oh, c + 1)
                    link(nc.vector.scalar_tensor_tensor(k.LOG[:], OH[c][:], -BIG, k.LOG[:], ALU.mult, ALU.add))
            for c in range(choices):
                dve.wait_ge(s_sig, c + 1)
                nc.vector.tensor_scalar(k.GATE[:, c], k.GATE[:, c], 0.5, 0.5, ALU.mult, ALU.add)
                dve.wait_ge(s_cnt, c + 1)
                within = ps[:, 1024 * c:1024 * c + 256].rearrange("p (e n) -> p e n", e=NE)
                total = ps[:, 1024 * c + 512:1024 * c + 768]
                link(nc.vector.tensor_tensor_scan(CI[:].rearrange("p e n -> p (e n)"), k.c("ones2"), total, 0.0,
                                                  ALU.mult, ALU.add))
                link(nc.vector.tensor_copy(ENDS[:], CI[:, :, NT - 1]))
                nc.vector.tensor_copy(OFF[:, 0:1], ZERO[:, 0:1])
                link(nc.vector.tensor_copy(OFF[:, 1:NE], ENDS[:, 0:NE - 1]))
                link(nc.vector.tensor_tensor(ENDS[:], ENDS[:], OFF[:], ALU.subtract))
                link(nc.vector.tensor_tensor(GT[:], ENDS[:].unsqueeze(2).broadcast_to((P, NE, NT)),
                                             k.c("m128").unsqueeze(1).broadcast_to((P, NE, NT)), ALU.is_gt))
                link(nc.vector.tensor_reduce(NTL[:], GT[:], AX_X, ALU.add))
                link(nc.vector.tensor_tensor_scan(START[:], k.c("ones2")[:, 0:NE], NTL[:], 0.0, ALU.mult, ALU.add))
                link(nc.vector.tensor_tensor(START[:], START[:], NTL[:], ALU.subtract))
                link(nc.vector.scalar_tensor_tensor(OFF[:], START[:], float(P), OFF[:], ALU.mult, ALU.subtract))
                link(nc.vector.tensor_tensor(CI[:].rearrange("p e n -> p (e n)"), CI[:].rearrange("p e n -> p (e n)"),
                                             total, ALU.subtract))
                link(nc.vector.tensor_tensor(POSF[:], CI[:], within, ALU.add))
                link(nc.vector.tensor_tensor(POSF[:], POSF[:], OFF[:].unsqueeze(2).broadcast_to((P, NE, NT)), ALU.add))
                link(nc.vector.tensor_tensor(POSF[:], POSF[:], OH[c][:], ALU.mult))
                link(nc.vector.tensor_reduce(POS1[:], POSF[:].rearrange("p e n -> p n e"), AX_X, ALU.add))
                nc.vector.tensor_copy(k.POS[:, c], POS1[:])
                link(nc.vector.tensor_tensor(TE[:], START[0:1, 1:NE].unsqueeze(1).broadcast_to((1, TILES, NE - 1)),
                                             k.c("tile")[0:1].unsqueeze(2).broadcast_to((1, TILES, NE - 1)), ALU.is_le))
                link(nc.vector.tensor_reduce(TEF[:], TE[:], AX_X, ALU.add))
                link(nc.vector.tensor_copy(k.TEX[:, c], TEF[:]))

        @block.scalar
        def _(act):
            for c in range(choices):
                act.wait_ge(s_mx, c + 1)
                nc.scalar.activation(k.GATE[:, c], MX[c][:], ACT.Tanh, scale=0.5).then_inc(s_sig, 1)

        @block.tensor
        def _(pe):
            for c in range(choices):
                pe.wait_ge(s_oh, c + 1)
                oh = OH[c][:].rearrange("p e n -> p (e n)")
                nc.tensor.matmul(ps[:, 1024 * c:1024 * c + 256], k.c("ahead"), oh, start=True, stop=True)
                nc.tensor.matmul(ps[:, 1024 * c + 512:1024 * c + 768], k.c("ones"), oh, start=True,
                                 stop=True).then_inc(s_cnt, 1)


FLOW = 4


def experts(nc, sb, ps, sem, dram, k, layer, choices):
    W1, WD = k.W1, k.WD
    XF = k.XF if layer == 0 else k.X
    X = k.X
    xs = [dram["sorted"][c] for c in range(2)]
    ys = [dram["expert_out"][c] for c in range(2)]
    ZS = sb("ZS", [P, FLOW, D])
    IX = sb("IX", [P, FLOW, 1], U32)
    XG = sb("XG", [P, FLOW, D])
    XGT = sb("XGT", [P, FLOW, P])
    SG = sb("SG", [P, FLOW, FF])
    HG = sb("HG", [P, FLOW, FF])
    HT = sb("HTG", [P, FLOW, 2, P])
    OG = sb("OG", [P, FLOW, D])
    SS = sb("SS", [P, SLOTS, 2, 512])
    HS = sb("HS", [P, SLOTS, 2, 512])
    ACC = k.ACC
    slots, turns = range(SLOTS), UNITS // SLOTS

    def one(t, n):
        return t[:, bass.ds(n, 1), :].rearrange("p a d -> p (a d)")

    if True:
        if True:
            psem = sem
            s_z = [psem(f"row_scaled{p}") for p in range(FLOW)]
            s_sc = [psem(f"row_scattered{p}") for p in range(FLOW)]
            s_gu = [psem(f"gate_up{p}") for p in slots]
            s_si = [psem(f"silu{p}") for p in slots]
            s_h = [psem(f"shared_h{p}") for p in slots]
            s_dn = [psem(f"shared_down{p}") for p in slots]
            s_acc = [psem(f"accumulated{p}") for p in slots]
            with nc.Block() as block:
                @block.gpsimd
                def _(pool):
                    for c in range(choices):
                        with pool.Fori(0, NT // FLOW) as j:
                            for p in range(FLOW):
                                pool.wait_ge(s_z[p], c * (NT // FLOW) + j + 1)
                                alone(pool)
                                nc.gpsimd.indirect_dma_start(
                                    out=xs[c], out_offset=bass.IndirectOffsetOnAxis(ap=IX[:, p], axis=0),
                                    in_=ZS[:, p], in_offset=None).then_inc(s_sc[p], 16)
                    for p in range(FLOW):
                        pool.wait_ge(s_sc[p], 16 * choices * (NT // FLOW))

                @block.vector
                def _(dve):
                    for c in range(choices):
                        with dve.Fori(0, NT // FLOW) as j:
                            for p in range(FLOW):
                                n = FLOW * j + p
                                dve.wait_ge(s_sc[p], 16 * (c * (NT // FLOW) + j))
                                nc.vector.tensor_copy(IX[:, p], k.POS[:, c, bass.ds(n, 1)])
                                nc.vector.tensor_scalar(ZS[:, p], one(XF, n), k.GATE[:, c, bass.ds(n, 1)], None,
                                                        ALU.mult).then_inc(s_z[p], 1)
                    with dve.Fori(0, turns) as j:
                        for p in slots:
                            dve.wait_ge(s_si[p], j + 1)
                            nc.vector.tensor_tensor(HS[:, p], SS[:, p], ps[:, 2048 * p + 1024:2048 * p + 2048].rearrange(
                                "p (c t) -> p c t", c=2), ALU.mult).then_inc(s_h[p], 1)
                        for p in slots:
                            dve.wait_ge(s_dn[p], j + 1)
                            t = bass.ds((turns * p + j) * 4, 4)
                            nc.vector.scalar_tensor_tensor(
                                ACC[:, t, :], X[:, t, :], 2.0 if layer == 0 else 1.0,
                                ps[:, 2048 * p:2048 * p + 512].rearrange("p (t d) -> p t d", d=D), ALU.mult,
                                ALU.add).then_inc(s_acc[p], 1)

                @block.scalar
                def _(act):
                    with act.Fori(0, turns) as j:
                        for p in slots:
                            act.wait_ge(s_gu[p], j + 1)
                            nc.scalar.activation(SS[:, p], ps[:, 2048 * p:2048 * p + 1024].rearrange(
                                "p (c t) -> p c t", c=2), ACT.Silu).then_inc(s_si[p], 1)

                @block.tensor
                def _(pe):
                    with pe.Fori(0, turns) as j:
                        for p in slots:
                            pe.wait_ge(s_acc[p], j)
                            for i in range(4):
                                last = nc.tensor.matmul(ps[:, 2048 * p + 512 * i:2048 * p + 512 * i + 512],
                                                        W1[:, NE, i * P:i * P + P],
                                                        k.XNT[:, bass.ds((turns * p + j) * 512, 512)], start=True, stop=True)
                            last.then_inc(s_gu[p], 1)
                        for p in slots:
                            pe.wait_ge(s_h[p], j + 1)
                            for t in range(4):
                                for f in range(2):
                                    last = nc.tensor.matmul(ps[:, 2048 * p + P * t:2048 * p + P * t + P],
                                                            HS[:, p, f, P * t:P * t + P], WD[:, NE, f], start=(f == 0),
                                                            stop=(f == 1))
                            last.then_inc(s_dn[p], 1)

    for c in range(choices):
        if True:
            def four(name):
                return [sem(f"{name}{c}_{p}") for p in range(FLOW)]
            s_ld, s_xt, s_xc, s_gu, s_si, s_h, s_ht, s_hc, s_dn, s_og, s_st = (four(n) for n in (
                "rows_in", "rows_turned", "rows_copied", "e_gate_up", "e_silu", "e_h", "h_turned", "h_copied", "e_down",
                "e_out", "e_stored"))
            tt = TILES // FLOW

            def ab(p, which, a=0, z=512):
                return ps[:, (2 * p + which) * 512 + a:(2 * p + which) * 512 + z]

            with nc.Block() as block:
                @block.sync
                def _(sp):
                    with sp.Fori(0, tt) as j:
                        for p in range(FLOW):
                            sp.wait_ge(s_xt[p], j)
                            sp.dma_start(XG[:, p], xs[c][bass.ds((FLOW * j + p) * P, P), :]).then_inc(s_ld[p], 16)
                        for p in range(FLOW):
                            sp.wait_ge(s_og[p], j + 1)
                            sp.dma_start(ys[c][bass.ds((FLOW * j + p) * P, P), :], OG[:, p]).then_inc(s_st[p], 16)
                    for p in range(FLOW):
                        sp.wait_ge(s_st[p], 16 * tt)

                @block.vector
                def _(dve):
                    with dve.Fori(0, tt) as j:
                        for p in range(FLOW):
                            dve.wait_ge(s_xt[p], j + 1)
                            nc.vector.tensor_copy(XGT[:, p], ab(p, 1, 0, P)).then_inc(s_xc[p], 1)
                        for p in range(FLOW):
                            dve.wait_ge(s_si[p], j + 1)
                            nc.vector.tensor_tensor(HG[:, p], SG[:, p], ab(p, 0, FF, 2 * FF), ALU.mult).then_inc(s_h[p], 1)
                        for p in range(FLOW):
                            dve.wait_ge(s_dn[p], j + 1)
                            dve.wait_ge(s_st[p], 16 * j)
                            nc.vector.tensor_copy(OG[:, p], ab(p, 0, 0, P)).then_inc(s_og[p], 1)

                @block.scalar
                def _(act):
                    with act.Fori(0, tt) as j:
                        for p in range(FLOW):
                            act.wait_ge(s_gu[p], j + 1)
                            nc.scalar.activation(SG[:, p], ab(p, 0, 0, FF), ACT.Silu).then_inc(s_si[p], 1)
                        for p in range(FLOW):
                            act.wait_ge(s_ht[p], j + 1)
                            nc.scalar.activation(HT[:, p].rearrange("p c t -> p (c t)"), ab(p, 1, P, 3 * P),
                                                 ACT.Copy).then_inc(s_hc[p], 1)

                @block.tensor
                def _(pe):
                    with pe.Fori(0, tt) as j:
                        which = [nc.tensor.value_load(k.TEX[0:1, c, bass.ds(FLOW * j + p, 1)], min_val=0, max_val=NE - 1)
                                 for p in range(FLOW)]
                        for p in range(FLOW):
                            pe.wait_ge(s_ld[p], 16 * (j + 1))
                            pe.wait_ge(s_hc[p], j)
                            nc.tensor.transpose(ab(p, 1, 0, P), XG[:, p], k.c("ident")).then_inc(s_xt[p], 1)
                        for p in range(FLOW):
                            pe.wait_ge(s_xc[p], j + 1)
                            pe.wait_ge(s_og[p], j)
                            nc.tensor.matmul(ab(p, 0), XGT[:, p], W1[:, bass.ds(which[p], 1), :].rearrange("p a f -> p (a f)"),
                                             start=True, stop=True).then_inc(s_gu[p], 1)
                        for p in range(FLOW):
                            pe.wait_ge(s_h[p], j + 1)
                            for f in range(2):
                                last = nc.tensor.transpose(ab(p, 1, P + f * P, 2 * P + f * P), HG[:, p, f * P:f * P + P],
                                                           k.c("ident"))
                            last.then_inc(s_ht[p], 1)
                        for p in range(FLOW):
                            pe.wait_ge(s_hc[p], j + 1)
                            for f in range(2):
                                last = nc.tensor.matmul(ab(p, 0, 0, P), HT[:, p, f],
                                                        WD[:, bass.ds(which[p], 1), f].rearrange("p a f -> p (a f)"),
                                                        start=(f == 0), stop=(f == 1))
                            last.then_inc(s_dn[p], 1)

    YB = sb("YB", [P, FLOW, choices, D])
    IXB = sb("IXB", [P, FLOW, choices], U32)
    WX = sb("WXF", [P, FLOW, D])
    BN = sb("BNX", [P, FLOW, 6])
    MV = sb("MVX", [P, FLOW, 2])
    if True:
        psem = sem
        s_ix, s_back, s_sum, s_var, s_rstd, s_x = ([psem(f"{n}{p}") for p in range(FLOW)] for n in (
            "places", "rows_back", "rows_added", "x_variance", "x_rstd", "x_normed"))
        s_link = psem("back_links")
        with nc.Block() as block:
            @block.gpsimd
            def _(pool):
                with pool.Fori(0, NT // FLOW) as j:
                    for p in range(FLOW):
                        pool.wait_ge(s_ix[p], j + 1)
                        pool.wait_ge(s_sum[p], j)
                        alone(pool)
                        for c in range(choices):
                            nc.gpsimd.indirect_dma_start(
                                out=YB[:, p, c], out_offset=None, in_=ys[c],
                                in_offset=bass.IndirectOffsetOnAxis(ap=IXB[:, p, c:c + 1], axis=0)).then_inc(s_back[p], 16)
                    for p in range(FLOW):
                        pool.wait_ge(s_var[p], j + 1)
                        nc.gpsimd.tensor_tensor(MV[:, p, 1:2], MV[:, p, 1:2], k.POWER[:, 0:1], ALU.pow).then_inc(s_rstd[p], 1)

            @block.vector
            def _(dve):
                with dve.Fori(0, NT // FLOW) as j:
                    link = Links(dve, s_link, FLOW * (choices + 1), j)
                    for p in range(FLOW):
                        dve.wait_ge(s_back[p], 16 * choices * j)
                        nc.vector.tensor_copy(IXB[:, p, 0:choices], k.POS[:, 0:choices, bass.ds(FLOW * j + p, 1)].rearrange(
                            "p c a -> p (c a)")).then_inc(s_ix[p], 1)
                    for p in range(FLOW):
                        dve.wait_ge(s_back[p], 16 * choices * (j + 1))
                        dve.wait_ge(s_x[p], j)
                        for c in range(choices):
                            ins = nc.vector.tensor_tensor(WX[:, p], YB[:, p, c], WX[:, p] if c else one(ACC, FLOW * j + p), ALU.add)
                            if c + 1 < choices:
                                link(ins)
                        ins.then_inc(s_sum[p], 1)
                        dve.wait_ge(s_sum[p], j + 1)
                        link(nc.vector.bn_stats(BN[:, p], WX[:, p]))
                        alone(dve)
                        link(nc.vector.bn_aggr(MV[:, p], BN[:, p]))
                        nc.vector.tensor_scalar(MV[:, p, 1:2], MV[:, p, 1:2], EPS, None, ALU.add).then_inc(s_var[p], 1)
                    for p in range(FLOW):
                        dve.wait_ge(s_rstd[p], j + 1)
                        nc.vector.tensor_scalar(one(X, FLOW * j + p), WX[:, p], MV[:, p, 0:1], MV[:, p, 1:2],
                                                ALU.subtract, ALU.mult).then_inc(s_x[p], 1)
                    link.close()


AH, AD = 16, 8
PAIRS = [(0, 0), (0, 1), (0, 2), (1, 0), (1, 1), (2, 0)]
HROWS = AD * len(PAIRS) + 6
MROW = 2 * HROWS
GROUPS = AH // 2


def alibi_parts(h):
    return 1 if h % 2 else 3


def alibi_at(h):
    return h // 2 * 4 + (3 if h % 2 else 0)


def qkv(nc, sb, ps, sem, dram, k):
    XS4 = sb("AXS4", [P, SLOTS, 4, D])
    XTS = sb("XTS", [P, SLOTS, 512])
    QF = sb("QF", [P, SLOTS, 2, 512])
    WQ = sb("WQ", [P, 3 * D])
    BQ = sb("BQ", [P, 2])
    BV = sb("BV", [P, D])
    slots, turns = range(SLOTS), UNITS // SLOTS
    s_w, s_b, s_one, s_bq = sem("qkv_loaded"), sem("attn_consts_loaded"), sem("ones_set"), sem("bias_scaled")
    s_link = sem("qkv_links")

    def two(name):
        return [sem(f"{name}{p}") for p in slots]

    s_x, s_tr, s_xt, s_qk, s_v, s_qf, s_vx, s_parts = (two(n) for n in (
        "a_tokens", "a_turned", "a_turned_kept", "qk_psum", "v_psum", "qk_kept", "v_kept", "qk_parts"))

    def bank(p, n, a=0, z=512):
        return ps[:, (4 * p + n) * 512 + a:(4 * p + n) * 512 + z]

    with nc.Block() as block:
        @block.sync
        def _(sp):
            sp.dma_start(WQ[:], dram["wqkv"]).then_inc(s_w, 16)
            sp.dma_start(BQ[:], dram["bqk"]).then_inc(s_w, 16)
            sp.dma_start(BV[:], dram["bv"]).then_inc(s_w, 16)
            for p in slots:
                sp.dma_start(k.QA[:, p], dram["qrows"]).then_inc(s_b, 16)
                sp.dma_start(k.KA[:, p], dram["krows"]).then_inc(s_b, 16)
            sp.dma_start(k.SI[:], dram["slopes"]).then_inc(s_b, 16)
            sp.dma_start(k.DL[:], dram["ramps"]).then_inc(s_b, 16)
            sp.dma_start(k.WP[:], dram["wproj"]).then_inc(s_b, 16)
            sp.wait_ge(s_b, 16 * (2 * SLOTS + 3))

        @block.gpsimd
        def _(pool):
            nc.gpsimd.memset(k.VX[:], 1.0).then_inc(s_one, 1)
            with pool.Fori(0, turns) as j:
                for p in slots:
                    pool.wait_ge(s_tr[p], j)
                    nc.gpsimd.tensor_copy(XS4[:, p], k.X[:, bass.ds((turns * p + j) * 4, 4), :]).then_inc(s_x[p], 1)

        @block.vector
        def _(dve):
            dve.wait_ge(s_w, 48)
            nc.vector.tensor_scalar(BQ[:, 0:1], BQ[:, 0:1], AD ** -0.5, None, ALU.mult).then_inc(s_bq, 1)
            dve.wait_ge(s_one, 1)
            with dve.Fori(0, turns) as j:
                link = Links(dve, s_link, 3 * 2 * SLOTS, j)
                for p in slots:
                    dve.wait_ge(s_v[p], j + 1)
                    for t in range(4):
                        last = nc.vector.tensor_tensor(
                            k.VX[:, bass.ds((turns * p + j) * 4 + t, 1), :, 0:AD].rearrange("p a h d -> p (a h) d"),
                            bank(p, 3, t * P, t * P + P).rearrange("p (h d) -> p h d", h=AH),
                            BV[:].rearrange("p (h d) -> p h d", h=AH), ALU.add)
                    last.then_inc(s_vx[p], 1)
                    dve.wait_ge(s_qf[p], j + 1)
                    cols = bass.ds((turns * p + j) * 512, 512)
                    for i, parts in enumerate((k.QP, k.KP)):
                        link(nc.vector.tensor_copy(parts[:, 0, cols], QF[:, p, i]))
                        link(nc.vector.tensor_tensor(QF[:, p, i], QF[:, p, i], parts[:, 0, cols], ALU.subtract))
                        link(nc.vector.tensor_copy(parts[:, 1, cols], QF[:, p, i]))
                        last = nc.vector.tensor_tensor(parts[:, 2, cols], QF[:, p, i], parts[:, 1, cols], ALU.subtract)
                    last.then_inc(s_parts[p], 1)
                link.close()

        @block.scalar
        def _(act):
            act.wait_ge(s_bq, 1)
            with act.Fori(0, turns) as j:
                for p in slots:
                    act.wait_ge(s_tr[p], j + 1)
                    act.wait_ge(s_v[p], j)
                    nc.scalar.activation(XTS[:, p], bank(p, 0), ACT.Copy).then_inc(s_xt[p], 1)
                for p in slots:
                    act.wait_ge(s_qk[p], j + 1)
                    act.wait_ge(s_parts[p], j)
                    nc.scalar.activation(QF[:, p, 0], bank(p, 1), ACT.Identity, bias=BQ[:, 0:1], scale=AD ** -0.5)
                    nc.scalar.activation(QF[:, p, 1], bank(p, 2), ACT.Identity, bias=BQ[:, 1:2]).then_inc(s_qf[p], 1)

        @block.tensor
        def _(pe):
            pe.wait_ge(s_w, 48)
            with pe.Fori(0, turns) as j:
                for p in slots:
                    pe.wait_ge(s_x[p], j + 1)
                    pe.wait_ge(s_xt[p], j)
                    for t in range(4):
                        last = nc.tensor.transpose(bank(p, 0, P * t, P * t + P), XS4[:, p, t], k.c("ident"))
                    last.then_inc(s_tr[p], 1)
                for p in slots:
                    pe.wait_ge(s_xt[p], j + 1)
                    pe.wait_ge(s_qf[p], j)
                    pe.wait_ge(s_vx[p], j)
                    for i in range(2):
                        last = nc.tensor.matmul(bank(p, 1 + i), WQ[:, i * D:i * D + D], XTS[:, p], start=True, stop=True)
                    last.then_inc(s_qk[p], 1)
                    for t in range(4):
                        last = nc.tensor.matmul(bank(p, 3, P * t, P * t + P), XTS[:, p, P * t:P * t + P], WQ[:, 2 * D:3 * D],
                                                start=True, stop=True)
                    last.then_inc(s_v[p], 1)


def attention(nc, sb, ps, sem, k):
    PR = sb("PRA", [P, 2, 4, 512])
    MX = sb("MXA", [P, SLOTS, TT, AH])
    MR = sb("MRA", [P, SLOTS, TT, AH])
    MP = sb("MPA", [P, SLOTS, TT, 3, AH], BF16)
    MT = sb("MTA", [3 * AH, SLOTS, T], BF16)
    OS = sb("OSA", [P, SLOTS, 4 * T])
    RC = sb("RCA", [P, SLOTS, TT, AH])
    YA = sb("YAA", [P, SLOTS, TT, D])
    YAT = sb("YATA", [P, SLOTS, T])
    WX = sb("WXA", [P, SLOTS, TT, D])
    BN = sb("BNA", [P, SLOTS, TT, 6])
    MV = sb("MVA", [P, SLOTS, TT, 2])
    VS = sb("VSA", [P, SLOTS, TT, AH, AD + 1])
    X = k.X
    psb = ps[:].bitcast(BF16)
    slots, turns = range(SLOTS), B // SLOTS
    s_link = sem("attn_links")
    s_s1, s_mx, s_s2, s_ex = sem("scores"), sem("maxima"), sem("scores_turned"), sem("exps")

    def two(name):
        return [sem(f"{name}{p}") for p in slots]

    s_q, s_mp, s_mt, s_mc, s_m, s_pv, s_vs = (two(n) for n in (
        "qk_rows", "max_parts", "max_turned", "max_kept", "max_rows", "values_mixed", "v_slot"))
    s_os, s_ot, s_ya, s_yt, s_yc, s_pj, s_wx, s_var, s_rs, s_x = (two(n) for n in (
        "mixed_kept", "mixed_turned", "y_heads", "yh_turned", "yh_kept", "projected", "ax_sum", "a_variance", "a_rstd",
        "ax_normed"))

    def pair(g):
        return 1024 * (g % 2)

    def obank(p, a=0, z=1024):
        return ps[:, 2048 + 1024 * p + a:2048 + 1024 * p + z]

    with nc.Block() as block:
        @block.sync
        def _(sp):
            with sp.Fori(0, turns) as j:
                def rows(p):
                    sp.wait_ge(s_pv[p], 4 * j)
                    cols = bass.ds((turns * p + j) * T, T)
                    for hh in range(2):
                        for c, (a, b) in enumerate(PAIRS):
                            r = HROWS * hh + AD * c
                            sp.dma_start(k.QA[r:r + AD, p, :, hh, :], k.QP[64 * hh:64 * hh + 64, a, cols]).then_inc(s_q[p], 16)
                            sp.dma_start(k.KA[r:r + AD, p, :, :], k.KP[64 * hh:64 * hh + 64, b, cols]).then_inc(s_q[p], 16)

                def maxima(p):
                    sp.wait_ge(s_mc[p], j + 1)
                    sp.dma_start(k.QA[MROW:MROW + 3, p].rearrange("p a b t -> p (a b) t"),
                                 MT[:, p]).then_inc(s_m[p], 16)

                for step in (rows, maxima):
                    for p in slots:
                        step(p)

        @block.gpsimd
        def _(pool):
            with pool.Fori(0, turns) as j:
                for p in slots:
                    pool.wait_ge(s_pv[p], 4 * j)
                    nc.gpsimd.tensor_copy(VS[:, p], k.VX[:, bass.ds((turns * p + j) * TT, TT), :, :]).then_inc(s_vs[p], 1)
                for p in slots:
                    pool.wait_ge(s_var[p], j + 1)
                    nc.gpsimd.tensor_tensor(MV[:, p, :, 1:2], MV[:, p, :, 1:2], k.POWER[:, 0:TT].unsqueeze(2),
                                            ALU.pow).then_inc(s_rs[p], 1)

        @block.vector
        def _(dve):
            with dve.Fori(0, turns) as j:
                link = Links(dve, s_link, SLOTS * 7, j)

                def maxima(p):
                    for g in range(GROUPS):
                        i = GROUPS * p + g
                        dve.wait_ge(s_s1, 2 * GROUPS * j + i + 1)
                        nc.vector.tensor_reduce(MX[:, p].rearrange("p t h -> p h t")[:, 2 * g:2 * g + 2],
                                                ps[:, pair(g):pair(g) + 1024].rearrange("p (h t s) -> p h t s", h=2, t=TT),
                                                AX_X, ALU.max).then_inc(s_mx, 1)
                    dve.wait_ge(s_mx, 2 * GROUPS * j + GROUPS * (p + 1))
                    link(nc.vector.tensor_scalar(MP[:, p, :, 0], MX[:, p], -1.0, None, ALU.mult))
                    link(nc.vector.scalar_tensor_tensor(MR[:, p], MX[:, p], -1.0, MP[:, p, :, 0], ALU.mult, ALU.subtract))
                    link(nc.vector.tensor_copy(MP[:, p, :, 1], MR[:, p]))
                    nc.vector.tensor_tensor(MP[:, p, :, 2], MR[:, p], MP[:, p, :, 1], ALU.subtract).then_inc(s_mp[p], 1)

                def kept(p):
                    dve.wait_ge(s_pv[p], 4 * (j + 1))
                    nc.vector.tensor_copy(OS[:, p], obank(p)).then_inc(s_os[p], 1)

                def heads(p):
                    dve.wait_ge(s_ot[p], j + 1)
                    o = obank(p).rearrange("p (t h c) -> p t h c", t=TT, h=AH)
                    for t in range(TT):
                        last = nc.vector.reciprocal(RC[:, p, t], o[:, t, :, AD])
                    link(last)
                    for t in range(TT):
                        last = nc.vector.tensor_tensor(YA[:, p, t].rearrange("p (h d) -> p h d", h=AH), o[:, t, :, 0:AD],
                                                       spread(RC[:, p, t], AD), ALU.mult)
                    last.then_inc(s_ya[p], 1)

                def sums(p):
                    xs = X[:, bass.ds(2 * (turns * p + j), 2), :]
                    dve.wait_ge(s_pj[p], j + 1)
                    link(nc.vector.tensor_tensor(WX[:, p], xs, obank(p, 512, 768).rearrange("p (t d) -> p t d", d=D), ALU.add))
                    for t in range(TT):
                        last = nc.vector.bn_stats(BN[:, p, t], WX[:, p, t])
                    link(last)
                    alone(dve)
                    for t in range(TT):
                        last = nc.vector.bn_aggr(MV[:, p, t], BN[:, p, t])
                    link(last)
                    nc.vector.tensor_scalar(MV[:, p, :, 1:2], MV[:, p, :, 1:2], EPS, None, ALU.add).then_inc(s_var[p], 1)

                def normed(p):
                    dve.wait_ge(s_rs[p], j + 1)
                    for t in range(TT):
                        last = nc.vector.tensor_scalar(X[:, bass.ds(2 * (turns * p + j) + t, 1), :].rearrange("p a d -> p (a d)"),
                                                       WX[:, p, t], MV[:, p, t, 0:1], MV[:, p, t, 1:2],
                                                       ALU.subtract, ALU.mult)
                    last.then_inc(s_x[p], 1)

                for step in (maxima, kept, heads, sums, normed):
                    for p in slots:
                        step(p)
                link.close()

        @block.scalar
        def _(act):
            with act.Fori(0, turns) as j:
                def kept(p):
                    act.wait_ge(s_mt[p], j + 1)
                    act.wait_ge(s_m[p], 16 * j)
                    nc.scalar.activation(MT[:, p], psb[0:3 * AH, 2 * (2048 + 1024 * p):2 * (2048 + 1024 * p) + T],
                                         ACT.Copy).then_inc(s_mc[p], 1)

                def exps(p):
                    for g in range(GROUPS):
                        i = GROUPS * p + g
                        act.wait_ge(s_s2, 2 * GROUPS * j + i + 1)
                        if g >= 4:
                            act.wait_ge(s_pv[p], 4 * j + g // 2 - 1)
                        elif p:
                            act.wait_ge(s_pv[0], 4 * j + 3 + g // 2)
                        else:
                            act.wait_ge(s_pv[1], 4 * j)
                        nc.scalar.activation(PR[:, g // 2 % 2, g % 2 * 2:g % 2 * 2 + 2],
                                             ps[:, pair(g):pair(g) + 1024].rearrange("p (h c) -> p h c", h=2),
                                             ACT.Exp).then_inc(s_ex, 1)

                def y_kept(p):
                    act.wait_ge(s_yt[p], j + 1)
                    nc.scalar.activation(YAT[:, p], obank(p, 0, T), ACT.Copy).then_inc(s_yc[p], 1)

                kept(0)
                kept(1)
                exps(0)
                exps(1)
                y_kept(0)
                y_kept(1)

        @block.tensor
        def _(pe):
            with pe.Fori(0, turns) as j:
                def pass1(p):
                    pe.wait_ge(s_q[p], 16 * 4 * len(PAIRS) * (j + 1))
                    for g in range(GROUPS):
                        i = GROUPS * p + g
                        if i >= 2:
                            pe.wait_ge(s_mx, 2 * GROUPS * j + i - 1)
                        else:
                            pe.wait_ge(s_ex, 2 * GROUPS * j)
                        for h in (2 * g, 2 * g + 1):
                            for t in range(TT):
                                o = ps[:, pair(g) + 512 * (h % 2) + T * t:pair(g) + 512 * (h % 2) + T * t + T]
                                nc.tensor.matmul(o, k.QA[0:MROW, p, h // 2, h % 2, t * P:t * P + P], k.KA[0:MROW, p, h // 2],
                                                 start=True, stop=False)
                                n = alibi_parts(h)
                                for a in range(n):
                                    last = nc.tensor.matmul(o[:, t * P:t * P + P], k.DL[:, 0], k.SI[:, alibi_at(h) + a],
                                                            start=False, stop=(a == n - 1))
                        last.then_inc(s_s1, 1)

                def turn_max(p):
                    pe.wait_ge(s_mp[p], j + 1)
                    pe.wait_ge(s_x[p], j)
                    alone(pe)
                    for t in range(TT):
                        at = 2 * (2048 + 1024 * p) + t * P
                        last = nc.tensor.transpose(psb[0:3 * AH, at:at + P], MP[:, p, t].rearrange("p a h -> p (a h)"), k.IDB[:])
                    last.then_inc(s_mt[p], 1)

                def mix(p, quad):
                    pe.wait_ge(s_ex, 2 * GROUPS * j + GROUPS * p + 2 * quad + 2)
                    if quad == 0:
                        pe.wait_ge(s_vs[p], j + 1)
                    for s in range(TT):
                        for h in range(4):
                            last = nc.tensor.matmul(obank(p, quad * T, quad * T + T)[32 * h:32 * h + AD + 1],
                                                    VS[:, p, s, 4 * quad + h], PR[:, quad % 2, h, s * T:s * T + T],
                                                    start=(s == 0), stop=(s == TT - 1), tile_position=(0, 32 * h))
                    last.then_inc(s_pv[p], 1)

                def pass2(p):
                    pe.wait_ge(s_m[p], 16 * (j + 1))
                    for g in range(GROUPS):
                        i = GROUPS * p + g
                        if i >= 2:
                            pe.wait_ge(s_ex, 2 * GROUPS * j + i - 1)
                        else:
                            pe.wait_ge(s_mx, 2 * GROUPS * (j + 1))
                        for h in (2 * g, 2 * g + 1):
                            for s in range(TT):
                                o = ps[:, pair(g) + 512 * (h % 2) + T * s:pair(g) + 512 * (h % 2) + T * s + T]
                                nc.tensor.matmul(o, k.KA[0:MROW + 3, p, h // 2, s * P:s * P + P],
                                                 k.QA[0:MROW + 3, p, h // 2, h % 2], start=True, stop=False)
                                n = alibi_parts(h)
                                for a in range(n):
                                    last = nc.tensor.matmul(o[:, s * P:s * P + P], k.DL[:, 1], k.SI[:, alibi_at(h) + a],
                                                            start=False, stop=(a == n - 1))
                        last.then_inc(s_s2, 1)
                        if g % 2 and g > 1:
                            mix(p, g // 2 - 1)
                    mix(p, GROUPS // 2 - 1)

                def turned(p):
                    pe.wait_ge(s_os[p], j + 1)
                    for t in range(TT):
                        for quad in range(4):
                            last = nc.tensor.transpose(obank(p, t * 512 + quad * P, t * 512 + quad * P + P),
                                                       OS[:, p, quad * T + t * P:quad * T + t * P + P], k.c("ident"))
                    last.then_inc(s_ot[p], 1)

                def y_turned(p):
                    pe.wait_ge(s_ya[p], j + 1)
                    for t in range(TT):
                        last = nc.tensor.transpose(obank(p, t * P, t * P + P), YA[:, p, t], k.c("ident"))
                    last.then_inc(s_yt[p], 1)

                def project(p):
                    pe.wait_ge(s_yc[p], j + 1)
                    for t in range(TT):
                        o = obank(p, 512 + t * P, 512 + t * P + P)
                        nc.tensor.matmul(o, YAT[:, p, t * P:t * P + P], k.WP[:, 0:D], start=True, stop=False)
                        last = nc.tensor.matmul(o, k.c("ones")[0:1], k.WP[0:1, D:2 * D], start=False, stop=True)
                    last.then_inc(s_pj[p], 1)

                pass1(0)
                pass1(1)
                turn_max(0)
                turn_max(1)
                pass2(0)
                pass2(1)
                for step in (turned, y_turned, project):
                    for p in slots:
                        step(p)


def staged(nc, tag, stage):
    with ExitStack() as ctx:
        sems = []

        def sem(name):
            sems.append(nc.alloc_semaphore(f"{tag}_{name}"))
            return sems[-1]

        stage(lambda name, shape, dtype=F32: ctx.enter_context(nc.sbuf_tensor(f"{tag}_{name}", shape, dtype)), sem)
        nc.all_engine_barrier()
        nc.clear_and_free_semaphores(sems)
        nc.all_engine_barrier()


def load_experts(nc, sem, dram, k, layer, sb):
    s_w, s_z, s_f = sem("experts_loaded"), sem("zero_tile"), sem("zeros_stored")
    Z = sb("Z", [P, TILES * D // 4])
    with nc.Block() as block:
        @block.sync
        def _(sp):
            sp.dma_start(k.W1[:], dram["w1"][layer]).then_inc(s_w, 16)
            sp.dma_start(k.WD[:].rearrange("p e f d -> p (e f d)"), dram["wd"][layer]).then_inc(s_w, 16)
            sp.dma_start(k.F[:], dram["wf"]).then_inc(s_w, 16)
            sp.wait_ge(s_w, 48)

        @block.gpsimd
        def _(pool):
            nc.gpsimd.memset(Z[:], 0.0).then_inc(s_z, 1)
            pool.wait_ge(s_z, 1)
            for c in range(2):
                for q in range(4):
                    rows = TILES * P // 4
                    pool.dma_start(dram["sorted"][c][rows * q:rows * q + rows, :].rearrange("(p a) d -> p (a d)", p=P),
                                   Z[:]).then_inc(s_f, 16)
            pool.wait_ge(s_f, 128)


def attention_stage(nc, ps, dram, k):
    with ExitStack() as ctx:
        def sb(name, shape, dtype=F32):
            return ctx.enter_context(nc.sbuf_tensor(name, shape, dtype))

        k.QP, k.KP = sb("QP", [P, 3, NT * P], BF16), sb("KP", [P, 3, NT * P], BF16)
        k.VX = sb("VX", [P, NT, AH, AD + 1])
        k.QA = sb("QA", [P, SLOTS, AH // 2, 2, T], BF16)
        k.KA = sb("KA_rows", [P, SLOTS, AH // 2, T], BF16)
        k.SI = sb("SI", [P, AH // 2 * 4, P], BF16)
        k.DL = sb("DL", [P, 2, P], BF16)
        k.WP = sb("WP", [P, 2 * D])
        staged(nc, "qkv", lambda sb, sem: qkv(nc, sb, ps, sem, dram, k))
        staged(nc, "attention", lambda sb, sem: attention(nc, sb, ps, sem, k))


def build(nc, dram, stages=4):
    with ExitStack() as ctx:
        def sb(name, shape, dtype=F32):
            return ctx.enter_context(nc.sbuf_tensor(name, shape, dtype))

        def sem(name):
            return ctx.enter_context(nc.semaphore(name))

        k = Kept()
        ps = ctx.enter_context(nc.psum_tensor("ps", [P, 8 * 512], F32))
        k.X = sb("X", [P, NT, D])
        k.C = sb("C", [P, CONST_W])
        k.XNT = sb("XNT", [P, NT * P])
        k.POWER = sb("POWER", [P, 16])
        k.IDB = sb("IDB", [P, P], BF16)
        k.F = sb("F", [P, WF_W])
        k.W1 = sb("W1", [P, NE + 1, 2 * FF])
        k.WD = sb("WD", [P, NE + 1, 2, D])
        with ExitStack() as inner:
            def own(name, shape, dtype=F32):
                return inner.enter_context(nc.sbuf_tensor(name, shape, dtype))

            k.W = own("W", [P, WA_W])
            k.LATER = own("LATER", [P, P], BF16)
            k.SEL = own("SEL", [96, TURNS * MH, T], BF16)
            k.CUMT = own("CUMT", [96, SLOTS, TT, P], BF16)
            k.NCUMT = own("NCUMT", [96, SLOTS, TT, P], BF16)
            k.DT = own("DT", [P, NT, MH])
            k.AT = own("AT", [P, P])
            k.VV = own("VV", [P, 2 * D])
            staged(nc, "prepare", lambda sb, sem: prepare(nc, sb, ps, sem, dram, k))
            staged(nc, "mamba", lambda sb, sem: mamba(nc, sb, ps, sem, k))
        k.LOG = sb("LOG", [P, NE, NT])
        k.GATE = sb("GATE", [P, 2, NT])
        k.POS = sb("POS", [P, 2, NT], U32)
        k.TEX = sb("TEX", [1, 2, TILES], mybir.dt.int32)
        for layer in range(2):
            if stages < (2, 3)[layer]:
                break
            choices = layer + 1
            if layer == 1:
                attention_stage(nc, ps, dram, k)
                if stages == 3:
                    break
            with ExitStack() as inner:
                k.XF = inner.enter_context(nc.sbuf_tensor(f"XF{layer}", [P, NT, D], F32))
                k.ACC = inner.enter_context(nc.sbuf_tensor(f"ACC{layer}", [P, NT, D], F32))
                staged(nc, f"load_experts{layer}", lambda sb, sem: load_experts(nc, sem, dram, k, layer, sb))
                staged(nc, f"ffn_tokens{layer}", lambda sb, sem: ffn_tokens(nc, sb, ps, sem, k, layer))
                staged(nc, f"route{layer}", lambda sb, sem: route(nc, sb, ps, sem, k, layer, choices))
                staged(nc, f"experts{layer}", lambda sb, sem: experts(nc, sb, ps, sem, dram, k, layer, choices))
        s_out = sem("stored")
        with nc.Block() as block:
            @block.sync
            def _(sp):
                sp.dma_start(dram["out"].rearrange("b (t p) d -> p (b t) d", p=P), k.X[:]).then_inc(s_out, 16)
                sp.wait_ge(s_out, 16)


def constants(np):
    i, j = np.arange(P)[:, None], np.arange(P)[None]
    c = np.zeros((P, CONST_W), np.float32)

    def put(name, value):
        a, z = CONST[name]
        c[:value.shape[0], a:z] = value

    put("ident", np.eye(P))
    put("tri", (i <= j) * 1.0)
    put("ones", np.ones((P, P)))
    put("ones2", np.ones((P, NE * NT)))
    put("ahead", (i < j) * 1.0)
    put("eight", np.tile(NE - np.arange(NE), (P, 1)))
    put("m128", np.tile(P * np.arange(NT), (P, 1)))
    put("tile", np.tile(np.arange(TILES), (P, 1)))
    put("later", (j < i) * -BIG)
    put("earlier", np.concatenate([(np.arange(T)[None] < i + P * t) * 1.0 for t in range(TT)], 1))
    put("slot", np.tile(np.arange(POOL), (P, 1)))
    r = np.arange(TURNS * 12)[:, None]
    put("sel", ((r // 12 == np.arange(TURNS * MH)[None] // MH) & (r % MH == np.arange(TURNS * MH)[None] % MH)) * 1.0)
    return c


def mamba_weights(np, g):
    def pad(a):
        return np.concatenate([a, np.zeros((P - a.shape[0], a.shape[1]), np.float32)]) if a.shape[0] < P else a

    w, f = {}, lambda n: np.asarray(g["L0_attn_" + n])
    w["inw"], w["dtw"] = f("in_w")[:768].T, f("in_w")[768:].T
    w["normw"] = f("norm_w")[:, None]
    w["convw"] = f("conv_w").reshape(4, P, TAPS).transpose(1, 0, 2).reshape(P, 16)
    w["convb"] = f("conv_b").reshape(4, P).T
    w["dtb"], w["alog"] = np.tile(f("dt_bias"), (P, 1)), np.tile(f("A_log"), (P, 1))
    w["dpar"] = np.repeat(f("D_param"), MP).reshape(2, P).T
    w["gnorm"] = f("gnorm_w").reshape(2, P).T
    w["outw"] = f("out_w").T.reshape(2, P, D).transpose(1, 0, 2).reshape(P, 2 * D)
    w["tapbc"] = np.broadcast_to(f("conv_w").reshape(4 * P, TAPS)[2 * P:].T.reshape(1, -1), (P, TAPS * 2 * P))
    w["w1"], w["w2"] = f("scorer_w1").T, f("scorer_w2").T
    w["summ"], w["qw"], w["kwt"], w["vwt"] = f("summ_w"), f("q_w"), f("k_w").T, f("v_w").T
    w["g1"], w["g2"] = f("gate_w")[:, :D].T, f("gate_w")[:, D:].T
    return np.ascontiguousarray(np.concatenate([pad(w[n]) for n in WA], 1))


def expert_weights(np, g):
    f = lambda n: np.asarray(g[n])
    g0 = np.concatenate([f("L0_ffn_gate_w"), f("L0_ffn_sh_gate")[None]])
    u0 = np.concatenate([f("L0_ffn_up_w"), f("L0_ffn_sh_up")[None]])
    d0 = np.concatenate([f("L0_ffn_down_w"), f("L0_ffn_sh_down")[None]])
    g1 = np.concatenate([f("L1_ffn_w_in_eDF"), f("L1_ffn_w_in_shared_FD").T[None]])
    u1 = np.concatenate([f("L1_ffn_w_swiglu_eDF"), f("L1_ffn_w_swiglu_FD").T[None]])
    d1 = np.concatenate([f("L1_ffn_w_out_eFD"), f("L1_ffn_w_out_shared_DF").T[None]])
    w1 = [np.concatenate([a, b], 2).transpose(1, 0, 2) for a, b in ((g0, u0), (g1, u1))]
    wd = [d.reshape(NE + 1, 2, P, D).transpose(2, 0, 1, 3).reshape(P, -1) for d in (d0, d1)]
    wf = np.concatenate([f("L0_ffn_router_w"), f("L1_ffn_router_DE"), np.tile(f("L0_ffn_ln_w"), (P, 1)),
                         np.tile(f("L0_ffn_ln_b"), (P, 1))], 1)
    return tuple(np.ascontiguousarray(a) for a in (np.stack(w1), np.stack(wd), wf))


def attention_constants(np, bf16):
    f32 = np.float32
    slope = np.array([2.0 ** (-0.5 * (h + 1)) for h in range(AH)]).astype(f32)
    s1 = slope.astype(bf16).astype(f32)
    s2 = (slope - s1).astype(bf16).astype(f32)
    s3 = slope - s1 - s2
    parts = np.stack([s1, s2, s3])
    at = np.arange(T, dtype=f32)
    last, first = (at >= P).astype(f32), (at < P).astype(f32)
    q = np.zeros((P, AH // 2, 2, T), f32)
    kk = np.zeros((P, AH // 2, T), f32)
    for h in range(AH):
        r = HROWS * (h % 2) + AD * len(PAIRS)
        for a in range(3):
            q[r + a, h // 2, h % 2], kk[r + a, h // 2] = -at * last, parts[a, h] * first
            q[r + 3 + a, h // 2, h % 2], kk[r + 3 + a, h // 2] = parts[a, h] * last, at * first
    kk[MROW:MROW + 3] = 1.0
    si = np.zeros((P, AH // 2 * 4, P), f32)
    for h in range(AH):
        for a in range(alibi_parts(h)):
            si[:, alibi_at(h) + a] = np.eye(P) * parts[a, h]
    i, j = np.arange(P)[:, None], np.arange(P)[None]
    ramps = np.stack([np.minimum(i - j, 0), np.minimum(j - i, 0)], 1)
    return {"qrows": q.astype(bf16), "krows": kk.astype(bf16), "slopes": si.astype(bf16), "ramps": ramps.astype(bf16)}


def attention_weights(np, g):
    f = lambda n: np.asarray(g["L1_attn_" + n])
    order = np.arange(D).reshape(AH // 2, 2, AD).transpose(1, 2, 0).reshape(-1)
    w, b = f("W_qkv"), f("b_qkv")
    out = {"wqkv": np.concatenate([w[:, order], w[:, D + order], w[:, 2 * D:]], 1),
           "bqk": np.stack([b[order], b[D + order]], 1), "bv": np.tile(b[2 * D:], (P, 1)),
           "wproj": np.concatenate([f("W_proj"), np.tile(f("b_proj"), (P, 1))], 1)}
    return {n: np.ascontiguousarray(a) for n, a in out.items()}


def kernel(**inputs):
    import numpy as _np
    import concourse.bacc as _bacc
    from concourse import mybir as _mybir
    from concourse.bass_utils import run_bass_kernel_spmd as _run

    w1, wd, wf = expert_weights(_np, inputs)
    import ml_dtypes
    bf16 = ml_dtypes.bfloat16
    arrays = {"w1": w1, "wd": wd, "wf": wf, "x": _np.ascontiguousarray(inputs["L0_attn_x"]), "const": constants(_np), "wa": mamba_weights(_np, inputs)}
    arrays.update(attention_constants(_np, bf16))
    arrays.update(attention_weights(_np, inputs))
    nc = _bacc.Bacc("TRN2", target_bir_lowering=False, num_devices=1)
    dram = {n: nc.dram_tensor(n, a.shape, _mybir.dt.from_np(a.dtype), kind="ExternalInput").ap() for n, a in arrays.items()}
    for n in ("sorted", "expert_out"):
        dram[n] = [nc.dram_tensor(f"{n}{c}", (TILES * P, D), _mybir.dt.float32).ap() for c in range(2)]
    dram["out"] = nc.dram_tensor("out", (B, T, D), _mybir.dt.float32, kind="ExternalOutput").ap()
    build(nc, dram)
    r = _run(nc, [arrays], core_ids=[0])
    return r.results[0]["out"]
```

```python
import numpy as np
import concourse.bass as bass
from concourse import mybir
from contextlib import ExitStack

F32 = mybir.dt.float32
BF16 = mybir.dt.bfloat16
ALU = mybir.AluOpType
ACT = mybir.ActivationFunctionType
AX_X = mybir.AxisListType.X

P = 128
B, T, D = 16, 256, 128
NT = B * T // P
TT = T // P
EPS = 1e-5
MH, MP = 4, 64
DI = MH * MP
TAPS = 4
POOL = 50
SLOTS = 2
TURNS = B // SLOTS
UNITS = B * T // 512
NE = 8
FF = 256
TILES = 40
BIG = 1.0e30
U32 = mybir.dt.uint32


def columns(table):
    at, out = 0, {}
    for name, width in table:
        out[name] = (at, at + width)
        at += width
    return out, at


CONST, CONST_W = columns([("ident", P), ("tri", P), ("ones", P), ("later", P), ("earlier", TT * T),
                          ("ones2", NE * NT), ("ahead", P), ("eight", NE), ("m128", NT), ("tile", TILES), ("slot", POOL), ("sel", TURNS * MH)])
WA, WA_W = columns([("inw", 768), ("dtw", MH), ("normw", 1), ("convw", 16), ("convb", 4), ("dtb", MH),
                    ("alog", MH), ("dpar", 2), ("gnorm", 2), ("outw", 2 * D), ("w1", 32), ("w2", 1), ("tapbc", 4 * 2 * P), ("summ", D),
                    ("qw", D), ("kwt", 64), ("vwt", D), ("g1", D), ("g2", D)])
WF, WF_W = columns([("router0", NE), ("router1", NE), ("lnw", D), ("lnb", D)])


class Links:

    def __init__(self, engine, sem, total=0, turn=0):
        self.engine, self.sem, self.base, self.total, self.n = engine, sem, turn * total, total, 0

    def __call__(self, ins):
        self.n += 1
        ins.then_inc(self.sem, 1)
        self.engine.wait_ge(self.sem, self.base + self.n)

    def close(self):
        assert self.n == self.total, f"links in the body: {self.n}, not {self.total}"


class Kept:

    def c(self, name):
        a, z = CONST[name]
        return self.C[:, a:z]

    def w(self, name):
        a, z = WA[name]
        return self.W[:, a:z]

    def cf(self, name):
        a, z = WF[name]
        return self.F[:, a:z]


def alone(engine):
    engine.nop(nofuse=True)


def spread(ap, n):
    return ap.unsqueeze(2).broadcast_to((ap.shape[0], ap.shape[1], n))


def prepare(nc, sb, ps, sem, dram, k):
    XN4 = sb("XN4", [P, SLOTS, 4, D])
    XNS = sb("XNS", [P, SLOTS, 4 * P])
    SQ = sb("SQ", [P, SLOTS, 4, D])
    MS = sb("MS", [P, SLOTS, 4])
    RS = sb("RS", [P, SLOTS, 4])
    MK = sb("MK", [64, D])
    VWT = sb("VWT", [P, D])
    DTR, RAW, E, U, DLT, LNU, LA = (sb(n, [P, NT, MH]) for n in ("DTR", "RAW", "E", "U", "DLT", "LNU", "LA"))
    LA2 = sb("LA2", [P, TT, B, MH])
    CUM = sb("CUM", [P, TT, B * MH])
    PARTS = sb("PARTS", [P, SLOTS, TT, 96], BF16)
    IDB = k.IDB
    psb = ps[:].bitcast(BF16)

    s_x, s_c, s_wa = sem("x_loaded"), sem("const_loaded"), sem("wa_loaded")
    s_pow, s_zt, s_f = sem("power_set"), sem("zero_tile"), sem("zeros_stored")
    Z = sb("Z", [P, TILES * D // 4])
    s_idb = sem("bf16_consts")
    s_mk, s_mkc = sem("mk"), sem("mk_copied")
    s_prod, s_prodc = sem("products"), sem("products_copied")
    s_link = sem("dve_links")
    s_ms = [sem(f"mean_square{p}") for p in range(SLOTS)]
    s_rs = [sem(f"rstd{p}") for p in range(SLOTS)]
    s_xn = [sem(f"xn{p}") for p in range(SLOTS)]
    s_tr = [sem(f"xn_transposed{p}") for p in range(SLOTS)]
    s_ev = [sem(f"xn_evacuated{p}") for p in range(SLOTS)]
    s_cp = [sem(f"xn_kept{p}") for p in range(SLOTS)]
    s_dt = [sem(f"dt_raw{p}") for p in range(SLOTS)]
    s_dtc = [sem(f"dt_copied{p}") for p in range(SLOTS)]
    s_sp = sem("softplus_act")
    s_abs = sem("abs_done")
    s_spd = sem("softplus_dve")
    s_cum = sem("cumulated")
    s_parts = sem("parts_split")
    s_cumt = sem("parts_transposed")
    s_done = sem("parts_kept")

    X, C, W = k.X, k.C, k.W
    with nc.Block() as block:
        @block.sync
        def _(sp):
            sp.dma_start(C[:], dram["const"]).then_inc(s_c, 16)
            sp.dma_start(X[:, 0:16], dram["x"][0:8].rearrange("b (t p) d -> p (b t) d", p=P)).then_inc(s_x, 16)
            sp.dma_start(W[:], dram["wa"]).then_inc(s_wa, 16)
            sp.dma_start(X[:, 16:32], dram["x"][8:16].rearrange("b (t p) d -> p (b t) d", p=P)).then_inc(s_x, 16)
            sp.dma_start(k.F[:], dram["wf"]).then_inc(s_f, 16)
            load_experts(sp, dram, k, 0)
            sp.wait_ge(s_zt, 1)
            for c in range(2):
                for q in range(4):
                    rows = TILES * P // 4
                    sp.dma_start(dram["sorted"][c][rows * q:rows * q + rows, :].rearrange("(p a) d -> p (a d)", p=P),
                                 Z[:]).then_inc(s_f, 16)
            sp.wait_ge(s_f, 16 * 9)

        @block.gpsimd
        def _(pool):
            nc.gpsimd.memset(Z[:], 0.0).then_inc(s_zt, 1)
            nc.gpsimd.memset(k.POWER[:], -0.5).then_inc(s_pow, 1)
            pool.wait_ge(s_pow, 1)
            with pool.Fori(0, UNITS // SLOTS) as j:
                for p in range(SLOTS):
                    pool.wait_ge(s_ms[p], j + 1)
                    pool.wait_ge(s_xn[p], j)
                    nc.gpsimd.tensor_tensor(RS[:, p], MS[:, p], k.POWER[:, 0:4], ALU.pow).then_inc(s_rs[p], 1)
                for p in range(SLOTS):
                    pool.wait_ge(s_ev[p], j + 1)
                    nc.gpsimd.tensor_copy(k.XNT[:, bass.ds((UNITS // 2 * p + j) * 512, 512)], XNS[:, p]).then_inc(s_cp[p], 1)

        @block.vector
        def _(dve):
            link = Links(dve, s_link)
            dve.wait_ge(s_c, 16)
            nc.vector.tensor_copy(IDB[:], k.c("ident"))
            nc.vector.tensor_copy(k.LATER[:], k.c("later"))
            link(nc.vector.tensor_copy(k.SEL[:], k.c("sel")[0:96].unsqueeze(2).broadcast_to((96, TURNS * MH, T))))
            dve.wait_ge(s_wa, 16)
            nc.vector.tensor_scalar(k.w("inw")[:, 0:DI], k.w("inw")[:, 0:DI], 0.5, None, ALU.mult)
            nc.vector.tensor_scalar(k.w("convw"), k.w("convw"), 0.5, None, ALU.mult)
            nc.vector.tensor_scalar(k.w("convb"), k.w("convb"), 0.5, None, ALU.mult)
            for tap in range(TAPS):
                w = k.w("tapbc")[:, 2 * P * tap:2 * P * tap + 2 * P]
                nc.vector.scalar_tensor_tensor(w, w, 0.5, k.w("inw")[:, 4 * P:6 * P], ALU.mult, ALU.mult)
            for ct in range(2):
                o = k.w("outw")[:, ct * D:(ct + 1) * D]
                last = nc.vector.tensor_scalar(o, o, k.w("gnorm")[:, ct:ct + 1], None, ALU.mult)
            link(last)
            dve.wait_ge(s_mk, 1)
            nc.vector.tensor_copy(MK[:], ps[0:64, 1024:1152]).then_inc(s_mkc, 1)
            nc.vector.tensor_copy(VWT[:], ps[:, 1536:1664]).then_inc(s_mkc, 1)
            dve.wait_ge(s_prod, 1)
            nc.vector.tensor_copy(k.AT[:], ps[:, 2048:2176])
            link(nc.vector.tensor_copy(k.VV[:], ps[:, 2560:2816]))
            dve.wait_ge(s_x, 32)
            with dve.Fori(0, UNITS // SLOTS) as j:
                ln = Links(dve, s_link, 2 * SLOTS, j)
                ln.base = ln.base + link.n
                for p in range(SLOTS):
                    xu = X[:, bass.ds((UNITS // 2 * p + j) * 4, 4), :]
                    dve.wait_ge(s_xn[p], j)
                    ln(nc.vector.tensor_tensor(SQ[:, p], xu, xu, ALU.mult))
                    ln(nc.vector.tensor_reduce(MS[:, p], SQ[:, p], AX_X, ALU.add))
                    nc.vector.tensor_scalar(MS[:, p], MS[:, p], 1.0 / D, EPS, ALU.mult, ALU.add).then_inc(s_ms[p], 1)
                for p in range(SLOTS):
                    xu = X[:, bass.ds((UNITS // 2 * p + j) * 4, 4), :]
                    dve.wait_ge(s_rs[p], j + 1)
                    dve.wait_ge(s_tr[p], j)
                    nc.vector.tensor_tensor(XN4[:, p], xu, spread(RS[:, p], D), ALU.mult).then_inc(s_xn[p], 1)
                for p in range(SLOTS):
                    dve.wait_ge(s_dt[p], j + 1)
                    nc.vector.tensor_copy(DTR[:, bass.ds((UNITS // 2 * p + j) * 4, 4), :],
                                          ps[:, 1024 + 512 * p:1040 + 512 * p].rearrange("p (t h) -> p t h", h=MH)
                                          ).then_inc(s_dtc[p], 1)
                ln.close()
            link.n += (UNITS // SLOTS) * 2 * SLOTS
            for p in range(SLOTS):
                dve.wait_ge(s_dtc[p], UNITS // SLOTS)
            nc.vector.tensor_tensor(RAW[:], DTR[:], k.w("dtb").unsqueeze(1).broadcast_to((P, NT, MH)),
                                    ALU.add).then_inc(s_spd, 1)
            dve.wait_ge(s_sp, 2)
            nc.vector.tensor_scalar(U[:], E[:], 1.0, None, ALU.add).then_inc(s_spd, 1)
            dve.wait_ge(s_spd, 2)
            link(nc.vector.tensor_scalar(DLT[:], U[:], 1.0, None, ALU.subtract))
            link(nc.vector.tensor_tensor(DLT[:], E[:], DLT[:], ALU.subtract))
            link(nc.vector.reciprocal(E[:], U[:]))
            link(nc.vector.tensor_tensor(DLT[:], DLT[:], E[:], ALU.mult))
            link(nc.vector.scalar_tensor_tensor(DLT[:], RAW[:], 0.0, DLT[:], ALU.max, ALU.add))
            dve.wait_ge(s_sp, 3)
            link(nc.vector.tensor_tensor(k.DT[:], DLT[:], LNU[:], ALU.add))
            link(nc.vector.scalar_tensor_tensor(LA[:], k.DT[:], -1.0,
                                                k.w("alog").unsqueeze(1).broadcast_to((P, NT, MH)),
                                                ALU.mult, ALU.mult))
            nc.vector.tensor_copy(LA2[:], LA[:].rearrange("p (b t) h -> p t b h", t=TT)).then_inc(s_spd, 1)
            dve.wait_ge(s_cum, 1)
            link(nc.vector.tensor_copy(CUM[:], ps[:, 0:TT * B * MH].rearrange("p (t c) -> p t c", t=TT)))
            for part in range(3):
                for t in range(TT):
                    for h2 in range(SLOTS):
                        last = nc.vector.tensor_copy(
                            PARTS[:, h2, t].rearrange("p (b c h) -> p b c h", c=3, h=MH)[:, :, part, :],
                            CUM[:, t, h2 * 32:h2 * 32 + 32].rearrange("p (b h) -> p b h", h=MH))
                if part < 2:
                    link(last)
                    for t in range(TT):
                        for h2 in range(SLOTS):
                            c = CUM[:, t, h2 * 32:h2 * 32 + 32].rearrange("p (b h) -> p b h", h=MH)
                            last = nc.vector.tensor_tensor(
                                c, c, PARTS[:, h2, t].rearrange("p (b c h) -> p b c h", c=3, h=MH)[:, :, part, :],
                                ALU.subtract)
                    link(last)
                else:
                    last.then_inc(s_parts, 1)
            dve.wait_ge(s_cumt, 1)
            for h2 in range(SLOTS):
                o = psb[0:96, h2 * 1024:h2 * 1024 + TT * P].rearrange("p (t c) -> p t c", t=TT)
                nc.vector.tensor_copy(k.CUMT[:, h2], o)
                last = nc.vector.tensor_scalar(k.NCUMT[:, h2], o, -1.0, None, ALU.mult)
            last.then_inc(s_done, 1)
            dve.wait_ge(s_done, 1)

        @block.scalar
        def _(act):
            with act.Fori(0, UNITS // SLOTS) as j:
                for p in range(SLOTS):
                    act.wait_ge(s_tr[p], j + 1)
                    act.wait_ge(s_cp[p], j)
                    act.wait_ge(s_dt[p], j)
                    nc.scalar.activation(XNS[:, p], ps[:, 512 * p:512 * p + 512], ACT.Copy,
                                         scale=k.w("normw")).then_inc(s_ev[p], 1)
            act.wait_ge(s_wa, 16)
            act.wait_ge(s_spd, 1)
            nc.scalar.activation(k.w("alog"), k.w("alog"), ACT.Exp).then_inc(s_sp, 1)
            nc.scalar.activation(E[:], RAW[:], ACT.Abs).then_inc(s_abs, 1)
            act.wait_ge(s_abs, 1)
            nc.scalar.activation(E[:], E[:], ACT.Exp, scale=-1.0).then_inc(s_sp, 1)
            act.wait_ge(s_spd, 2)
            nc.scalar.activation(LNU[:], U[:], ACT.Ln).then_inc(s_sp, 1)

        @block.tensor
        def _(pe):
            pe.wait_ge(s_c, 16)
            pe.wait_ge(s_wa, 16)
            pe.wait_ge(s_link, 2)
            nc.tensor.matmul(ps[0:64, 1024:1152], k.w("kwt")[0:64], k.w("summ")[0:64], start=True, stop=True)
            nc.tensor.matmul(ps[:, 1536:1664], k.w("vwt")[0:64], k.w("summ")[0:64], start=True,
                             stop=True).then_inc(s_mk, 1)
            pe.wait_ge(s_mkc, 2)
            nc.tensor.matmul(ps[:, 2048:2176], MK[:], k.w("qw")[0:64], start=True, stop=True)
            nc.tensor.matmul(ps[:, 2560:2688], k.w("summ")[0:64], k.w("vwt")[0:64], start=True, stop=True)
            nc.tensor.matmul(ps[:, 2688:2816], VWT[:], k.w("g2"), start=True, stop=True).then_inc(s_prod, 1)
            with pe.Fori(0, UNITS // SLOTS) as j:
                for p in range(SLOTS):
                    pe.wait_ge(s_xn[p], j + 1)
                    pe.wait_ge(s_ev[p], j)
                    for t in range(4):
                        last = nc.tensor.transpose(ps[:, 512 * p + 128 * t:512 * p + 128 * t + 128], XN4[:, p, t, :],
                                                   k.c("ident"))
                    last.then_inc(s_tr[p], 1)
                for p in range(SLOTS):
                    pe.wait_ge(s_ev[p], j + 1)
                    pe.wait_ge(s_dtc[p], j)
                    for t in range(4):
                        last = nc.tensor.matmul(ps[:, 1024 + 512 * p + 4 * t:1028 + 512 * p + 4 * t],
                                                XNS[:, p, P * t:P * t + P], k.w("dtw"), start=True, stop=True)
                    last.then_inc(s_dt[p], 1)
            pe.wait_ge(s_spd, 3)
            nc.tensor.matmul(ps[:, 0:64], k.c("tri"), LA2[:, 0], start=True, stop=True)
            nc.tensor.matmul(ps[:, 64:128], k.c("tri"), LA2[:, 1], start=True, stop=False)
            nc.tensor.matmul(ps[:, 64:128], k.c("ones"), LA2[:, 0], start=False, stop=True).then_inc(s_cum, 1)
            pe.wait_ge(s_parts, 1)
            for h2 in range(SLOTS):
                for t in range(TT):
                    last = nc.tensor.transpose(psb[0:96, h2 * 1024 + t * P:h2 * 1024 + t * P + P], PARTS[:, h2, t],
                                               IDB[:])
            last.then_inc(s_cumt, 1)


def mamba(nc, sb, ps, sem, k):
    PAD = TAPS - 1
    CB = sb("CB", [P, SLOTS, 2, PAD + T])
    TH = sb("TH", [P, SLOTS, 4 * T])
    ZZ = sb("ZZ", [P, SLOTS, 2 * T])
    CV = sb("CV", [P, SLOTS, 4, T])
    XS = sb("XS", [P, SLOTS, 4, T])
    EX = sb("EX", [P, SLOTS, MH, T + P])
    DTX = sb("DTX", [P, SLOTS, TT * MH, MP])
    YG = sb("YG", [P, SLOTS, 2, T])
    YSQ = sb("YSQ", [P, SLOTS, 2, T])
    MS = sb("MSY", [P, SLOTS, TT])
    RS = sb("RSY", [P, SLOTS, TT])
    YO = sb("YO", [P, SLOTS, TT, D])
    YT = sb("YT", [P, SLOTS, T])
    HT = sb("HT", [32, SLOTS, T])
    W2 = sb("W2", [32, P])
    SC = sb("SC", [P, SLOTS, T])
    SCC = sb("SCC", [P, SLOTS, TT])
    MEAN = sb("MEAN", [P, SLOTS])
    JUNK = sb("JUNK", [P, SLOTS, TT, T])
    JUNK2 = sb("JUNK2", [P, SLOTS, TT, T])
    RANK = sb("RANK", [P, SLOTS, 2 * TT])
    HIGH = sb("HIGH", [P, SLOTS, TT])
    PICK = sb("PICK", [P, SLOTS, TT, POOL])
    YSEL = sb("YSEL", [P, SLOTS, POOL])
    EMPTY = sb("EMPTY", [1, SLOTS, POOL])
    KA = sb("KA", [P, SLOTS, POOL])
    VSEL = sb("VSEL", [P, SLOTS, 2 * D])
    LG = sb("LG", [P, SLOTS, TT, POOL])
    MX = sb("MX", [P, SLOTS, TT])
    SM = sb("SM", [P, SLOTS, TT])
    PRT = sb("PRT", [P, SLOTS, T])
    TG = sb("TG", [P, SLOTS, TT, D])
    GR = sb("GR", [P, SLOTS, TT, D])
    WX = sb("WX", [P, SLOTS, TT, D])
    BN = sb("BN", [P, SLOTS, TT, 6])
    MV = sb("MV", [P, SLOTS, TT, 2])
    X, C, psb = k.X, k.C, ps[:].bitcast(BF16)

    def two(name):
        return [sem(f"{name}{p}") for p in range(SLOTS)]

    s_zero, s_w2 = sem("zeroed"), sem("w2_spread")
    s_link = sem("mamba_dve_links")
    s_in, s_inz, s_cb, s_thz, s_zz = two("in_proj"), two("z_proj"), two("conv_in"), two("tanh_z"), two("silu_z")
    s_cvx, s_inbc, s_thx, s_thb, s_xs, s_bc = two("conv_x"), two("bc_psum"), two("tanh_x"), two("tanh_bc"), two("xs"), two("bc")
    s_g, s_xt, s_dec, s_ex, s_m, s_dtx = two("g"), two("x_tokens"), two("decay"), two("decay_exp"), two("m"), two("dtx")
    s_y, s_yd, s_yg, s_sq, s_yo, s_ms, s_rs = two("y"), two("y_d"), two("y_gated"), two("y_sq"), two("y_out"), two("y_ms"), two("y_rs")
    s_yoc, s_ytp, s_yt, s_hp, s_ht, s_zsp, s_tsc = two("yo_kept"), two("yt_psum"), two("yt"), two("h_psum"), two("ht"), two("score_psum"), two("score_tanh")
    s_sc, s_sct, s_pick, s_self, s_ysel, s_kv, s_ka, s_vs = two("scores"), two("scores_turned"), two("picked"), two("sel_psum"), two("ysel"), two("kv_psum"), two("ka"), two("vsel")
    s_lg, s_sub, s_ep, s_pr, s_prt, s_prc = two("logits"), two("logits_less_max"), two("exps"), two("probs"), two("probs_turned"), two("prt")
    s_rg, s_tg, s_gr, s_wx, s_var, s_lrs, s_res = two("retrieved"), two("gate_tanh"), two("gated"), two("x2_y"), two("variance"), two("ln_rstd"), two("x_written")

    def bank(p, n, a=0, z=512):
        return ps[:, (4 * p + n) * 512 + a:(4 * p + n) * 512 + z]

    LINKS_DVE = 2 * 15
    slots = range(SLOTS)
    with nc.Block() as block:
        @block.gpsimd
        def _(pool):
            for t in (CB, VSEL, PRT):
                last = nc.gpsimd.memset(t[:], 0.0)
            last.then_inc(s_zero, 1)
            with pool.Fori(0, TURNS) as j:
                def power(p):
                    pool.wait_ge(s_ms[p], j + 1)
                    nc.gpsimd.tensor_tensor(RS[:, p], MS[:, p], k.POWER[:, 0:TT], ALU.pow).then_inc(s_rs[p], 1)

                def ln_power(p):
                    pool.wait_ge(s_var[p], j + 1)
                    nc.gpsimd.tensor_tensor(MV[:, p, :, 1:2], MV[:, p, :, 1:2],
                                            k.POWER[:, 0:TT].unsqueeze(2), ALU.pow).then_inc(s_lrs[p], 1)

                for step in (power, ln_power):
                    for p in slots:
                        step(p)

        @block.vector
        def _(dve):
            dve.wait_ge(s_zero, 1)
            nc.vector.tensor_copy(W2[:], k.w("w2")[0:32].broadcast_to((32, P))).then_inc(s_w2, 1)
            with dve.Fori(0, TURNS) as j:
                link = Links(dve, s_link, LINKS_DVE, j)
                n = j + 1

                def silu_z(p):
                    dve.wait_ge(s_thz[p], n)
                    nc.vector.scalar_tensor_tensor(ZZ[:, p], TH[:, p, 0:2 * T], 1.0, bank(p, 2), ALU.add,
                                                   ALU.mult).then_inc(s_zz[p], 1)

                def conv(p):
                    dve.wait_ge(s_cb[p], n)
                    for ct in (0, 1):
                        w, b = k.w("convw")[:, 4 * ct:4 * ct + 4], k.w("convb")[:, ct:ct + 1]
                        last = nc.vector.tensor_scalar(CV[:, p, ct], CB[:, p, ct, 0:T], w[:, 0:1], b, ALU.mult, ALU.add)
                    link(last)
                    for tap in range(1, TAPS):
                        for ct in (0, 1):
                            w = k.w("convw")[:, 4 * ct + tap:4 * ct + tap + 1]
                            last = nc.vector.scalar_tensor_tensor(CV[:, p, ct], CB[:, p, ct, tap:tap + T], w,
                                                                  CV[:, p, ct], ALU.mult, ALU.add)
                        if tap < TAPS - 1:
                            link(last)
                    last.then_inc(s_cvx[p], 1)

                def silu_x(p):
                    dve.wait_ge(s_thx[p], n)
                    nc.vector.scalar_tensor_tensor(XS[:, p, 0:2], TH[:, p, 0:2 * T].rearrange("p (c t) -> p c t", t=T), 1.0,
                                                   CV[:, p, 0:2], ALU.add, ALU.mult).then_inc(s_xs[p], 1)

                def silu_bc(p):
                    dve.wait_ge(s_thb[p], n)
                    nc.vector.scalar_tensor_tensor(XS[:, p, 2:4], TH[:, p, 2 * T:4 * T].rearrange("p (c t) -> p c t", t=T), 1.0,
                                                   CV[:, p, 2:4], ALU.add, ALU.mult).then_inc(s_bc[p], 1)

                def dt_x(p):
                    dve.wait_ge(s_xt[p], n)
                    nc.vector.tensor_tensor(DTX[:, p], bank(p, 3).rearrange("p (a b) -> p a b", b=MP),
                                            spread(k.DT[:, bass.ds(16 * p + 2 * j, 2), :].rearrange("p t h -> p (t h)"), MP),
                                            ALU.mult).then_inc(s_dtx[p], 1)

                def mix(p):
                    dve.wait_ge(s_ex[p], 2 * n)
                    dve.wait_ge(s_g[p], n)
                    nc.vector.tensor_tensor(EX[:, p], EX[:, p], bank(p, 2, 0, T + P).unsqueeze(1).broadcast_to((P, MH, T + P)),
                                            ALU.mult).then_inc(s_m[p], 1)

                def gated_y(p):
                    dve.wait_ge(s_y[p], n)
                    for ct in range(2):
                        last = nc.vector.scalar_tensor_tensor(YG[:, p, ct], XS[:, p, ct], k.w("dpar")[:, ct:ct + 1],
                                                              bank(p, 0, ct * T, ct * T + T), ALU.mult, ALU.add)
                    link(last)
                    nc.vector.tensor_tensor(YG[:, p], YG[:, p], ZZ[:, p].rearrange("p (c t) -> p c t", t=T),
                                            ALU.mult).then_inc(s_yg[p], 1)

                def mean_square(p):
                    dve.wait_ge(s_yo[p], n)
                    nc.vector.tensor_scalar(MS[:, p], bank(p, 1, T, T + TT), 1.0 / DI, EPS, ALU.mult,
                                            ALU.add).then_inc(s_ms[p], 1)

                def scaled_y(p):
                    dve.wait_ge(s_rs[p], n)
                    nc.vector.tensor_tensor(YO[:, p], bank(p, 1, 0, T).rearrange("p (t d) -> p t d", d=D),
                                            spread(RS[:, p], D), ALU.mult).then_inc(s_yoc[p], 1)

                def scores(p):
                    dve.wait_ge(s_tsc[p], n)
                    nc.vector.tensor_scalar(SC[:, p], SC[:, p], 0.5, 0.5, ALU.mult, ALU.add).then_inc(s_sc[p], 1)
                    dve.wait_ge(s_sc[p], n)
                    link(nc.vector.tensor_reduce(MEAN[:, p:p + 1], SC[:, p], AX_X, ALU.add))
                    nc.vector.tensor_scalar(MEAN[:, p:p + 1], MEAN[:, p:p + 1], 1.0 / T, None, ALU.mult)

                def ranks(p):
                    dve.wait_ge(s_sct[p], n)
                    link(nc.vector.tensor_copy(SCC[:, p], bank(p, 0, T, T + TT)))
                    nc.vector.tensor_scalar(HIGH[:, p], SCC[:, p], 0.5, None, ALU.is_gt)
                    for t in range(TT):
                        nc.vector.tensor_scalar(JUNK[:, p, t], SC[:, p], SCC[:, p, t:t + 1], None, ALU.is_gt, ALU.add,
                                                accum_out=RANK[:, p, t:t + 1])
                        last = nc.vector.scalar_tensor_tensor(JUNK2[:, p, t], SC[:, p], SCC[:, p, t:t + 1],
                                                              k.c("earlier")[:, t * T:t * T + T], ALU.is_equal, ALU.mult,
                                                              accum_out=RANK[:, p, TT + t:TT + t + 1])
                    link(last)
                    link(nc.vector.tensor_tensor(RANK[:, p, 0:TT], RANK[:, p, 0:TT], RANK[:, p, TT:2 * TT], ALU.add))
                    for t in range(TT):
                        last = nc.vector.tensor_scalar(PICK[:, p, t], k.c("slot"), RANK[:, p, t:t + 1],
                                                       HIGH[:, p, t:t + 1], ALU.is_equal, ALU.mult)
                    last.then_inc(s_pick[p], 1)

                def empty(p):
                    dve.wait_ge(s_self[p], n)
                    nc.vector.tensor_scalar(EMPTY[:, p], bank(p, 1, 64, 64 + POOL)[0:1], 1.0, 4.0e9, ALU.subtract, ALU.mult)
                    nc.vector.tensor_copy(YSEL[:, p], bank(p, 1, 0, POOL)).then_inc(s_ysel[p], 1)

                def less_max(p):
                    dve.wait_ge(s_lg[p], n)
                    lg = bank(p, 0, 0, TT * POOL).rearrange("p (t s) -> p t s", s=POOL)
                    link(nc.vector.tensor_reduce(MX[:, p], lg, AX_X, ALU.max))
                    nc.vector.tensor_tensor(LG[:, p], lg, spread(MX[:, p], POOL), ALU.subtract).then_inc(s_sub[p], 1)

                def probs(p):
                    dve.wait_ge(s_ep[p], n)
                    link(nc.vector.tensor_reduce(SM[:, p], LG[:, p], AX_X, ALU.add))
                    link(nc.vector.reciprocal(SM[:, p], SM[:, p]))
                    nc.vector.tensor_tensor(LG[:, p], LG[:, p], spread(SM[:, p], POOL), ALU.mult).then_inc(s_pr[p], 1)

                def gate(p):
                    xs = X[:, bass.ds(16 * p + 2 * j, 2), :]
                    link(nc.vector.scalar_tensor_tensor(WX[:, p], xs, 2.0, YO[:, p], ALU.mult, ALU.add))
                    nc.vector.tensor_scalar(MEAN[:, p:p + 1], MEAN[:, p:p + 1], 0.3, 0.5, ALU.is_gt, ALU.mult)
                    dve.wait_ge(s_tg[p], n)
                    nc.vector.scalar_tensor_tensor(GR[:, p], TG[:, p], 1.0,
                                                   bank(p, 1).rearrange("p (t c) -> p t c", t=TT)[:, :, 0:D],
                                                   ALU.add, ALU.mult).then_inc(s_gr[p], 1)
                    dve.wait_ge(s_gr[p], n)
                    link(nc.vector.scalar_tensor_tensor(WX[:, p], GR[:, p], MEAN[:, p:p + 1], WX[:, p], ALU.mult, ALU.add))

                def stats(p):
                    for t in range(TT):
                        last = nc.vector.bn_stats(BN[:, p, t], WX[:, p, t])
                    link(last)
                    alone(dve)
                    for t in range(TT):
                        last = nc.vector.bn_aggr(MV[:, p, t], BN[:, p, t])
                    link(last)
                    nc.vector.tensor_scalar(MV[:, p, :, 1:2], MV[:, p, :, 1:2], EPS, None, ALU.add).then_inc(s_var[p], 1)

                def normed(p):
                    dve.wait_ge(s_lrs[p], n)
                    for t in range(TT):
                        last = nc.vector.tensor_scalar(X[:, bass.ds(16 * p + 2 * j + t, 1), :].rearrange("p a d -> p (a d)"),
                                                       WX[:, p, t], MV[:, p, t, 0:1], MV[:, p, t, 1:2],
                                                       ALU.subtract, ALU.mult)
                    last.then_inc(s_res[p], 1)

                for step in (silu_z, conv, silu_x, silu_bc, dt_x, mix, gated_y, mean_square, scaled_y, scores, ranks,
                             empty, less_max, probs, gate, stats, normed):
                    for p in slots:
                        step(p)
                link.close()

        @block.scalar
        def _(act):
            act.wait_ge(s_zero, 1)
            with act.Fori(0, TURNS) as j:
                n = j + 1

                def tanh_z(p):
                    act.wait_ge(s_inz[p], n)
                    act.wait_ge(s_res[p], j)
                    nc.scalar.activation(TH[:, p, 0:2 * T], bank(p, 2), ACT.Tanh).then_inc(s_thz[p], 1)

                def conv_in(p):
                    act.wait_ge(s_in[p], n)
                    nc.scalar.activation(CB[:, p, :, PAD:], bank(p, 0).rearrange("p (c t) -> p c t", t=T),
                                         ACT.Copy).then_inc(s_cb[p], 1)

                def tanh_x(p):
                    act.wait_ge(s_cvx[p], n)
                    act.wait_ge(s_zz[p], n)
                    nc.scalar.activation(TH[:, p, 0:2 * T].rearrange("p (c t) -> p c t", t=T), CV[:, p, 0:2],
                                         ACT.Tanh).then_inc(s_thx[p], 1)

                def tanh_bc(p):
                    act.wait_ge(s_inbc[p], n)
                    for i in range(2):
                        bias = k.w("convb")[:, 2 + i:3 + i]
                        nc.scalar.activation(CV[:, p, 2 + i], bank(p, 1, i * T, i * T + T), ACT.Identity, bias=bias)
                        last = nc.scalar.activation(TH[:, p, 2 * T + i * T:3 * T + i * T], bank(p, 1, i * T, i * T + T),
                                                    ACT.Tanh, bias=bias)
                    last.then_inc(s_thb[p], 1)

                def decays(i):
                    def step(p):
                        act.wait_ge(s_dec[p], 2 * j + i + 1)
                        nc.scalar.activation(EX[:, p, 2 * i:2 * i + 2],
                                             ps[:, 2048 * p:2048 * p + 1024].rearrange("p (h c) -> p h c", h=2)[:, :, 0:T + P],
                                             ACT.Exp).then_inc(s_ex[p], 1)
                    return step

                def squares(p):
                    act.wait_ge(s_yg[p], n)
                    nc.scalar.activation(YSQ[:, p], YG[:, p], ACT.Square).then_inc(s_sq[p], 1)

                def yt(p):
                    act.wait_ge(s_ytp[p], n)
                    nc.scalar.activation(YT[:, p], bank(p, 2, 0, T), ACT.Copy).then_inc(s_yt[p], 1)

                def relu(p):
                    act.wait_ge(s_hp[p], n)
                    nc.scalar.activation(HT[:, p], bank(p, 3, 0, T)[0:32], ACT.Relu).then_inc(s_ht[p], 1)

                def score(p):
                    act.wait_ge(s_zsp[p], n)
                    nc.scalar.activation(SC[:, p], bank(p, 0, 0, T), ACT.Tanh, scale=0.5).then_inc(s_tsc[p], 1)

                def kv(p):
                    act.wait_ge(s_kv[p], n)
                    nc.scalar.activation(KA[:, p], bank(p, 3, 256, 256 + POOL), ACT.Copy).then_inc(s_ka[p], 1)
                    nc.scalar.activation(VSEL[0:POOL, p], bank(p, 2, 256, 512)[0:POOL], ACT.Copy).then_inc(s_vs[p], 1)

                def exps(p):
                    act.wait_ge(s_sub[p], n)
                    nc.scalar.activation(LG[:, p], LG[:, p], ACT.Exp, scale=0.25).then_inc(s_ep[p], 1)

                def prt(p):
                    act.wait_ge(s_prt[p], n)
                    nc.scalar.activation(PRT[0:POOL, p], bank(p, 3, 0, T)[0:POOL], ACT.Copy).then_inc(s_prc[p], 1)

                def tanh_gate(p):
                    act.wait_ge(s_rg[p], n)
                    nc.scalar.activation(TG[:, p], bank(p, 1).rearrange("p (t c) -> p t c", t=TT)[:, :, D:2 * D],
                                         ACT.Tanh, scale=0.5).then_inc(s_tg[p], 1)

                for step in (tanh_z, conv_in, tanh_x, tanh_bc, decays(0), decays(1), squares, yt, relu, score, kv, exps,
                             prt, tanh_gate):
                    for p in slots:
                        step(p)

        @block.tensor
        def _(pe):
            pe.wait_ge(s_w2, 1)
            with pe.Fori(0, TURNS) as j:
                n = j + 1

                def in_proj(p):
                    pe.wait_ge(s_gr[p], j)
                    rhs = k.XNT[:, bass.ds((8 * p + j) * T, T)]
                    for i, ct in enumerate((0, 1)):
                        last = nc.tensor.matmul(bank(p, 2, i * T, i * T + T), k.w("inw")[:, ct * P:ct * P + P], rhs,
                                                start=True, stop=True)
                    last.then_inc(s_inz[p], 1)
                    for i, ct in enumerate((2, 3)):
                        last = nc.tensor.matmul(bank(p, 0, i * T, i * T + T), k.w("inw")[:, ct * P:ct * P + P],
                                                rhs, start=True, stop=True)
                    last.then_inc(s_in[p], 1)
                    for i in range(2):
                        for back in range(TAPS):
                            w = k.w("tapbc")[:, 2 * P * (TAPS - 1 - back) + i * P:2 * P * (TAPS - 1 - back) + i * P + P]
                            last = nc.tensor.matmul(bank(p, 1, i * T + back, i * T + T), w,
                                                    k.XNT[:, bass.ds((8 * p + j) * T, T - back)], start=(back == 0),
                                                    stop=(back == TAPS - 1))
                    last.then_inc(s_inbc[p], 1)

                def x_tokens(p):
                    pe.wait_ge(s_xs[p], n)
                    for t in range(TT):
                        for ct in range(2):
                            last = nc.tensor.transpose(bank(p, 3, (2 * t + ct) * P, (2 * t + ct) * P + P),
                                                       XS[:, p, ct, t * P:t * P + P], k.c("ident"))
                    last.then_inc(s_xt[p], 1)

                def b_c(p):
                    pe.wait_ge(s_bc[p], n)
                    pe.wait_ge(s_zz[p], n)
                    nc.tensor.matmul(bank(p, 2, 0, T), XS[:, p, 2, 0:P], XS[:, p, 3], start=True, stop=True)
                    nc.tensor.matmul(bank(p, 2, T, T + P), XS[:, p, 2, P:T], XS[:, p, 3, P:T], start=True,
                                     stop=True).then_inc(s_g[p], 1)

                def decay(i):
                    def step(p):
                        if i == 0:
                            pe.wait_ge(s_cb[p], n)
                            pe.wait_ge(s_thb[p], n)
                        else:
                            pe.wait_ge(s_ex[p], 2 * j + 1)
                        for h in (0, 1):
                            one = k.SEL[:, bass.ds(MH * j + 2 * i + h, 1), :].rearrange("p a c -> p (a c)")
                            for s in range(TT):
                                w = T - s * P
                                o = bank(p, h, s * T, s * T + w)
                                nc.tensor.matmul(o, one[:, 0:P], k.CUMT[:, p, s:].rearrange("p t c -> p (t c)"),
                                                 start=True, stop=False)
                                nc.tensor.matmul(o, k.NCUMT[:, p, s], one[:, 0:w], start=False, stop=False)
                                last = nc.tensor.matmul(o[:, 0:P], k.IDB[:], k.LATER[:], start=False, stop=True)
                        last.then_inc(s_dec[p], 1)
                    return step

                def scan(p):
                    pe.wait_ge(s_m[p], n)
                    pe.wait_ge(s_dtx[p], n)
                    for h in range(MH):
                        o = bank(p, 0, h // 2 * T, h // 2 * T + T)[MP * (h % 2):MP * (h % 2) + MP]
                        nc.tensor.matmul(o, DTX[:, p, h], EX[:, p, h, 0:T], start=True, stop=False)
                        last = nc.tensor.matmul(o[:, P:T], DTX[:, p, MH + h], EX[:, p, h, T:T + P], start=False, stop=True)
                    last.then_inc(s_y[p], 1)

                def out_proj(p):
                    pe.wait_ge(s_sq[p], n)
                    for t in range(TT):
                        for ct in range(2):
                            nc.tensor.matmul(bank(p, 1, t * D, t * D + D), YG[:, p, ct, t * P:t * P + P],
                                             k.w("outw")[:, ct * D:ct * D + D], start=(ct == 0), stop=(ct == 1))
                    for t in range(TT):
                        for ct in range(2):
                            last = nc.tensor.matmul(bank(p, 1, T + t, T + t + 1), YSQ[:, p, ct, t * P:t * P + P],
                                                    k.c("ones")[:, 0:1], start=(ct == 0), stop=(ct == 1))
                    last.then_inc(s_yo[p], 1)

                def y_turn(p):
                    pe.wait_ge(s_yoc[p], n)
                    for t in range(TT):
                        last = nc.tensor.transpose(bank(p, 2, t * P, t * P + P), YO[:, p, t], k.c("ident"))
                    last.then_inc(s_ytp[p], 1)

                def hidden(p):
                    pe.wait_ge(s_yt[p], n)
                    nc.tensor.matmul(bank(p, 3, 0, T)[0:32], k.w("w1"), YT[:, p], start=True, stop=True).then_inc(s_hp[p], 1)

                def score(p):
                    pe.wait_ge(s_ht[p], n)
                    nc.tensor.matmul(bank(p, 0, 0, T), W2[:], HT[:, p], start=True, stop=True).then_inc(s_zsp[p], 1)

                def score_turn(p):
                    pe.wait_ge(s_sc[p], n)
                    alone(pe)
                    for t in range(TT):
                        last = nc.tensor.transpose(bank(p, 0, T + t, T + t + 1), SC[0:1, p, t * P:t * P + P],
                                                   k.c("ident")[0:1, 0:1])
                    last.then_inc(s_sct[p], 1)

                def select(p):
                    pe.wait_ge(s_pick[p], n)
                    for t in range(TT):
                        nc.tensor.matmul(bank(p, 1, 0, POOL), YO[:, p, t], PICK[:, p, t], start=(t == 0), stop=(t == TT - 1))
                    for t in range(TT):
                        last = nc.tensor.matmul(bank(p, 1, 64, 64 + POOL)[0:1], k.c("ones")[:, 0:1], PICK[:, p, t],
                                                start=(t == 0), stop=(t == TT - 1))
                    last.then_inc(s_self[p], 1)

                def keys_values(p):
                    pe.wait_ge(s_ysel[p], n)
                    nc.tensor.matmul(bank(p, 3, 256, 256 + POOL), k.AT[:], YSEL[:, p], start=True, stop=True)
                    nc.tensor.matmul(bank(p, 2, 256, 512)[0:POOL], YSEL[:, p], k.VV[:], start=True,
                                     stop=True).then_inc(s_kv[p], 1)

                def logits(p):
                    pe.wait_ge(s_ka[p], n)
                    for t in range(TT):
                        o = bank(p, 0, t * POOL, t * POOL + POOL)
                        nc.tensor.matmul(o, YT[:, p, t * P:t * P + P], KA[:, p], start=True, stop=False)
                        last = nc.tensor.matmul(o, k.c("ones")[0:1], EMPTY[:, p], start=False, stop=True)
                    last.then_inc(s_lg[p], 1)

                def probs_turn(p):
                    pe.wait_ge(s_pr[p], n)
                    alone(pe)
                    for t in range(TT):
                        last = nc.tensor.transpose(bank(p, 3, t * P, t * P + P)[0:POOL], LG[:, p, t], k.c("ident"))
                    last.then_inc(s_prt[p], 1)

                def retrieve(p):
                    pe.wait_ge(s_prc[p], n)
                    pe.wait_ge(s_vs[p], n)
                    for t in range(TT):
                        o = bank(p, 1, t * 2 * D, (t + 1) * 2 * D)
                        nc.tensor.matmul(o, PRT[:, p, t * P:t * P + P], VSEL[:, p], start=True, stop=False)
                        last = nc.tensor.matmul(o[:, D:2 * D], YT[:, p, t * P:t * P + P], k.w("g1"), start=False, stop=True)
                    last.then_inc(s_rg[p], 1)

                for step in (in_proj, x_tokens, b_c, decay(0), decay(1), scan, out_proj, y_turn, hidden, score,
                             score_turn, select, keys_values, logits, probs_turn, retrieve):
                    for p in slots:
                        step(p)


def ahead(engine, sems, by=1):
    for s in sems:
        engine.sem_inc(s, by)


def ffn_tokens(nc, sb, ps, sem, k, layer):
    norm = layer == 0
    X = k.X
    router = k.cf("router0" if norm else "router1")
    L = 4
    BN = sb("BN", [P, L, 4, 6])
    MV = sb("MV", [P, L, 4, 2])
    XN = sb("XN", [P, L, 4, D])
    XS4 = sb("XS4", [P, L, 4, D])
    XFS = sb("XFS", [P, L, 4 * P])
    lanes, turns = range(L), UNITS // L

    def lane_sems(name):
        return [sem(f"{name}{p}") for p in lanes]

    s_link = sem("links")
    s_var, s_rstd, s_xf, s_tr, s_ev, s_kept, s_lg, s_lgc = (lane_sems(n) for n in (
        "variance", "rstd", "tokens", "turned", "turned_in_slot", "all_kept", "logits", "logits_kept"))

    def tiles(p, j, t=0, n=4):
        return bass.ds((turns * p + j) * 4 + t, n)

    with nc.Block() as block:
        @block.gpsimd
        def _(pool):
            if norm:
                with pool.Fori(0, turns) as j:
                    for p in lanes:
                        pool.wait_ge(s_var[p], j + 1)
                        nc.gpsimd.tensor_tensor(MV[:, p, :, 1:2], MV[:, p, :, 1:2], k.POWER[:, 0:4].unsqueeze(2),
                                                ALU.pow).then_inc(s_rstd[p], 1)

        @block.vector
        def _(dve):
            ahead(dve, s_lgc)
            with dve.Fori(0, turns) as j:
                link = Links(dve, s_link, 4 * L if norm else 0, j)

                def stats(p):
                    for t in range(4):
                        last = nc.vector.bn_stats(BN[:, p, t], X[:, tiles(p, j, t, 1), :].rearrange("p a d -> p (a d)"))
                    link(last)
                    alone(dve)
                    for t in range(4):
                        last = nc.vector.bn_aggr(MV[:, p, t], BN[:, p, t])
                    link(last)
                    nc.vector.tensor_scalar(MV[:, p, :, 1:2], MV[:, p, :, 1:2], EPS, None, ALU.add).then_inc(s_var[p], 1)

                def normed(p):
                    dve.wait_ge(s_rstd[p], j + 1)
                    for t in range(4):
                        last = nc.vector.tensor_scalar(XN[:, p, t], X[:, tiles(p, j, t, 1), :].rearrange("p a d -> p (a d)"),
                                                       MV[:, p, t, 0:1], MV[:, p, t, 1:2], ALU.subtract, ALU.mult)
                    link(last)
                    link(nc.vector.tensor_tensor(XN[:, p], XN[:, p], k.cf("lnw").unsqueeze(1).broadcast_to((P, 4, D)),
                                                 ALU.mult))
                    dve.wait_ge(s_kept[p], j + 1)
                    nc.vector.tensor_tensor(XS4[:, p], XN[:, p], k.cf("lnb").unsqueeze(1).broadcast_to((P, 4, D)),
                                            ALU.add).then_inc(s_xf[p], 1)

                def logits(p):
                    dve.wait_ge(s_lg[p], j + 1)
                    nc.vector.tensor_copy(k.LOG[:, :, tiles(p, j)],
                                          ps[:, 2048 + 512 * p:2080 + 512 * p].rearrange("p (n e) -> p e n", e=NE)
                                          ).then_inc(s_lgc[p], 1)

                for step in ((stats, normed, logits) if norm else (logits,)):
                    for p in lanes:
                        step(p)
                link.close()

        @block.scalar
        def _(act):
            ahead(act, s_ev)
            ahead(act, s_kept)
            with act.Fori(0, turns) as j:
                if not norm:
                    for p in lanes:
                        act.wait_ge(s_kept[p], j + 1)
                        nc.scalar.activation(XS4[:, p], X[:, tiles(p, j), :], ACT.Copy).then_inc(s_xf[p], 1)
                for p in lanes:
                    act.wait_ge(s_tr[p], j + 1)
                    nc.scalar.activation(XFS[:, p], ps[:, 512 * p:512 * p + 512], ACT.Copy).then_inc(s_ev[p], 1)
                    last = nc.scalar.activation(k.XNT[:, bass.ds((turns * p + j) * 512, 512)],
                                                ps[:, 512 * p:512 * p + 512], ACT.Copy)
                    if norm:
                        last = nc.scalar.activation(k.XF[:, tiles(p, j), :], XS4[:, p], ACT.Copy)
                    last.then_inc(s_kept[p], 1)

        @block.tensor
        def _(pe):
            with pe.Fori(0, turns) as j:
                for p in lanes:
                    pe.wait_ge(s_xf[p], j + 1)
                    pe.wait_ge(s_kept[p], j + 1)
                    for t in range(4):
                        last = nc.tensor.transpose(ps[:, 512 * p + P * t:512 * p + P * t + P], XS4[:, p, t], k.c("ident"))
                    last.then_inc(s_tr[p], 1)
                for p in lanes:
                    pe.wait_ge(s_ev[p], j + 2)
                    pe.wait_ge(s_lgc[p], j + 1)
                    for t in range(4):
                        last = nc.tensor.matmul(ps[:, 2048 + 512 * p + NE * t:2048 + 512 * p + NE * t + NE],
                                                XFS[:, p, P * t:P * t + P], router, start=True, stop=True)
                    last.then_inc(s_lg[p], 1)


def route(nc, sb, ps, sem, k, layer, choices):
    OH = [sb(f"OH{c}", [P, NE, NT]) for c in range(choices)]
    EQ = sb("EQ", [P, NE, NT])
    MX = [sb(f"MXR{c}", [P, NT]) for c in range(choices)]
    FI = sb("FI", [P, NT])
    CI = sb("CI", [P, NE, NT])
    ENDS, NTL, START, OFF, ZERO = (sb(n, [P, NE]) for n in ("ENDS", "NTL", "START", "OFF", "ZERO"))
    GT = sb("GT", [P, NE, NT])
    POSF = sb("POSF", [P, NE, NT])
    POS1 = sb("POS1", [P, NT])
    TE = sb("TE", [1, TILES, NE - 1])
    TEF = sb("TEF", [1, TILES])
    s_link, s_mx, s_sig, s_oh, s_cnt, s_done = (sem(n) for n in (
        "route_links", "best_logit", "route_tanh", "experts_marked", "counted", "routed"))
    with nc.Block() as block:
        @block.vector
        def _(dve):
            link = Links(dve, s_link)
            link(nc.vector.memset(ZERO[:], 0.0))
            rev = k.c("eight").unsqueeze(2).broadcast_to((P, NE, NT))
            for c in range(choices):
                nc.vector.tensor_reduce(MX[c][:], k.LOG[:].rearrange("p e n -> p n e"), AX_X, ALU.max).then_inc(s_mx, 1)
                dve.wait_ge(s_mx, c + 1)
                best = MX[c][:].unsqueeze(1).broadcast_to((P, NE, NT))
                link(nc.vector.tensor_tensor(EQ[:], k.LOG[:], best, ALU.is_equal))
                link(nc.vector.tensor_tensor(EQ[:], EQ[:], rev, ALU.mult))
                link(nc.vector.tensor_reduce(FI[:], EQ[:].rearrange("p e n -> p n e"), AX_X, ALU.max))
                nc.vector.tensor_tensor(OH[c][:], rev, FI[:].unsqueeze(1).broadcast_to((P, NE, NT)),
                                        ALU.is_equal).then_inc(s_oh, 1)
                if c + 1 < choices:
                    dve.wait_ge(s_oh, c + 1)
                    link(nc.vector.scalar_tensor_tensor(k.LOG[:], OH[c][:], -BIG, k.LOG[:], ALU.mult, ALU.add))
            for c in range(choices):
                dve.wait_ge(s_sig, c + 1)
                nc.vector.tensor_scalar(k.GATE[:, c], k.GATE[:, c], 0.5, 0.5, ALU.mult, ALU.add)
                dve.wait_ge(s_cnt, c + 1)
                within = ps[:, 1024 * c:1024 * c + 256].rearrange("p (e n) -> p e n", e=NE)
                total = ps[:, 1024 * c + 512:1024 * c + 768]
                link(nc.vector.tensor_tensor_scan(CI[:].rearrange("p e n -> p (e n)"), k.c("ones2"), total, 0.0,
                                                  ALU.mult, ALU.add))
                link(nc.vector.tensor_copy(ENDS[:], CI[:, :, NT - 1]))
                nc.vector.tensor_copy(OFF[:, 0:1], ZERO[:, 0:1])
                link(nc.vector.tensor_copy(OFF[:, 1:NE], ENDS[:, 0:NE - 1]))
                link(nc.vector.tensor_tensor(ENDS[:], ENDS[:], OFF[:], ALU.subtract))
                link(nc.vector.tensor_tensor(GT[:], ENDS[:].unsqueeze(2).broadcast_to((P, NE, NT)),
                                             k.c("m128").unsqueeze(1).broadcast_to((P, NE, NT)), ALU.is_gt))
                link(nc.vector.tensor_reduce(NTL[:], GT[:], AX_X, ALU.add))
                link(nc.vector.tensor_tensor_scan(START[:], k.c("ones2")[:, 0:NE], NTL[:], 0.0, ALU.mult, ALU.add))
                link(nc.vector.tensor_tensor(START[:], START[:], NTL[:], ALU.subtract))
                link(nc.vector.scalar_tensor_tensor(OFF[:], START[:], float(P), OFF[:], ALU.mult, ALU.subtract))
                link(nc.vector.tensor_tensor(CI[:].rearrange("p e n -> p (e n)"), CI[:].rearrange("p e n -> p (e n)"),
                                             total, ALU.subtract))
                link(nc.vector.tensor_tensor(POSF[:], CI[:], within, ALU.add))
                link(nc.vector.tensor_tensor(POSF[:], POSF[:], OFF[:].unsqueeze(2).broadcast_to((P, NE, NT)), ALU.add))
                link(nc.vector.tensor_tensor(POSF[:], POSF[:], OH[c][:], ALU.mult))
                link(nc.vector.tensor_reduce(POS1[:], POSF[:].rearrange("p e n -> p n e"), AX_X, ALU.add))
                nc.vector.tensor_copy(k.POS[:, c], POS1[:])
                link(nc.vector.tensor_tensor(TE[:], START[0:1, 1:NE].unsqueeze(1).broadcast_to((1, TILES, NE - 1)),
                                             k.c("tile")[0:1].unsqueeze(2).broadcast_to((1, TILES, NE - 1)), ALU.is_le))
                link(nc.vector.tensor_reduce(TEF[:], TE[:], AX_X, ALU.add))
                link(nc.vector.tensor_copy(k.TEX[:, c], TEF[:]))

        @block.scalar
        def _(act):
            for c in range(choices):
                act.wait_ge(s_mx, c + 1)
                nc.scalar.activation(k.GATE[:, c], MX[c][:], ACT.Tanh, scale=0.5).then_inc(s_sig, 1)

        @block.tensor
        def _(pe):
            for c in range(choices):
                pe.wait_ge(s_oh, c + 1)
                oh = OH[c][:].rearrange("p e n -> p (e n)")
                nc.tensor.matmul(ps[:, 1024 * c:1024 * c + 256], k.c("ahead"), oh, start=True, stop=True)
                nc.tensor.matmul(ps[:, 1024 * c + 512:1024 * c + 768], k.c("ones"), oh, start=True,
                                 stop=True).then_inc(s_cnt, 1)


FLOW = 8
SENDS = 4


def experts(nc, sb, ps, sem, dram, k, layer, choices):
    W1, WD, X, ACC = k.W1, k.WD, k.X, k.ACC
    XF = k.XF if layer == 0 else k.X
    xs, ys = dram["sorted"], dram["expert_out"]
    ZS = sb("ZS", [P, SENDS, D])
    IX = sb("IX", [P, SENDS, 1], U32)
    XG = sb("XG", [P, FLOW, D])
    XGT = sb("XGT", [P, FLOW, P])
    SG = sb("SG", [P, FLOW, FF])
    HG = sb("HG", [P, FLOW, FF])
    HT = sb("HT", [P, FLOW, 2, P])
    OG = sb("OG", [P, FLOW, D])
    SS = sb("SS", [P, SLOTS, 2, 512])
    HS = sb("HS", [P, SLOTS, 2, 512])
    YB = sb("YB", [P, FLOW, D])
    IXB = sb("IXB", [P, FLOW, 1], U32)
    WX = sb("WX", [P, FLOW, D])
    BN = sb("BN", [P, FLOW, 6])
    MV = sb("MV", [P, FLOW, 2])
    slots, turns = range(SLOTS), UNITS // SLOTS
    sends, flow = NT // SENDS, TILES // FLOW

    def one(t, n):
        return t[:, bass.ds(n, 1), :].rearrange("p a d -> p (a d)")

    s_z, s_sc, s_free = ([sem(f"{n}{p}") for p in range(SENDS)] for n in ("row_scaled", "row_out", "row_slot_free"))
    s_gu, s_si, s_h, s_dn, s_acc = ([sem(f"{n}{p}") for p in slots] for n in (
        "gate_up", "silu", "shared_h", "shared_down", "accumulated"))
    with nc.Block() as block:
        @block.sync
        def _(sp):
            ahead(sp, s_free)
            with sp.Fori(0, sends) as j:
                for p in range(SENDS):
                    sp.wait_ge(s_sc[p], 16 * (j + 1))
                    sp.sem_inc(s_free[p], 1)

        @block.gpsimd
        def _(pool):
            with pool.Fori(0, sends) as j:
                for p in range(SENDS):
                    pool.wait_ge(s_z[p], j + 1)
                    alone(pool)
                    nc.gpsimd.indirect_dma_start(out=xs[0], out_offset=bass.IndirectOffsetOnAxis(ap=IX[:, p], axis=0),
                                                 in_=ZS[:, p], in_offset=None).then_inc(s_sc[p], 16)
            for p in range(SENDS):
                pool.wait_ge(s_sc[p], 16 * sends)

        @block.vector
        def _(dve):
            ahead(dve, s_acc)
            with dve.Fori(0, turns) as j:
                for p in slots:
                    dve.wait_ge(s_si[p], j + 1)
                    nc.vector.tensor_tensor(HS[:, p], SS[:, p], ps[:, 2048 * p + 1024:2048 * p + 2048].rearrange(
                        "p (c t) -> p c t", c=2), ALU.mult).then_inc(s_h[p], 1)
                for p in slots:
                    dve.wait_ge(s_dn[p], j + 1)
                    t = bass.ds((turns * p + j) * 4, 4)
                    nc.vector.scalar_tensor_tensor(
                        ACC[:, t, :], X[:, t, :], 2.0 if layer == 0 else 1.0,
                        ps[:, 2048 * p:2048 * p + 512].rearrange("p (t d) -> p t d", d=D), ALU.mult,
                        ALU.add).then_inc(s_acc[p], 1)

        @block.scalar
        def _(act):
            with act.Fori(0, turns) as j:
                for p in slots:
                    for i in range(SENDS):
                        n = SENDS * SLOTS * j + SENDS * p + i
                        act.wait_ge(s_free[i], SLOTS * j + p + 1)
                        nc.scalar.activation(IX[:, i], k.POS[:, 0, bass.ds(n, 1)], ACT.Copy)
                        nc.scalar.activation(ZS[:, i], one(XF, n), ACT.Copy,
                                             scale=k.GATE[:, 0, bass.ds(n, 1)]).then_inc(s_z[i], 1)
                    act.wait_ge(s_gu[p], j + 1)
                    act.wait_ge(s_acc[p], j + 1)
                    nc.scalar.activation(SS[:, p], ps[:, 2048 * p:2048 * p + 1024].rearrange("p (c t) -> p c t", c=2),
                                         ACT.Silu).then_inc(s_si[p], 1)

        @block.tensor
        def _(pe):
            pe.wait_ge(k.s_w[layer], 32)
            with pe.Fori(0, turns) as j:
                for p in slots:
                    pe.wait_ge(s_acc[p], j + 1)
                    for i in range(4):
                        last = nc.tensor.matmul(ps[:, 2048 * p + 512 * i:2048 * p + 512 * i + 512],
                                                W1[:, NE, i * P:i * P + P],
                                                k.XNT[:, bass.ds((turns * p + j) * 512, 512)], start=True, stop=True)
                    last.then_inc(s_gu[p], 1)
                for p in slots:
                    pe.wait_ge(s_h[p], j + 1)
                    for t in range(4):
                        for f in range(2):
                            last = nc.tensor.matmul(ps[:, 2048 * p + P * t:2048 * p + P * t + P],
                                                    HS[:, p, f, P * t:P * t + P], WD[:, NE, f], start=(f == 0),
                                                    stop=(f == 1))
                    last.then_inc(s_dn[p], 1)

    for c in range(choices):
        s_ld, s_xt, s_xc, s_gu, s_si, s_h, s_ht, s_hc, s_dn, s_og, s_st = ([sem(f"{n}{c}_{p}") for p in range(FLOW)] for n in (
            "rows_in", "rows_turned", "rows_kept", "e_gate_up", "e_silu", "e_h", "h_turned", "h_kept", "e_down",
            "e_out", "e_stored")) if c == 0 else k.flow_sems
        k.flow_sems = (s_ld, s_xt, s_xc, s_gu, s_si, s_h, s_ht, s_hc, s_dn, s_og, s_st)
        s_prep, s_out, s_back = sem(f"pool_links{c}"), sem(f"next_out{c}"), sem(f"first_back{c}")
        base = c * flow

        def bank(p, a=0, z=512):
            return ps[:, p * 512 + a:p * 512 + z]

        with nc.Block() as block:
            @block.sync
            def _(sp):
                with sp.Fori(base, base + flow) as j:
                    row = (j - base) * (FLOW * P)
                    for p in range(FLOW):
                        sp.wait_ge(s_xt[p], j + 1)
                        sp.dma_start(XG[:, p], xs[c][bass.ds(row + p * P, P), :]).then_inc(s_ld[p], 16)
                    for p in range(FLOW):
                        sp.wait_ge(s_og[p], j + 2)
                        sp.dma_start(ys[c][bass.ds(row + p * P, P), :], OG[:, p]).then_inc(s_st[p], 16)
                for p in range(FLOW):
                    sp.wait_ge(s_st[p], 16 * (base + flow + 1))

            @block.gpsimd
            def _(pool):
                if c + 1 < choices:
                    with pool.Fori(0, NT) as n:
                        nc.gpsimd.tensor_tensor(ZS[:, 0], one(XF, n), k.GATE[:, c + 1, bass.ds(n, 1)].broadcast_to((P, D)),
                                                ALU.mult)
                        nc.gpsimd.tensor_copy(IX[:, 0], k.POS[:, c + 1, bass.ds(n, 1)]).then_inc(s_prep, 1)
                        pool.wait_ge(s_prep, n + 1)
                        alone(pool)
                        nc.gpsimd.indirect_dma_start(out=xs[c + 1], out_offset=bass.IndirectOffsetOnAxis(ap=IX[:, 0], axis=0),
                                                     in_=ZS[:, 0], in_offset=None).then_inc(s_out, 16)
                        pool.wait_ge(s_out, 16 * (n + 1))
                if c:
                    ahead(pool, [s_prep], 1)
                    with pool.Fori(0, NT) as n:
                        pool.wait_ge(s_prep, 2 * n + 1)
                        nc.gpsimd.tensor_copy(IX[:, 0], k.POS[:, c - 1, bass.ds(n, 1)]).then_inc(s_prep, 1)
                        pool.wait_ge(s_prep, 2 * n + 2)
                        alone(pool)
                        nc.gpsimd.indirect_dma_start(out=ZS[:, 0], out_offset=None, in_=ys[c - 1],
                                                     in_offset=bass.IndirectOffsetOnAxis(ap=IX[:, 0], axis=0)
                                                     ).then_inc(s_back, 16)
                        pool.wait_ge(s_back, 16 * (n + 1))
                        nc.gpsimd.tensor_tensor(one(ACC, n), one(ACC, n), ZS[:, 0], ALU.add).then_inc(s_prep, 1)

            @block.vector
            def _(dve):
                if c == 0:
                    ahead(dve, s_og)
                with dve.Fori(base, base + flow) as j:
                    for p in range(FLOW):
                        dve.wait_ge(s_xt[p], j + 2)
                        nc.vector.tensor_copy(XGT[:, p], bank(p, 0, P)).then_inc(s_xc[p], 1)
                    for p in range(FLOW):
                        dve.wait_ge(s_si[p], j + 1)
                        nc.vector.tensor_tensor(HG[:, p], SG[:, p], bank(p, FF, 2 * FF), ALU.mult).then_inc(s_h[p], 1)
                    for p in range(FLOW):
                        dve.wait_ge(s_dn[p], j + 1)
                        dve.wait_ge(s_st[p], 16 * (j + 1))
                        nc.vector.tensor_copy(OG[:, p], bank(p, 2 * P, 3 * P)).then_inc(s_og[p], 1)

            @block.scalar
            def _(act):
                if c == 0:
                    ahead(act, s_xt)
                    ahead(act, s_st, 16)
                with act.Fori(base, base + flow) as j:
                    for p in range(FLOW):
                        act.wait_ge(s_gu[p], j + 1)
                        nc.scalar.activation(SG[:, p], bank(p, 0, FF), ACT.Silu).then_inc(s_si[p], 1)
                    for p in range(FLOW):
                        act.wait_ge(s_ht[p], j + 1)
                        nc.scalar.activation(HT[:, p].rearrange("p c t -> p (c t)"), bank(p, 0, 2 * P),
                                             ACT.Copy).then_inc(s_hc[p], 1)

            @block.tensor
            def _(pe):
                with pe.Fori(base, base + flow) as j:
                    which = [nc.tensor.value_load(k.TEX[0:1, c, bass.ds((j - base) * FLOW + p, 1)], min_val=0,
                                                  max_val=NE - 1) for p in range(FLOW)]
                    for p in range(FLOW):
                        pe.wait_ge(s_ld[p], 16 * (j + 1))
                        pe.wait_ge(s_og[p], j + 1)
                        nc.tensor.transpose(bank(p, 0, P), XG[:, p], k.c("ident")).then_inc(s_xt[p], 1)
                    for p in range(FLOW):
                        pe.wait_ge(s_xc[p], j + 1)
                        nc.tensor.matmul(bank(p), XGT[:, p], W1[:, bass.ds(which[p], 1), :].rearrange("p a f -> p (a f)"),
                                         start=True, stop=True).then_inc(s_gu[p], 1)
                    for p in range(FLOW):
                        pe.wait_ge(s_h[p], j + 1)
                        for f in range(2):
                            last = nc.tensor.transpose(bank(p, f * P, P + f * P), HG[:, p, f * P:f * P + P], k.c("ident"))
                        last.then_inc(s_ht[p], 1)
                    for p in range(FLOW):
                        pe.wait_ge(s_hc[p], j + 1)
                        for f in range(2):
                            last = nc.tensor.matmul(bank(p, 2 * P, 3 * P), HT[:, p, f],
                                                    WD[:, bass.ds(which[p], 1), f].rearrange("p a f -> p (a f)"),
                                                    start=(f == 0), stop=(f == 1))
                        last.then_inc(s_dn[p], 1)

    s_ix, s_back, s_sum, s_x = ([sem(f"{n}{p}") for p in range(FLOW)] for n in ("places", "rows_back", "rows_added", "x_normed"))
    s_link, s_var, s_rstd = sem("back_links"), sem("x_variance"), sem("x_rstd")
    backs, c = NT // FLOW, choices - 1
    with nc.Block() as block:
        @block.gpsimd
        def _(pool):
            with pool.Fori(0, backs) as j:
                for p in range(FLOW):
                    pool.wait_ge(s_ix[p], j + 1)
                    pool.wait_ge(s_sum[p], j + 1)
                    alone(pool)
                    nc.gpsimd.indirect_dma_start(out=YB[:, p], out_offset=None, in_=ys[c],
                                                 in_offset=bass.IndirectOffsetOnAxis(ap=IXB[:, p], axis=0)
                                                 ).then_inc(s_back[p], 16)
                pool.wait_ge(s_var, j + 1)
                nc.gpsimd.tensor_tensor(MV[:, :, 1], MV[:, :, 1], k.POWER[:, 0:FLOW], ALU.pow).then_inc(s_rstd, 1)

        @block.scalar
        def _(act):
            with act.Fori(0, backs) as j:
                for p in range(FLOW):
                    act.wait_ge(s_sum[p], j + 1)
                    nc.scalar.activation(IXB[:, p], k.POS[:, c, bass.ds(FLOW * j + p, 1)], ACT.Copy).then_inc(s_ix[p], 1)

        @block.vector
        def _(dve):
            ahead(dve, s_sum)
            with dve.Fori(0, backs) as j:
                link = Links(dve, s_link, 2, j)
                for p in range(FLOW):
                    dve.wait_ge(s_back[p], 16 * (j + 1))
                    nc.vector.tensor_tensor(WX[:, p], YB[:, p], one(ACC, FLOW * j + p), ALU.add).then_inc(s_sum[p], 1)
                for p in range(FLOW):
                    dve.wait_ge(s_sum[p], j + 2)
                    last = nc.vector.bn_stats(BN[:, p], WX[:, p])
                link(last)
                alone(dve)
                for p in range(FLOW):
                    last = nc.vector.bn_aggr(MV[:, p], BN[:, p])
                link(last)
                nc.vector.tensor_scalar(MV[:, :, 1], MV[:, :, 1], EPS, None, ALU.add).then_inc(s_var, 1)
                dve.wait_ge(s_rstd, j + 1)
                for p in range(FLOW):
                    nc.vector.tensor_scalar(one(X, FLOW * j + p), WX[:, p], MV[:, p, 0:1], MV[:, p, 1:2],
                                            ALU.subtract, ALU.mult).then_inc(s_x[p], 1)
                dve.wait_ge(s_x[FLOW - 1], j + 1)
                link.close()


AH, AD = 16, 8
PAIRS = [(0, 0), (0, 1), (0, 2), (1, 0), (1, 1), (2, 0)]
HROWS = AD * len(PAIRS) + 6
MROW = 2 * HROWS
GROUPS = AH // 2


def alibi_parts(h):
    return 1 if h % 2 else 3


def alibi_at(h):
    return h // 2 * 4 + (3 if h % 2 else 0)


def qkv(nc, sb, ps, sem, dram, k):
    XS4 = sb("AXS4", [P, SLOTS, 4, D])
    XTS = sb("XTS", [P, SLOTS, 512])
    QF = sb("QF", [P, SLOTS, 2, 512])
    WQ = sb("WQ", [P, 3 * D])
    BQ = sb("BQ", [P, 2])
    BV = sb("BV", [P, D])
    slots, turns = range(SLOTS), UNITS // SLOTS
    s_w, s_b, s_one, s_bq = sem("qkv_loaded"), sem("attn_consts_loaded"), sem("ones_set"), sem("bias_scaled")
    s_link = sem("qkv_links")

    def two(name):
        return [sem(f"{name}{p}") for p in slots]

    s_x, s_tr, s_xt, s_qk, s_v, s_qf, s_vx, s_parts = (two(n) for n in (
        "a_tokens", "a_turned", "a_turned_kept", "qk_psum", "v_psum", "qk_kept", "v_kept", "qk_parts"))

    def bank(p, n, a=0, z=512):
        return ps[:, (4 * p + n) * 512 + a:(4 * p + n) * 512 + z]

    with nc.Block() as block:
        @block.sync
        def _(sp):
            load_experts(sp, dram, k, 1)
            sp.dma_start(WQ[:], dram["wqkv"]).then_inc(s_w, 16)
            sp.dma_start(BQ[:], dram["bqk"]).then_inc(s_w, 16)
            sp.dma_start(BV[:], dram["bv"]).then_inc(s_w, 16)
            for p in slots:
                sp.dma_start(k.QA[:, p], dram["qrows"]).then_inc(s_b, 16)
                sp.dma_start(k.KA[:, p], dram["krows"]).then_inc(s_b, 16)
            sp.dma_start(k.SI[:], dram["slopes"]).then_inc(s_b, 16)
            sp.dma_start(k.DL[:], dram["ramps"]).then_inc(s_b, 16)
            sp.dma_start(k.WP[:], dram["wproj"]).then_inc(s_b, 16)
            sp.wait_ge(s_b, 16 * (2 * SLOTS + 3))

        @block.gpsimd
        def _(pool):
            nc.gpsimd.memset(k.VX[:], 1.0).then_inc(s_one, 1)
            with pool.Fori(0, turns) as j:
                for p in slots:
                    pool.wait_ge(s_tr[p], j)
                    nc.gpsimd.tensor_copy(XS4[:, p], k.X[:, bass.ds((turns * p + j) * 4, 4), :]).then_inc(s_x[p], 1)

        @block.vector
        def _(dve):
            dve.wait_ge(s_w, 48)
            nc.vector.tensor_scalar(BQ[:, 0:1], BQ[:, 0:1], AD ** -0.5, None, ALU.mult).then_inc(s_bq, 1)
            dve.wait_ge(s_one, 1)
            with dve.Fori(0, turns) as j:
                link = Links(dve, s_link, 3 * 2 * SLOTS, j)
                for p in slots:
                    dve.wait_ge(s_v[p], j + 1)
                    for t in range(4):
                        last = nc.vector.tensor_tensor(
                            k.VX[:, bass.ds((turns * p + j) * 4 + t, 1), :, 0:AD].rearrange("p a h d -> p (a h) d"),
                            bank(p, 3, t * P, t * P + P).rearrange("p (h d) -> p h d", h=AH),
                            BV[:].rearrange("p (h d) -> p h d", h=AH), ALU.add)
                    last.then_inc(s_vx[p], 1)
                    dve.wait_ge(s_qf[p], j + 1)
                    cols = bass.ds((turns * p + j) * 512, 512)
                    for i, parts in enumerate((k.QP, k.KP)):
                        link(nc.vector.tensor_copy(parts[:, 0, cols], QF[:, p, i]))
                        link(nc.vector.tensor_tensor(QF[:, p, i], QF[:, p, i], parts[:, 0, cols], ALU.subtract))
                        link(nc.vector.tensor_copy(parts[:, 1, cols], QF[:, p, i]))
                        last = nc.vector.tensor_tensor(parts[:, 2, cols], QF[:, p, i], parts[:, 1, cols], ALU.subtract)
                    last.then_inc(s_parts[p], 1)
                link.close()

        @block.scalar
        def _(act):
            act.wait_ge(s_bq, 1)
            with act.Fori(0, turns) as j:
                for p in slots:
                    act.wait_ge(s_tr[p], j + 1)
                    act.wait_ge(s_v[p], j)
                    nc.scalar.activation(XTS[:, p], bank(p, 0), ACT.Copy).then_inc(s_xt[p], 1)
                for p in slots:
                    act.wait_ge(s_qk[p], j + 1)
                    act.wait_ge(s_parts[p], j)
                    nc.scalar.activation(QF[:, p, 0], bank(p, 1), ACT.Identity, bias=BQ[:, 0:1], scale=AD ** -0.5)
                    nc.scalar.activation(QF[:, p, 1], bank(p, 2), ACT.Identity, bias=BQ[:, 1:2]).then_inc(s_qf[p], 1)

        @block.tensor
        def _(pe):
            pe.wait_ge(s_w, 48)
            with pe.Fori(0, turns) as j:
                for p in slots:
                    pe.wait_ge(s_x[p], j + 1)
                    pe.wait_ge(s_xt[p], j)
                    for t in range(4):
                        last = nc.tensor.transpose(bank(p, 0, P * t, P * t + P), XS4[:, p, t], k.c("ident"))
                    last.then_inc(s_tr[p], 1)
                for p in slots:
                    pe.wait_ge(s_xt[p], j + 1)
                    pe.wait_ge(s_qf[p], j)
                    pe.wait_ge(s_vx[p], j)
                    for i in range(2):
                        last = nc.tensor.matmul(bank(p, 1 + i), WQ[:, i * D:i * D + D], XTS[:, p], start=True, stop=True)
                    last.then_inc(s_qk[p], 1)
                    for t in range(4):
                        last = nc.tensor.matmul(bank(p, 3, P * t, P * t + P), XTS[:, p, P * t:P * t + P], WQ[:, 2 * D:3 * D],
                                                start=True, stop=True)
                    last.then_inc(s_v[p], 1)


def attention(nc, sb, ps, sem, k):
    PR = sb("PRA", [P, 2, 4, 512])
    MX = sb("MXA", [P, SLOTS, TT, AH])
    MR = sb("MRA", [P, SLOTS, TT, AH])
    MP = sb("MPA", [P, SLOTS, TT, 3, AH], BF16)
    MT = sb("MTA", [3 * AH, SLOTS, T], BF16)
    OS = sb("OSA", [P, SLOTS, 4 * T])
    RC = sb("RCA", [P, SLOTS, TT, AH])
    YA = sb("YAA", [P, SLOTS, TT, D])
    YAT = sb("YATA", [P, SLOTS, T])
    WX = sb("WXA", [P, SLOTS, TT, D])
    BN = sb("BNA", [P, SLOTS, TT, 6])
    MV = sb("MVA", [P, SLOTS, TT, 2])
    VS = sb("VSA", [P, SLOTS, TT, AH, AD + 1])
    X = k.X
    psb = ps[:].bitcast(BF16)
    slots, turns = range(SLOTS), B // SLOTS
    s_link = sem("attn_links")
    s_s1, s_mx, s_s2, s_ex = sem("scores"), sem("maxima"), sem("scores_turned"), sem("exps")

    def two(name):
        return [sem(f"{name}{p}") for p in slots]

    s_q, s_mp, s_mt, s_mc, s_m, s_pv, s_vs = (two(n) for n in (
        "qk_rows", "max_parts", "max_turned", "max_kept", "max_rows", "values_mixed", "v_slot"))
    s_os, s_ot, s_ya, s_yt, s_yc, s_pj, s_wx, s_var, s_rs, s_x = (two(n) for n in (
        "mixed_kept", "mixed_turned", "y_heads", "yh_turned", "yh_kept", "projected", "ax_sum", "a_variance", "a_rstd",
        "ax_normed"))

    def pair(g):
        return 1024 * (g % 2)

    def obank(p, a=0, z=1024):
        return ps[:, 2048 + 1024 * p + a:2048 + 1024 * p + z]

    with nc.Block() as block:
        @block.sync
        def _(sp):
            with sp.Fori(0, turns) as j:
                def rows(p):
                    sp.wait_ge(s_pv[p], 4 * j)
                    cols = bass.ds((turns * p + j) * T, T)
                    for hh in range(2):
                        for c, (a, b) in enumerate(PAIRS):
                            r = HROWS * hh + AD * c
                            sp.dma_start(k.QA[r:r + AD, p, :, hh, :], k.QP[64 * hh:64 * hh + 64, a, cols]).then_inc(s_q[p], 16)
                            sp.dma_start(k.KA[r:r + AD, p, :, :], k.KP[64 * hh:64 * hh + 64, b, cols]).then_inc(s_q[p], 16)

                def maxima(p):
                    sp.wait_ge(s_mc[p], j + 1)
                    sp.dma_start(k.QA[MROW:MROW + 3, p].rearrange("p a b t -> p (a b) t"),
                                 MT[:, p]).then_inc(s_m[p], 16)

                for step in (rows, maxima):
                    for p in slots:
                        step(p)

        @block.gpsimd
        def _(pool):
            with pool.Fori(0, turns) as j:
                for p in slots:
                    pool.wait_ge(s_pv[p], 4 * j)
                    nc.gpsimd.tensor_copy(VS[:, p], k.VX[:, bass.ds((turns * p + j) * TT, TT), :, :]).then_inc(s_vs[p], 1)
                for p in slots:
                    pool.wait_ge(s_var[p], j + 1)
                    nc.gpsimd.tensor_tensor(MV[:, p, :, 1:2], MV[:, p, :, 1:2], k.POWER[:, 0:TT].unsqueeze(2),
                                            ALU.pow).then_inc(s_rs[p], 1)

        @block.vector
        def _(dve):
            with dve.Fori(0, turns) as j:
                link = Links(dve, s_link, SLOTS * 7, j)

                def maxima(p):
                    for g in range(GROUPS):
                        i = GROUPS * p + g
                        dve.wait_ge(s_s1, 2 * GROUPS * j + i + 1)
                        nc.vector.tensor_reduce(MX[:, p].rearrange("p t h -> p h t")[:, 2 * g:2 * g + 2],
                                                ps[:, pair(g):pair(g) + 1024].rearrange("p (h t s) -> p h t s", h=2, t=TT),
                                                AX_X, ALU.max).then_inc(s_mx, 1)
                    dve.wait_ge(s_mx, 2 * GROUPS * j + GROUPS * (p + 1))
                    link(nc.vector.tensor_scalar(MP[:, p, :, 0], MX[:, p], -1.0, None, ALU.mult))
                    link(nc.vector.scalar_tensor_tensor(MR[:, p], MX[:, p], -1.0, MP[:, p, :, 0], ALU.mult, ALU.subtract))
                    link(nc.vector.tensor_copy(MP[:, p, :, 1], MR[:, p]))
                    nc.vector.tensor_tensor(MP[:, p, :, 2], MR[:, p], MP[:, p, :, 1], ALU.subtract).then_inc(s_mp[p], 1)

                def kept(p):
                    dve.wait_ge(s_pv[p], 4 * (j + 1))
                    nc.vector.tensor_copy(OS[:, p], obank(p)).then_inc(s_os[p], 1)

                def heads(p):
                    dve.wait_ge(s_ot[p], j + 1)
                    o = obank(p).rearrange("p (t h c) -> p t h c", t=TT, h=AH)
                    for t in range(TT):
                        last = nc.vector.reciprocal(RC[:, p, t], o[:, t, :, AD])
                    link(last)
                    for t in range(TT):
                        last = nc.vector.tensor_tensor(YA[:, p, t].rearrange("p (h d) -> p h d", h=AH), o[:, t, :, 0:AD],
                                                       spread(RC[:, p, t], AD), ALU.mult)
                    last.then_inc(s_ya[p], 1)

                def sums(p):
                    xs = X[:, bass.ds(2 * (turns * p + j), 2), :]
                    dve.wait_ge(s_pj[p], j + 1)
                    link(nc.vector.tensor_tensor(WX[:, p], xs, obank(p, 512, 768).rearrange("p (t d) -> p t d", d=D), ALU.add))
                    for t in range(TT):
                        last = nc.vector.bn_stats(BN[:, p, t], WX[:, p, t])
                    link(last)
                    alone(dve)
                    for t in range(TT):
                        last = nc.vector.bn_aggr(MV[:, p, t], BN[:, p, t])
                    link(last)
                    nc.vector.tensor_scalar(MV[:, p, :, 1:2], MV[:, p, :, 1:2], EPS, None, ALU.add).then_inc(s_var[p], 1)

                def normed(p):
                    dve.wait_ge(s_rs[p], j + 1)
                    for t in range(TT):
                        last = nc.vector.tensor_scalar(X[:, bass.ds(2 * (turns * p + j) + t, 1), :].rearrange("p a d -> p (a d)"),
                                                       WX[:, p, t], MV[:, p, t, 0:1], MV[:, p, t, 1:2],
                                                       ALU.subtract, ALU.mult)
                    last.then_inc(s_x[p], 1)

                for step in (maxima, kept, heads, sums, normed):
                    for p in slots:
                        step(p)
                link.close()

        @block.scalar
        def _(act):
            with act.Fori(0, turns) as j:
                def kept(p):
                    act.wait_ge(s_mt[p], j + 1)
                    act.wait_ge(s_m[p], 16 * j)
                    nc.scalar.activation(MT[:, p], psb[0:3 * AH, 2 * (2048 + 1024 * p):2 * (2048 + 1024 * p) + T],
                                         ACT.Copy).then_inc(s_mc[p], 1)

                def exps(p):
                    for g in range(GROUPS):
                        i = GROUPS * p + g
                        act.wait_ge(s_s2, 2 * GROUPS * j + i + 1)
                        if g >= 4:
                            act.wait_ge(s_pv[p], 4 * j + g // 2 - 1)
                        elif p:
                            act.wait_ge(s_pv[0], 4 * j + 3 + g // 2)
                        else:
                            act.wait_ge(s_pv[1], 4 * j)
                        nc.scalar.activation(PR[:, g // 2 % 2, g % 2 * 2:g % 2 * 2 + 2],
                                             ps[:, pair(g):pair(g) + 1024].rearrange("p (h c) -> p h c", h=2),
                                             ACT.Exp).then_inc(s_ex, 1)

                def y_kept(p):
                    act.wait_ge(s_yt[p], j + 1)
                    nc.scalar.activation(YAT[:, p], obank(p, 0, T), ACT.Copy).then_inc(s_yc[p], 1)

                kept(0)
                kept(1)
                exps(0)
                exps(1)
                y_kept(0)
                y_kept(1)

        @block.tensor
        def _(pe):
            with pe.Fori(0, turns) as j:
                def pass1(p):
                    pe.wait_ge(s_q[p], 16 * 4 * len(PAIRS) * (j + 1))
                    for g in range(GROUPS):
                        i = GROUPS * p + g
                        if i >= 2:
                            pe.wait_ge(s_mx, 2 * GROUPS * j + i - 1)
                        else:
                            pe.wait_ge(s_ex, 2 * GROUPS * j)
                        for h in (2 * g, 2 * g + 1):
                            for t in range(TT):
                                o = ps[:, pair(g) + 512 * (h % 2) + T * t:pair(g) + 512 * (h % 2) + T * t + T]
                                nc.tensor.matmul(o, k.QA[0:MROW, p, h // 2, h % 2, t * P:t * P + P], k.KA[0:MROW, p, h // 2],
                                                 start=True, stop=False)
                                n = alibi_parts(h)
                                for a in range(n):
                                    last = nc.tensor.matmul(o[:, t * P:t * P + P], k.DL[:, 0], k.SI[:, alibi_at(h) + a],
                                                            start=False, stop=(a == n - 1))
                        last.then_inc(s_s1, 1)

                def turn_max(p):
                    pe.wait_ge(s_mp[p], j + 1)
                    pe.wait_ge(s_x[p], j)
                    alone(pe)
                    for t in range(TT):
                        at = 2 * (2048 + 1024 * p) + t * P
                        last = nc.tensor.transpose(psb[0:3 * AH, at:at + P], MP[:, p, t].rearrange("p a h -> p (a h)"), k.IDB[:])
                    last.then_inc(s_mt[p], 1)

                def mix(p, quad):
                    pe.wait_ge(s_ex, 2 * GROUPS * j + GROUPS * p + 2 * quad + 2)
                    if quad == 0:
                        pe.wait_ge(s_vs[p], j + 1)
                    for s in range(TT):
                        for h in range(4):
                            last = nc.tensor.matmul(obank(p, quad * T, quad * T + T)[32 * h:32 * h + AD + 1],
                                                    VS[:, p, s, 4 * quad + h], PR[:, quad % 2, h, s * T:s * T + T],
                                                    start=(s == 0), stop=(s == TT - 1), tile_position=(0, 32 * h))
                    last.then_inc(s_pv[p], 1)

                def pass2(p):
                    pe.wait_ge(s_m[p], 16 * (j + 1))
                    for g in range(GROUPS):
                        i = GROUPS * p + g
                        if i >= 2:
                            pe.wait_ge(s_ex, 2 * GROUPS * j + i - 1)
                        else:
                            pe.wait_ge(s_mx, 2 * GROUPS * (j + 1))
                        for h in (2 * g, 2 * g + 1):
                            for s in range(TT):
                                o = ps[:, pair(g) + 512 * (h % 2) + T * s:pair(g) + 512 * (h % 2) + T * s + T]
                                nc.tensor.matmul(o, k.KA[0:MROW + 3, p, h // 2, s * P:s * P + P],
                                                 k.QA[0:MROW + 3, p, h // 2, h % 2], start=True, stop=False)
                                n = alibi_parts(h)
                                for a in range(n):
                                    last = nc.tensor.matmul(o[:, s * P:s * P + P], k.DL[:, 1], k.SI[:, alibi_at(h) + a],
                                                            start=False, stop=(a == n - 1))
                        last.then_inc(s_s2, 1)
                        if g % 2 and g > 1:
                            mix(p, g // 2 - 1)
                    mix(p, GROUPS // 2 - 1)

                def turned(p):
                    pe.wait_ge(s_os[p], j + 1)
                    for t in range(TT):
                        for quad in range(4):
                            last = nc.tensor.transpose(obank(p, t * 512 + quad * P, t * 512 + quad * P + P),
                                                       OS[:, p, quad * T + t * P:quad * T + t * P + P], k.c("ident"))
                    last.then_inc(s_ot[p], 1)

                def y_turned(p):
                    pe.wait_ge(s_ya[p], j + 1)
                    for t in range(TT):
                        last = nc.tensor.transpose(obank(p, t * P, t * P + P), YA[:, p, t], k.c("ident"))
                    last.then_inc(s_yt[p], 1)

                def project(p):
                    pe.wait_ge(s_yc[p], j + 1)
                    for t in range(TT):
                        o = obank(p, 512 + t * P, 512 + t * P + P)
                        nc.tensor.matmul(o, YAT[:, p, t * P:t * P + P], k.WP[:, 0:D], start=True, stop=False)
                        last = nc.tensor.matmul(o, k.c("ones")[0:1], k.WP[0:1, D:2 * D], start=False, stop=True)
                    last.then_inc(s_pj[p], 1)

                pass1(0)
                pass1(1)
                turn_max(0)
                turn_max(1)
                pass2(0)
                pass2(1)
                for step in (turned, y_turned, project):
                    for p in slots:
                        step(p)


def staged(nc, tag, stage):
    with ExitStack() as ctx:
        sems = []

        def sem(name):
            sems.append(nc.alloc_semaphore(f"{tag}_{name}"))
            return sems[-1]

        stage(lambda name, shape, dtype=F32: ctx.enter_context(nc.sbuf_tensor(f"{tag}_{name}", shape, dtype)), sem)
        nc.all_engine_barrier()
        nc.clear_and_free_semaphores(sems)
        nc.all_engine_barrier()


def load_experts(sp, dram, k, layer):
    sp.dma_start(k.W1[:], dram["w1"][layer]).then_inc(k.s_w[layer], 16)
    sp.dma_start(k.WD[:].rearrange("p e f d -> p (e f d)"), dram["wd"][layer]).then_inc(k.s_w[layer], 16)


def attention_stage(nc, ps, dram, k):
    with ExitStack() as ctx:
        def sb(name, shape, dtype=F32):
            return ctx.enter_context(nc.sbuf_tensor(name, shape, dtype))

        k.QP, k.KP = sb("QP", [P, 3, NT * P], BF16), sb("KP", [P, 3, NT * P], BF16)
        k.VX = sb("VX", [P, NT, AH, AD + 1])
        k.QA = sb("QA", [P, SLOTS, AH // 2, 2, T], BF16)
        k.KA = sb("KA_rows", [P, SLOTS, AH // 2, T], BF16)
        k.SI = sb("SI", [P, AH // 2 * 4, P], BF16)
        k.DL = sb("DL", [P, 2, P], BF16)
        k.WP = sb("WP", [P, 2 * D])
        staged(nc, "qkv", lambda sb, sem: qkv(nc, sb, ps, sem, dram, k))
        staged(nc, "attention", lambda sb, sem: attention(nc, sb, ps, sem, k))


def build(nc, dram, stages=4):
    with ExitStack() as ctx:
        def sb(name, shape, dtype=F32):
            return ctx.enter_context(nc.sbuf_tensor(name, shape, dtype))

        def sem(name):
            return ctx.enter_context(nc.semaphore(name))

        k = Kept()
        ps = ctx.enter_context(nc.psum_tensor("ps", [P, 8 * 512], F32))
        k.X = sb("X", [P, NT, D])
        k.C = sb("C", [P, CONST_W])
        k.XNT = sb("XNT", [P, NT * P])
        k.POWER = sb("POWER", [P, 16])
        k.IDB = sb("IDB", [P, P], BF16)
        k.F = sb("F", [P, WF_W])
        k.s_w = [sem(f"experts_loaded{layer}") for layer in range(2)]
        k.W1 = sb("W1", [P, NE + 1, 2 * FF])
        k.WD = sb("WD", [P, NE + 1, 2, D])
        with ExitStack() as inner:
            def own(name, shape, dtype=F32):
                return inner.enter_context(nc.sbuf_tensor(name, shape, dtype))

            k.W = own("W", [P, WA_W])
            k.LATER = own("LATER", [P, P], BF16)
            k.SEL = own("SEL", [96, TURNS * MH, T], BF16)
            k.CUMT = own("CUMT", [96, SLOTS, TT, P], BF16)
            k.NCUMT = own("NCUMT", [96, SLOTS, TT, P], BF16)
            k.DT = own("DT", [P, NT, MH])
            k.AT = own("AT", [P, P])
            k.VV = own("VV", [P, 2 * D])
            staged(nc, "prepare", lambda sb, sem: prepare(nc, sb, ps, sem, dram, k))
            staged(nc, "mamba", lambda sb, sem: mamba(nc, sb, ps, sem, k))
        k.LOG = sb("LOG", [P, NE, NT])
        k.GATE = sb("GATE", [P, 2, NT])
        k.POS = sb("POS", [P, 2, NT], U32)
        k.TEX = sb("TEX", [1, 2, TILES], mybir.dt.int32)
        for layer in range(2):
            if stages < (2, 3)[layer]:
                break
            choices = layer + 1
            if layer == 1:
                attention_stage(nc, ps, dram, k)
                if stages == 3:
                    break
            with ExitStack() as inner:
                k.XF = inner.enter_context(nc.sbuf_tensor(f"XF{layer}", [P, NT, D], F32))
                k.ACC = inner.enter_context(nc.sbuf_tensor(f"ACC{layer}", [P, NT, D], F32))
                staged(nc, f"ffn_tokens{layer}", lambda sb, sem: ffn_tokens(nc, sb, ps, sem, k, layer))
                staged(nc, f"route{layer}", lambda sb, sem: route(nc, sb, ps, sem, k, layer, choices))
                staged(nc, f"experts{layer}", lambda sb, sem: experts(nc, sb, ps, sem, dram, k, layer, choices))
        s_out = sem("stored")
        with nc.Block() as block:
            @block.sync
            def _(sp):
                sp.dma_start(dram["out"].rearrange("b (t p) d -> p (b t) d", p=P), k.X[:]).then_inc(s_out, 16)
                sp.wait_ge(s_out, 16)


def constants(np):
    i, j = np.arange(P)[:, None], np.arange(P)[None]
    c = np.zeros((P, CONST_W), np.float32)

    def put(name, value):
        a, z = CONST[name]
        c[:value.shape[0], a:z] = value

    put("ident", np.eye(P))
    put("tri", (i <= j) * 1.0)
    put("ones", np.ones((P, P)))
    put("ones2", np.ones((P, NE * NT)))
    put("ahead", (i < j) * 1.0)
    put("eight", np.tile(NE - np.arange(NE), (P, 1)))
    put("m128", np.tile(P * np.arange(NT), (P, 1)))
    put("tile", np.tile(np.arange(TILES), (P, 1)))
    put("later", (j < i) * -BIG)
    put("earlier", np.concatenate([(np.arange(T)[None] < i + P * t) * 1.0 for t in range(TT)], 1))
    put("slot", np.tile(np.arange(POOL), (P, 1)))
    r = np.arange(TURNS * 12)[:, None]
    put("sel", ((r // 12 == np.arange(TURNS * MH)[None] // MH) & (r % MH == np.arange(TURNS * MH)[None] % MH)) * 1.0)
    return c


def mamba_weights(np, g):
    def pad(a):
        return np.concatenate([a, np.zeros((P - a.shape[0], a.shape[1]), np.float32)]) if a.shape[0] < P else a

    w, f = {}, lambda n: np.asarray(g["L0_attn_" + n])
    w["inw"], w["dtw"] = f("in_w")[:768].T, f("in_w")[768:].T
    w["normw"] = f("norm_w")[:, None]
    w["convw"] = f("conv_w").reshape(4, P, TAPS).transpose(1, 0, 2).reshape(P, 16)
    w["convb"] = f("conv_b").reshape(4, P).T
    w["dtb"], w["alog"] = np.tile(f("dt_bias"), (P, 1)), np.tile(f("A_log"), (P, 1))
    w["dpar"] = np.repeat(f("D_param"), MP).reshape(2, P).T
    w["gnorm"] = f("gnorm_w").reshape(2, P).T
    w["outw"] = f("out_w").T.reshape(2, P, D).transpose(1, 0, 2).reshape(P, 2 * D)
    w["tapbc"] = np.broadcast_to(f("conv_w").reshape(4 * P, TAPS)[2 * P:].T.reshape(1, -1), (P, TAPS * 2 * P))
    w["w1"], w["w2"] = f("scorer_w1").T, f("scorer_w2").T
    w["summ"], w["qw"], w["kwt"], w["vwt"] = f("summ_w"), f("q_w"), f("k_w").T, f("v_w").T
    w["g1"], w["g2"] = f("gate_w")[:, :D].T, f("gate_w")[:, D:].T
    return np.ascontiguousarray(np.concatenate([pad(w[n]) for n in WA], 1))


def expert_weights(np, g):
    f = lambda n: np.asarray(g[n])
    g0 = np.concatenate([f("L0_ffn_gate_w"), f("L0_ffn_sh_gate")[None]])
    u0 = np.concatenate([f("L0_ffn_up_w"), f("L0_ffn_sh_up")[None]])
    d0 = np.concatenate([f("L0_ffn_down_w"), f("L0_ffn_sh_down")[None]])
    g1 = np.concatenate([f("L1_ffn_w_in_eDF"), f("L1_ffn_w_in_shared_FD").T[None]])
    u1 = np.concatenate([f("L1_ffn_w_swiglu_eDF"), f("L1_ffn_w_swiglu_FD").T[None]])
    d1 = np.concatenate([f("L1_ffn_w_out_eFD"), f("L1_ffn_w_out_shared_DF").T[None]])
    w1 = [np.concatenate([a, b], 2).transpose(1, 0, 2) for a, b in ((g0, u0), (g1, u1))]
    wd = [d.reshape(NE + 1, 2, P, D).transpose(2, 0, 1, 3).reshape(P, -1) for d in (d0, d1)]
    wf = np.concatenate([f("L0_ffn_router_w"), f("L1_ffn_router_DE"), np.tile(f("L0_ffn_ln_w"), (P, 1)),
                         np.tile(f("L0_ffn_ln_b"), (P, 1))], 1)
    return tuple(np.ascontiguousarray(a) for a in (np.stack(w1), np.stack(wd), wf))


def attention_constants(np, bf16):
    f32 = np.float32
    slope = np.array([2.0 ** (-0.5 * (h + 1)) for h in range(AH)]).astype(f32)
    s1 = slope.astype(bf16).astype(f32)
    s2 = (slope - s1).astype(bf16).astype(f32)
    s3 = slope - s1 - s2
    parts = np.stack([s1, s2, s3])
    at = np.arange(T, dtype=f32)
    last, first = (at >= P).astype(f32), (at < P).astype(f32)
    q = np.zeros((P, AH // 2, 2, T), f32)
    kk = np.zeros((P, AH // 2, T), f32)
    for h in range(AH):
        r = HROWS * (h % 2) + AD * len(PAIRS)
        for a in range(3):
            q[r + a, h // 2, h % 2], kk[r + a, h // 2] = -at * last, parts[a, h] * first
            q[r + 3 + a, h // 2, h % 2], kk[r + 3 + a, h // 2] = parts[a, h] * last, at * first
    kk[MROW:MROW + 3] = 1.0
    si = np.zeros((P, AH // 2 * 4, P), f32)
    for h in range(AH):
        for a in range(alibi_parts(h)):
            si[:, alibi_at(h) + a] = np.eye(P) * parts[a, h]
    i, j = np.arange(P)[:, None], np.arange(P)[None]
    ramps = np.stack([np.minimum(i - j, 0), np.minimum(j - i, 0)], 1)
    return {"qrows": q.astype(bf16), "krows": kk.astype(bf16), "slopes": si.astype(bf16), "ramps": ramps.astype(bf16)}


def attention_weights(np, g):
    f = lambda n: np.asarray(g["L1_attn_" + n])
    order = np.arange(D).reshape(AH // 2, 2, AD).transpose(1, 2, 0).reshape(-1)
    w, b = f("W_qkv"), f("b_qkv")
    out = {"wqkv": np.concatenate([w[:, order], w[:, D + order], w[:, 2 * D:]], 1),
           "bqk": np.stack([b[order], b[D + order]], 1), "bv": np.tile(b[2 * D:], (P, 1)),
           "wproj": np.concatenate([f("W_proj"), np.tile(f("b_proj"), (P, 1))], 1)}
    return {n: np.ascontiguousarray(a) for n, a in out.items()}


def kernel(**inputs):
    import numpy as _np
    import concourse.bacc as _bacc
    from concourse import mybir as _mybir
    from concourse.bass_utils import run_bass_kernel_spmd as _run

    w1, wd, wf = expert_weights(_np, inputs)
    import ml_dtypes
    bf16 = ml_dtypes.bfloat16
    arrays = {"w1": w1, "wd": wd, "wf": wf, "x": _np.ascontiguousarray(inputs["L0_attn_x"]), "const": constants(_np), "wa": mamba_weights(_np, inputs)}
    arrays.update(attention_constants(_np, bf16))
    arrays.update(attention_weights(_np, inputs))
    nc = _bacc.Bacc("TRN2", target_bir_lowering=False, num_devices=1)
    dram = {n: nc.dram_tensor(n, a.shape, _mybir.dt.from_np(a.dtype), kind="ExternalInput").ap() for n, a in arrays.items()}
    for n in ("sorted", "expert_out"):
        dram[n] = [nc.dram_tensor(f"{n}{c}", (TILES * P, D), _mybir.dt.float32).ap() for c in range(2)]
    dram["out"] = nc.dram_tensor("out", (B, T, D), _mybir.dt.float32, kind="ExternalOutput").ap()
    build(nc, dram)
    r = _run(nc, [arrays], core_ids=[0])
    return r.results[0]["out"]
```

```python
import numpy as np
import concourse.bass as bass
from concourse import mybir
from contextlib import ExitStack

F32 = mybir.dt.float32
BF16 = mybir.dt.bfloat16
F16 = mybir.dt.float16
ALU = mybir.AluOpType
ACT = mybir.ActivationFunctionType
AX_X = mybir.AxisListType.X

P = 128
B, T, D = 16, 256, 128
NT = B * T // P
TT = T // P
EPS = 1e-5
MH, MP = 4, 64
DI = MH * MP
TAPS = 4
POOL = 50
SLOTS = 2
TURNS = B // SLOTS
UNITS = B * T // 512
NE = 8
FF = 256
TILES = 40
BIG = 1.0e30
U32 = mybir.dt.uint32


def columns(table):
    at, out = 0, {}
    for name, width in table:
        out[name] = (at, at + width)
        at += width
    return out, at


CONST, CONST_W = columns([("ident", P), ("tri", P), ("ones", P), ("later", P), ("earlier", TT * T),
                          ("ones2", NE * NT), ("ahead", P), ("eight", NE), ("m128", NT), ("tile", TILES), ("octal", TILES), ("slot", POOL), ("sel", TURNS * MH)])
WA, WA_W = columns([("inw", 768), ("dtw", MH), ("normw", 1), ("convw", 16), ("convb", 4), ("dtb", MH),
                    ("alog", MH), ("dpar", 2), ("gnorm", 2), ("outw", 2 * D), ("w1", 32), ("w2", 1), ("tapbc", 4 * 2 * P), ("summ", D),
                    ("qw", D), ("kwt", 64), ("vwt", D), ("g1", D), ("g2", D)])
WF, WF_W = columns([("router0", NE), ("router1", NE), ("lnw", D), ("lnb", D)])


class Links:

    def __init__(self, engine, sem, total=0, turn=0):
        self.engine, self.sem, self.base, self.total, self.n = engine, sem, turn * total, total, 0

    def __call__(self, ins):
        self.n += 1
        ins.then_inc(self.sem, 1)
        self.engine.wait_ge(self.sem, self.base + self.n)

    def start(self, turn):
        self.base, self.n = turn * self.total, 0

    def close(self, empty=False):
        assert self.n == (0 if empty else self.total), f"links in the body: {self.n}, not {self.total}"


class Kept:

    def c(self, name):
        a, z = CONST[name]
        return self.C[:, a:z]

    def w(self, name):
        a, z = WA[name]
        return self.W[:, a:z]

    def cf(self, name):
        a, z = WF[name]
        return self.F[:, a:z]


def alone(engine):
    engine.nop(nofuse=True)


def spread(ap, n):
    return ap.unsqueeze(2).broadcast_to((ap.shape[0], ap.shape[1], n))


def prepare(nc, sb, ps, sem, dram, k):
    XN4 = sb("XN4", [P, 4, 4, D])
    XNS = sb("XNS", [P, 4, 4 * P])
    SQ = sb("SQ", [P, NT // 2, D])
    MS = sb("MS", [P, NT])
    RS = sb("RS", [P, NT])
    MK = sb("MK", [64, D])
    VWT = sb("VWT", [P, D])
    DTR, RAW, E, U, DLT, LNU, LA = (sb(n, [P, NT, MH]) for n in ("DTR", "RAW", "E", "U", "DLT", "LNU", "LA"))
    LA2 = sb("LA2", [P, TT, B, MH])
    CUM = sb("CUM", [P, TT, B * MH])
    PARTS = sb("PARTS", [P, SLOTS, TT, 96], BF16)
    IDB = k.IDB
    psb = ps[:].bitcast(BF16)

    s_c, s_wa = sem("const_loaded"), sem("wa_loaded")
    s_x = [sem(f"x_loaded{half}") for half in range(2)]
    s_pow, s_zt, s_f = sem("power_set"), sem("zero_tile"), sem("zeros_stored")
    Z = sb("Z", [P, TILES * D // 4])
    s_idb = sem("bf16_consts")
    s_mk, s_mkc = sem("mk"), sem("mk_copied")
    s_prod, s_prodc = sem("products"), sem("products_copied")
    s_link = sem("dve_links")
    lanes, turns = range(4), UNITS // 4
    s_ms, s_rs = sem("mean_square"), sem("rstd")
    s_xn = [sem(f"xn{p}") for p in lanes]
    s_tr = [sem(f"xn_transposed{p}") for p in lanes]
    s_ev = [sem(f"xn_evacuated{p}") for p in lanes]
    s_cp = [sem(f"xn_kept{p}") for p in lanes]
    s_dt = [sem(f"dt_raw{p}") for p in lanes]
    s_dtc = [sem(f"dt_copied{p}") for p in lanes]
    s_sp = sem("softplus_act")
    s_abs = sem("abs_done")
    s_spd = sem("softplus_dve")
    s_cum = sem("cumulated")
    s_parts = sem("parts_split")
    s_cumt = sem("parts_transposed")
    s_done = sem("parts_kept")

    X, C, W = k.X, k.C, k.W
    with nc.Block() as block:
        @block.sync
        def _(sp):
            sp.dma_start(C[:], dram["const"]).then_inc(s_c, 16)
            sp.dma_start(X[:, 0:16], dram["x"][0:8].rearrange("b (t p) d -> p (b t) d", p=P)).then_inc(s_x[0], 16)
            sp.dma_start(W[:], dram["wa"]).then_inc(s_wa, 16)
            sp.dma_start(X[:, 16:32], dram["x"][8:16].rearrange("b (t p) d -> p (b t) d", p=P)).then_inc(s_x[1], 16)
            sp.dma_start(k.F[:], dram["wf"]).then_inc(s_f, 16)
            load_experts(sp, dram, k, 0)
            sp.wait_ge(s_zt, 1)
            for c in range(2):
                for q in range(4):
                    rows = TILES * P // 4
                    sp.dma_start(dram["sorted"][c][rows * q:rows * q + rows, :].rearrange("(p a) d -> p (a d)", p=P),
                                 Z[:]).then_inc(s_f, 16)
            sp.wait_ge(s_f, 16 * 9)

        @block.gpsimd
        def _(pool):
            nc.gpsimd.memset(Z[:], 0.0).then_inc(s_zt, 1)
            nc.gpsimd.memset(k.POWER[:], -0.5).then_inc(s_pow, 1)
            pool.wait_ge(s_pow, 1)
            for half in range(2):
                pool.wait_ge(s_ms, half + 1)
                nc.gpsimd.tensor_tensor(RS[:, 16 * half:16 * half + 16], MS[:, 16 * half:16 * half + 16],
                                        k.POWER[:], ALU.pow).then_inc(s_rs, 1)
            ahead(pool, s_cp)
            with pool.Fori(0, turns) as j:
                for p in lanes:
                    pool.wait_ge(s_ev[p], j + 2)
                    nc.gpsimd.tensor_copy(k.XNT[:, bass.ds((turns * p + j) * 512, 512)], XNS[:, p]).then_inc(s_cp[p], 1)

        @block.vector
        def _(dve):
            link = Links(dve, s_link)
            dve.wait_ge(s_c, 16)
            nc.vector.tensor_copy(IDB[:], k.c("ident"))
            nc.vector.tensor_copy(k.LATER[:], k.c("later"))
            link(nc.vector.tensor_copy(k.SEL[:], k.c("sel")[0:96].unsqueeze(2).broadcast_to((96, TURNS * MH, T))))

            def mean_squares(half):
                dve.wait_ge(s_x[half], 16)
                xs = X[:, 16 * half:16 * half + 16]
                ms = MS[:, 16 * half:16 * half + 16]
                link(nc.vector.tensor_tensor(SQ[:], xs, xs, ALU.mult))
                link(nc.vector.tensor_reduce(ms, SQ[:], AX_X, ALU.add))
                nc.vector.tensor_scalar(ms, ms, 1.0 / D, EPS, ALU.mult, ALU.add).then_inc(s_ms, 1)

            mean_squares(0)
            dve.wait_ge(s_wa, 16)
            nc.vector.tensor_scalar(k.w("inw")[:, 0:DI], k.w("inw")[:, 0:DI], 0.5, None, ALU.mult)
            nc.vector.tensor_scalar(k.w("convw"), k.w("convw"), 0.5, None, ALU.mult)
            nc.vector.tensor_scalar(k.w("convb"), k.w("convb"), 0.5, None, ALU.mult)
            for tap in range(TAPS):
                w = k.w("tapbc")[:, 2 * P * tap:2 * P * tap + 2 * P]
                nc.vector.scalar_tensor_tensor(w, w, 0.5, k.w("inw")[:, 4 * P:6 * P], ALU.mult, ALU.mult)
            for ct in range(2):
                o = k.w("outw")[:, ct * D:(ct + 1) * D]
                last = nc.vector.tensor_scalar(o, o, k.w("gnorm")[:, ct:ct + 1], None, ALU.mult)
            link(last)
            mean_squares(1)
            dve.wait_ge(s_mk, 1)
            nc.vector.tensor_copy(MK[:], ps[0:64, 1024:1152]).then_inc(s_mkc, 1)
            nc.vector.tensor_copy(VWT[:], ps[:, 1536:1664]).then_inc(s_mkc, 1)
            dve.wait_ge(s_prod, 1)
            nc.vector.tensor_copy(k.AT[:], ps[:, 2048:2176])
            link(nc.vector.tensor_copy(k.VV[:], ps[:, 2560:2816]))
            dve.wait_ge(s_rs, 2)
            ahead(dve, s_xn + s_dtc)
            with dve.Fori(0, turns) as j:
                for p in lanes:
                    at = bass.ds((turns * p + j) * 4, 4)
                    dve.wait_ge(s_tr[p], j + 1)
                    nc.vector.tensor_tensor(XN4[:, p], X[:, at, :], spread(RS[:, at], D), ALU.mult).then_inc(s_xn[p], 1)
                for p in lanes:
                    dve.wait_ge(s_dt[p], j + 2)
                    nc.vector.tensor_copy(DTR[:, bass.ds((turns * p + j) * 4, 4), :],
                                          ps[:, 2048 + 512 * p:2064 + 512 * p].rearrange("p (t h) -> p t h", h=MH)
                                          ).then_inc(s_dtc[p], 1)
            for p in lanes:
                dve.wait_ge(s_dtc[p], turns + 1)
            nc.vector.tensor_tensor(RAW[:], DTR[:], k.w("dtb").unsqueeze(1).broadcast_to((P, NT, MH)),
                                    ALU.add).then_inc(s_spd, 1)
            dve.wait_ge(s_sp, 2)
            nc.vector.tensor_scalar(U[:], E[:], 1.0, None, ALU.add).then_inc(s_spd, 1)
            dve.wait_ge(s_spd, 2)
            link(nc.vector.tensor_scalar(DLT[:], U[:], 1.0, None, ALU.subtract))
            link(nc.vector.tensor_tensor(DLT[:], E[:], DLT[:], ALU.subtract))
            link(nc.vector.reciprocal(E[:], U[:]))
            link(nc.vector.tensor_tensor(DLT[:], DLT[:], E[:], ALU.mult))
            link(nc.vector.scalar_tensor_tensor(DLT[:], RAW[:], 0.0, DLT[:], ALU.max, ALU.add))
            dve.wait_ge(s_sp, 3)
            link(nc.vector.tensor_tensor(k.DT[:], DLT[:], LNU[:], ALU.add))
            link(nc.vector.scalar_tensor_tensor(LA[:], k.DT[:], -1.0,
                                                k.w("alog").unsqueeze(1).broadcast_to((P, NT, MH)),
                                                ALU.mult, ALU.mult))
            nc.vector.tensor_copy(LA2[:], LA[:].rearrange("p (b t) h -> p t b h", t=TT)).then_inc(s_spd, 1)
            dve.wait_ge(s_cum, 1)
            link(nc.vector.tensor_copy(CUM[:], ps[:, 0:TT * B * MH].rearrange("p (t c) -> p t c", t=TT)))
            for part in range(3):
                for t in range(TT):
                    for h2 in range(SLOTS):
                        last = nc.vector.tensor_copy(
                            PARTS[:, h2, t].rearrange("p (b c h) -> p b c h", c=3, h=MH)[:, :, part, :],
                            CUM[:, t, h2 * 32:h2 * 32 + 32].rearrange("p (b h) -> p b h", h=MH))
                if part < 2:
                    link(last)
                    for t in range(TT):
                        for h2 in range(SLOTS):
                            c = CUM[:, t, h2 * 32:h2 * 32 + 32].rearrange("p (b h) -> p b h", h=MH)
                            last = nc.vector.tensor_tensor(
                                c, c, PARTS[:, h2, t].rearrange("p (b c h) -> p b c h", c=3, h=MH)[:, :, part, :],
                                ALU.subtract)
                    link(last)
                else:
                    last.then_inc(s_parts, 1)
            dve.wait_ge(s_cumt, 1)
            for h2 in range(SLOTS):
                o = psb[0:96, h2 * 1024:h2 * 1024 + TT * P].rearrange("p (t c) -> p t c", t=TT)
                nc.vector.tensor_copy(k.CUMT[:, h2], o)
                last = nc.vector.tensor_scalar(k.NCUMT[:, h2], o, -1.0, None, ALU.mult)
            last.then_inc(s_done, 1)
            dve.wait_ge(s_done, 1)

        @block.scalar
        def _(act):
            ahead(act, s_ev)
            with act.Fori(0, turns) as j:
                for p in lanes:
                    act.wait_ge(s_tr[p], j + 2)
                    act.wait_ge(s_cp[p], j + 1)
                    act.wait_ge(s_dt[p], j + 1)
                    nc.scalar.activation(XNS[:, p], ps[:, 512 * p:512 * p + 512], ACT.Copy,
                                         scale=k.w("normw")).then_inc(s_ev[p], 1)
            act.wait_ge(s_wa, 16)
            act.wait_ge(s_spd, 1)
            nc.scalar.activation(k.w("alog"), k.w("alog"), ACT.Exp).then_inc(s_sp, 1)
            nc.scalar.activation(E[:], RAW[:], ACT.Abs).then_inc(s_abs, 1)
            act.wait_ge(s_abs, 1)
            nc.scalar.activation(E[:], E[:], ACT.Exp, scale=-1.0).then_inc(s_sp, 1)
            act.wait_ge(s_spd, 2)
            nc.scalar.activation(LNU[:], U[:], ACT.Ln).then_inc(s_sp, 1)

        @block.tensor
        def _(pe):
            pe.wait_ge(s_c, 16)
            pe.wait_ge(s_wa, 16)
            pe.wait_ge(s_link, 4)
            nc.tensor.matmul(ps[0:64, 1024:1152], k.w("kwt")[0:64], k.w("summ")[0:64], start=True, stop=True)
            nc.tensor.matmul(ps[:, 1536:1664], k.w("vwt")[0:64], k.w("summ")[0:64], start=True,
                             stop=True).then_inc(s_mk, 1)
            pe.wait_ge(s_mkc, 2)
            nc.tensor.matmul(ps[:, 2048:2176], MK[:], k.w("qw")[0:64], start=True, stop=True)
            nc.tensor.matmul(ps[:, 2560:2688], k.w("summ")[0:64], k.w("vwt")[0:64], start=True, stop=True)
            nc.tensor.matmul(ps[:, 2688:2816], VWT[:], k.w("g2"), start=True, stop=True).then_inc(s_prod, 1)
            ahead(pe, s_tr + s_dt)
            with pe.Fori(0, turns) as j:
                for p in lanes:
                    pe.wait_ge(s_xn[p], j + 2)
                    pe.wait_ge(s_ev[p], j + 1)
                    for t in range(4):
                        last = nc.tensor.transpose(ps[:, 512 * p + 128 * t:512 * p + 128 * t + 128], XN4[:, p, t, :],
                                                   k.c("ident"))
                    last.then_inc(s_tr[p], 1)
                for p in lanes:
                    pe.wait_ge(s_ev[p], j + 2)
                    pe.wait_ge(s_dtc[p], j + 1)
                    for t in range(4):
                        last = nc.tensor.matmul(ps[:, 2048 + 512 * p + 4 * t:2052 + 512 * p + 4 * t],
                                                XNS[:, p, P * t:P * t + P], k.w("dtw"), start=True, stop=True)
                    last.then_inc(s_dt[p], 1)
            pe.wait_ge(s_spd, 3)
            nc.tensor.matmul(ps[:, 0:64], k.c("tri"), LA2[:, 0], start=True, stop=True)
            nc.tensor.matmul(ps[:, 64:128], k.c("tri"), LA2[:, 1], start=True, stop=False)
            nc.tensor.matmul(ps[:, 64:128], k.c("ones"), LA2[:, 0], start=False, stop=True).then_inc(s_cum, 1)
            pe.wait_ge(s_parts, 1)
            for h2 in range(SLOTS):
                for t in range(TT):
                    last = nc.tensor.transpose(psb[0:96, h2 * 1024 + t * P:h2 * 1024 + t * P + P], PARTS[:, h2, t],
                                               IDB[:])
            last.then_inc(s_cumt, 1)


FIRST_HALF = ("""in_proj tanh_z silu_z conv_in conv tanh_x silu_x tanh_bc silu_bc x_tokens dt_x b_c decay_a exp_a decay_b
    exp_b mix scan gated_y squares""").split()
ORDER = ("""in_proj0 out_proj0 tanh_z0 out_proj1 silu_z0 mean_square0 mean_square1 in_proj1 power0 scaled_y0 power1
    scaled_y1 y_turn0 y_turn1 tanh_z1 silu_z1 conv_in0 conv_in1 yt0 yt1 hidden1 hidden0 relu1 relu0 x2_y1 conv0
    x2_y0 tanh_x0 score1 conv1 score0 tanh_bc0 scores1 scores0 silu_x0 tanh_x1 tanh_bc1 silu_x1 silu_bc0 silu_bc1
    score_turn1 x_tokens0 dt_x0 x_tokens1 dt_x1 score_turn0 b_c0 ranks0 ranks1 decay_a0 select0 empty0 b_c1
    decay_a1 select1 keys_values0 empty1 kv0 keys_values1 logits0 exp_a0 less_max0 kv1 logits1 decay_b0 exp_a1
    exps0 less_max1 probs0 probs_turn0 exps1 exp_b0 prt0 decay_b1 probs1 exp_b1 probs_turn1 retrieve0 prt1 mix0
    scan0 tanh_gate0 mix1 scan1 gate0 retrieve1 tanh_gate1 gated_y0 gated_y1 stats0 squares0 gate1 stats1
    squares1 ln_power0 normed0 ln_power1 normed1""").split()


def mamba(nc, sb, ps, sem, k):
    PAD = TAPS - 1
    CB = sb("CB", [P, SLOTS, 2, PAD + T])
    TH = sb("TH", [P, SLOTS, 4 * T])
    ZZ = sb("ZZ", [P, SLOTS, 2 * T])
    CV = sb("CV", [P, SLOTS, 4, T])
    XS = sb("XS", [P, SLOTS, 4, T])
    EX = sb("EX", [P, SLOTS, MH, T + P])
    DTX = sb("DTX", [P, SLOTS, TT * MH, MP])
    YG = sb("YG", [P, SLOTS, 2, T])
    YSQ = sb("YSQ", [P, SLOTS, 2, T])
    MS = sb("MSY", [P, SLOTS, TT])
    RS = sb("RSY", [P, SLOTS, TT])
    YO = sb("YO", [P, SLOTS, TT, D])
    YT = sb("YT", [P, SLOTS, T])
    HT = sb("HT", [32, SLOTS, T])
    W2 = sb("W2", [32, P])
    SC = sb("SC", [P, SLOTS, T])
    SCC = sb("SCC", [P, SLOTS, TT])
    MEAN = sb("MEAN", [P, SLOTS])
    JUNK = sb("JUNK", [P, SLOTS, TT, T])
    JUNK2 = sb("JUNK2", [P, SLOTS, TT, T])
    RANK = sb("RANK", [P, SLOTS, 2 * TT])
    HIGH = sb("HIGH", [P, SLOTS, TT])
    PICK = sb("PICK", [P, SLOTS, TT, POOL])
    YSEL = sb("YSEL", [P, SLOTS, POOL])
    EMPTY = sb("EMPTY", [1, SLOTS, POOL])
    KA = sb("KA", [P, SLOTS, POOL])
    VSEL = sb("VSEL", [P, SLOTS, 2 * D])
    LG = sb("LG", [P, SLOTS, TT, POOL])
    MX = sb("MX", [P, SLOTS, TT])
    SM = sb("SM", [P, SLOTS, TT])
    PRT = sb("PRT", [P, SLOTS, T])
    TG = sb("TG", [P, SLOTS, TT, D])
    GR = sb("GR", [P, SLOTS, TT, D])
    WX = sb("WX", [P, SLOTS, TT, D])
    BN = sb("BN", [P, SLOTS, TT, 6])
    MV = sb("MV", [P, SLOTS, TT, 2])
    X, C, psb = k.X, k.C, ps[:].bitcast(BF16)

    def two(name):
        return [sem(f"{name}{p}") for p in range(SLOTS)]

    s_zero, s_w2 = sem("zeroed"), sem("w2_spread")
    s_front_link, s_back_link = sem("mamba_front_links"), sem("mamba_back_links")
    s_in, s_inz, s_cb, s_thz, s_zz = two("in_proj"), two("z_proj"), two("conv_in"), two("tanh_z"), two("silu_z")
    s_cvx, s_inbc, s_thx, s_thb, s_xs, s_bc = two("conv_x"), two("bc_psum"), two("tanh_x"), two("tanh_bc"), two("xs"), two("bc")
    s_g, s_xt, s_dec, s_ex, s_m, s_dtx = two("g"), two("x_tokens"), two("decay"), two("decay_exp"), two("m"), two("dtx")
    s_y, s_yd, s_yg, s_sq, s_yo, s_ms, s_rs = two("y"), two("y_d"), two("y_gated"), two("y_sq"), two("y_out"), two("y_ms"), two("y_rs")
    s_yoc, s_ytp, s_yt, s_hp, s_ht, s_zsp, s_tsc = two("yo_kept"), two("yt_psum"), two("yt"), two("h_psum"), two("ht"), two("score_psum"), two("score_tanh")
    s_sc, s_sct, s_pick, s_self, s_ysel, s_kv, s_ka, s_vs = two("scores"), two("scores_turned"), two("picked"), two("sel_psum"), two("ysel"), two("kv_psum"), two("ka"), two("vsel")
    s_lg, s_sub, s_ep, s_pr, s_prt, s_prc = two("logits"), two("logits_less_max"), two("exps"), two("probs"), two("probs_turned"), two("prt")
    s_rg, s_tg, s_gr, s_wx, s_var, s_lrs, s_res = two("retrieved"), two("gate_tanh"), two("gated"), two("x2_y"), two("variance"), two("ln_rstd"), two("x_written")

    def bank(p, n, a=0, z=512):
        return ps[:, (4 * p + n) * 512 + a:(4 * p + n) * 512 + z]

    LINKS_FRONT, LINKS_BACK = SLOTS * 4, SLOTS * 10
    slots = range(SLOTS)

    def halves(engine, mine, front=None, back=None):
        def turn(first, second):
            if front:
                front.start(0 if first is None else first)
                back.start(0 if second is None else second)
            for step in ORDER:
                name, p = step[:-1], int(step[-1])
                j = first if name in FIRST_HALF else second
                if name in mine and j is not None:
                    mine[name](p, j)
            if front:
                front.close(empty=first is None)
                back.close(empty=second is None)

        turn(0, None)
        with engine.Fori(0, TURNS - 1) as j:
            turn(j + 1, j)
        turn(None, TURNS - 1)

    with nc.Block() as block:
        @block.gpsimd
        def _(pool):
            for t in (CB, VSEL, PRT):
                last = nc.gpsimd.memset(t[:], 0.0)
            last.then_inc(s_zero, 1)
            def power(p, j):
                n = j + 1
                pool.wait_ge(s_ms[p], j + 1)
                nc.gpsimd.tensor_tensor(RS[:, p], MS[:, p], k.POWER[:, 0:TT], ALU.pow).then_inc(s_rs[p], 1)

            def x2_y(p, j):
                n = j + 1
                xs = X[:, bass.ds(16 * p + 2 * j, 2), :]
                pool.wait_ge(s_yoc[p], n)
                pool.wait_ge(s_res[p], n)
                alone(pool)
                nc.gpsimd.tensor_tensor(WX[:, p], xs, YO[:, p], ALU.add).then_inc(s_wx[p], 1)
                pool.wait_ge(s_wx[p], 2 * n - 1)
                alone(pool)
                nc.gpsimd.tensor_tensor(WX[:, p], WX[:, p], xs, ALU.add).then_inc(s_wx[p], 1)

            def ln_power(p, j):
                n = j + 1
                pool.wait_ge(s_var[p], j + 1)
                nc.gpsimd.tensor_tensor(MV[:, p, :, 1:2], MV[:, p, :, 1:2],
                                        k.POWER[:, 0:TT].unsqueeze(2), ALU.pow).then_inc(s_lrs[p], 1)

            halves(pool, {"power": power, "x2_y": x2_y, "ln_power": ln_power})

        @block.vector
        def _(dve):
            dve.wait_ge(s_zero, 1)
            nc.vector.tensor_copy(W2[:], k.w("w2")[0:32].broadcast_to((32, P))).then_inc(s_w2, 1)
            front, back = Links(dve, s_front_link, LINKS_FRONT), Links(dve, s_back_link, LINKS_BACK)
            ahead(dve, s_gr + s_yg + s_res)
            def silu_z(p, j):
                n = j + 1
                dve.wait_ge(s_thz[p], n)
                nc.vector.scalar_tensor_tensor(ZZ[:, p], TH[:, p, 0:2 * T], 1.0, bank(p, 2), ALU.add,
                                               ALU.mult).then_inc(s_zz[p], 1)

            def conv(p, j):
                n = j + 1
                dve.wait_ge(s_cb[p], n)
                for ct in (0, 1):
                    w, b = k.w("convw")[:, 4 * ct:4 * ct + 4], k.w("convb")[:, ct:ct + 1]
                    last = nc.vector.tensor_scalar(CV[:, p, ct], CB[:, p, ct, 0:T], w[:, 0:1], b, ALU.mult, ALU.add)
                front(last)
                for tap in range(1, TAPS):
                    for ct in (0, 1):
                        w = k.w("convw")[:, 4 * ct + tap:4 * ct + tap + 1]
                        last = nc.vector.scalar_tensor_tensor(CV[:, p, ct], CB[:, p, ct, tap:tap + T], w,
                                                              CV[:, p, ct], ALU.mult, ALU.add)
                    if tap < TAPS - 1:
                        front(last)
                last.then_inc(s_cvx[p], 1)

            def silu_x(p, j):
                n = j + 1
                dve.wait_ge(s_thx[p], n)
                nc.vector.scalar_tensor_tensor(XS[:, p, 0:2], TH[:, p, 0:2 * T].rearrange("p (c t) -> p c t", t=T), 1.0,
                                               CV[:, p, 0:2], ALU.add, ALU.mult).then_inc(s_xs[p], 1)

            def silu_bc(p, j):
                n = j + 1
                dve.wait_ge(s_thb[p], n)
                nc.vector.scalar_tensor_tensor(XS[:, p, 2:4], TH[:, p, 2 * T:4 * T].rearrange("p (c t) -> p c t", t=T), 1.0,
                                               CV[:, p, 2:4], ALU.add, ALU.mult).then_inc(s_bc[p], 1)

            def dt_x(p, j):
                n = j + 1
                dve.wait_ge(s_xt[p], n)
                nc.vector.tensor_tensor(DTX[:, p], bank(p, 0).rearrange("p (a b) -> p a b", b=MP),
                                        spread(k.DT[:, bass.ds(16 * p + 2 * j, 2), :].rearrange("p t h -> p (t h)"), MP),
                                        ALU.mult).then_inc(s_dtx[p], 1)

            def mix(p, j):
                n = j + 1
                dve.wait_ge(s_ex[p], 2 * n)
                dve.wait_ge(s_g[p], n)
                nc.vector.tensor_tensor(EX[:, p], EX[:, p], bank(p, 2, 0, T + P).unsqueeze(1).broadcast_to((P, MH, T + P)),
                                        ALU.mult).then_inc(s_m[p], 1)

            def gated_y(p, j):
                n = j + 1
                dve.wait_ge(s_y[p], n)
                for ct in range(2):
                    last = nc.vector.scalar_tensor_tensor(YG[:, p, ct], XS[:, p, ct], k.w("dpar")[:, ct:ct + 1],
                                                          bank(p, 0, ct * T, ct * T + T), ALU.mult, ALU.add)
                front(last)
                nc.vector.tensor_tensor(YG[:, p], YG[:, p], ZZ[:, p].rearrange("p (c t) -> p c t", t=T),
                                        ALU.mult).then_inc(s_yg[p], 1)

            def mean_square(p, j):
                n = j + 1
                dve.wait_ge(s_yo[p], n)
                nc.vector.tensor_scalar(MS[:, p], bank(p, 3, T, T + TT), 1.0 / DI, EPS, ALU.mult,
                                        ALU.add).then_inc(s_ms[p], 1)

            def scaled_y(p, j):
                n = j + 1
                dve.wait_ge(s_rs[p], n)
                nc.vector.tensor_tensor(YO[:, p], bank(p, 3, 0, T).rearrange("p (t d) -> p t d", d=D),
                                        spread(RS[:, p], D), ALU.mult).then_inc(s_yoc[p], 1)

            def scores(p, j):
                n = j + 1
                dve.wait_ge(s_tsc[p], n)
                nc.vector.tensor_scalar(SC[:, p], SC[:, p], 0.5, 0.5, ALU.mult, ALU.add).then_inc(s_sc[p], 1)
                dve.wait_ge(s_sc[p], n)
                back(nc.vector.tensor_reduce(MEAN[:, p:p + 1], SC[:, p], AX_X, ALU.add))
                nc.vector.tensor_scalar(MEAN[:, p:p + 1], MEAN[:, p:p + 1], 1.0 / T, None, ALU.mult)

            def ranks(p, j):
                n = j + 1
                dve.wait_ge(s_sct[p], n)
                back(nc.vector.tensor_copy(SCC[:, p], bank(p, 3, T, T + TT)))
                nc.vector.tensor_scalar(HIGH[:, p], SCC[:, p], 0.5, None, ALU.is_gt)
                for t in range(TT):
                    nc.vector.tensor_scalar(JUNK[:, p, t], SC[:, p], SCC[:, p, t:t + 1], None, ALU.is_gt, ALU.add,
                                            accum_out=RANK[:, p, t:t + 1])
                    last = nc.vector.scalar_tensor_tensor(JUNK2[:, p, t], SC[:, p], SCC[:, p, t:t + 1],
                                                          k.c("earlier")[:, t * T:t * T + T], ALU.is_equal, ALU.mult,
                                                          accum_out=RANK[:, p, TT + t:TT + t + 1])
                back(last)
                back(nc.vector.tensor_tensor(RANK[:, p, 0:TT], RANK[:, p, 0:TT], RANK[:, p, TT:2 * TT], ALU.add))
                for t in range(TT):
                    last = nc.vector.tensor_scalar(PICK[:, p, t], k.c("slot"), RANK[:, p, t:t + 1],
                                                   HIGH[:, p, t:t + 1], ALU.is_equal, ALU.mult)
                last.then_inc(s_pick[p], 1)

            def empty(p, j):
                n = j + 1
                dve.wait_ge(s_self[p], n)
                nc.vector.tensor_scalar(EMPTY[:, p], bank(p, 3, 64, 64 + POOL)[0:1], 1.0, 4.0e9, ALU.subtract, ALU.mult)
                nc.vector.tensor_copy(YSEL[:, p], bank(p, 3, 0, POOL)).then_inc(s_ysel[p], 1)

            def less_max(p, j):
                n = j + 1
                dve.wait_ge(s_lg[p], n)
                lg = bank(p, 3, 0, TT * POOL).rearrange("p (t s) -> p t s", s=POOL)
                back(nc.vector.tensor_reduce(MX[:, p], lg, AX_X, ALU.max))
                nc.vector.tensor_tensor(LG[:, p], lg, spread(MX[:, p], POOL), ALU.subtract).then_inc(s_sub[p], 1)

            def probs(p, j):
                n = j + 1
                dve.wait_ge(s_ep[p], n)
                back(nc.vector.tensor_reduce(SM[:, p], LG[:, p], AX_X, ALU.add))
                back(nc.vector.reciprocal(SM[:, p], SM[:, p]))
                nc.vector.tensor_tensor(LG[:, p], LG[:, p], spread(SM[:, p], POOL), ALU.mult).then_inc(s_pr[p], 1)

            def gate(p, j):
                n = j + 1
                nc.vector.tensor_scalar(MEAN[:, p:p + 1], MEAN[:, p:p + 1], 0.3, 0.5, ALU.is_gt, ALU.mult)
                dve.wait_ge(s_tg[p], n)
                nc.vector.scalar_tensor_tensor(GR[:, p], TG[:, p], 1.0,
                                               bank(p, 3).rearrange("p (t c) -> p t c", t=TT)[:, :, 0:D],
                                               ALU.add, ALU.mult).then_inc(s_gr[p], 1)
                dve.wait_ge(s_gr[p], n + 1)
                dve.wait_ge(s_wx[p], 2 * n)
                back(nc.vector.scalar_tensor_tensor(WX[:, p], GR[:, p], MEAN[:, p:p + 1], WX[:, p], ALU.mult, ALU.add))

            def stats(p, j):
                n = j + 1
                for t in range(TT):
                    last = nc.vector.bn_stats(BN[:, p, t], WX[:, p, t])
                back(last)
                alone(dve)
                for t in range(TT):
                    last = nc.vector.bn_aggr(MV[:, p, t], BN[:, p, t])
                back(last)
                nc.vector.tensor_scalar(MV[:, p, :, 1:2], MV[:, p, :, 1:2], EPS, None, ALU.add).then_inc(s_var[p], 1)

            def normed(p, j):
                n = j + 1
                dve.wait_ge(s_lrs[p], n)
                for t in range(TT):
                    last = nc.vector.tensor_scalar(X[:, bass.ds(16 * p + 2 * j + t, 1), :].rearrange("p a d -> p (a d)"),
                                                   WX[:, p, t], MV[:, p, t, 0:1], MV[:, p, t, 1:2],
                                                   ALU.subtract, ALU.mult)
                last.then_inc(s_res[p], 1)

            halves(dve, {f.__name__: f for f in (
                silu_z, conv, silu_x, silu_bc, dt_x, mix, gated_y, mean_square, scaled_y, scores, ranks, empty,
                less_max, probs, gate, stats, normed)}, front, back)

        @block.scalar
        def _(act):
            act.wait_ge(s_zero, 1)
            def tanh_z(p, j):
                n = j + 1
                act.wait_ge(s_inz[p], n)
                nc.scalar.activation(TH[:, p, 0:2 * T], bank(p, 2), ACT.Tanh).then_inc(s_thz[p], 1)

            def conv_in(p, j):
                n = j + 1
                act.wait_ge(s_in[p], n)
                nc.scalar.activation(CB[:, p, :, PAD:], bank(p, 0).rearrange("p (c t) -> p c t", t=T),
                                     ACT.Copy).then_inc(s_cb[p], 1)

            def tanh_x(p, j):
                n = j + 1
                act.wait_ge(s_cvx[p], n)
                act.wait_ge(s_zz[p], n)
                nc.scalar.activation(TH[:, p, 0:2 * T].rearrange("p (c t) -> p c t", t=T), CV[:, p, 0:2],
                                     ACT.Tanh).then_inc(s_thx[p], 1)

            def tanh_bc(p, j):
                n = j + 1
                act.wait_ge(s_inbc[p], n)
                for i in range(2):
                    bias = k.w("convb")[:, 2 + i:3 + i]
                    nc.scalar.activation(CV[:, p, 2 + i], bank(p, 1, i * T, i * T + T), ACT.Identity, bias=bias)
                    last = nc.scalar.activation(TH[:, p, 2 * T + i * T:3 * T + i * T], bank(p, 1, i * T, i * T + T),
                                                ACT.Tanh, bias=bias)
                last.then_inc(s_thb[p], 1)

            def decays(i):
                def step(p, j):
                    n = j + 1
                    act.wait_ge(s_dec[p], 2 * j + i + 1)
                    nc.scalar.activation(EX[:, p, 2 * i:2 * i + 2],
                                         ps[:, 2048 * p:2048 * p + 1024].rearrange("p (h c) -> p h c", h=2)[:, :, 0:T + P],
                                         ACT.Exp).then_inc(s_ex[p], 1)
                return step

            def squares(p, j):
                n = j + 1
                act.wait_ge(s_yg[p], n + 1)
                nc.scalar.activation(YSQ[:, p], YG[:, p], ACT.Square).then_inc(s_sq[p], 1)

            def yt(p, j):
                n = j + 1
                act.wait_ge(s_ytp[p], n)
                nc.scalar.activation(YT[:, p], bank(p, 3, 0, T), ACT.Copy).then_inc(s_yt[p], 1)

            def relu(p, j):
                n = j + 1
                act.wait_ge(s_hp[p], n)
                nc.scalar.activation(HT[:, p], bank(p, 3, 0, T)[0:32], ACT.Relu).then_inc(s_ht[p], 1)

            def score(p, j):
                n = j + 1
                act.wait_ge(s_zsp[p], n)
                nc.scalar.activation(SC[:, p], bank(p, 3, 0, T), ACT.Tanh, scale=0.5).then_inc(s_tsc[p], 1)

            def kv(p, j):
                n = j + 1
                act.wait_ge(s_kv[p], n)
                nc.scalar.activation(KA[:, p], bank(p, 3, 256, 256 + POOL), ACT.Copy).then_inc(s_ka[p], 1)
                nc.scalar.activation(VSEL[0:POOL, p], bank(p, 3, 0, 256)[0:POOL], ACT.Copy).then_inc(s_vs[p], 1)

            def exps(p, j):
                n = j + 1
                act.wait_ge(s_sub[p], n)
                nc.scalar.activation(LG[:, p], LG[:, p], ACT.Exp, scale=0.25).then_inc(s_ep[p], 1)

            def prt(p, j):
                n = j + 1
                act.wait_ge(s_prt[p], n)
                nc.scalar.activation(PRT[0:POOL, p], bank(p, 3, 0, T)[0:POOL], ACT.Copy).then_inc(s_prc[p], 1)

            def tanh_gate(p, j):
                n = j + 1
                act.wait_ge(s_rg[p], n)
                nc.scalar.activation(TG[:, p], bank(p, 3).rearrange("p (t c) -> p t c", t=TT)[:, :, D:2 * D],
                                     ACT.Tanh, scale=0.5).then_inc(s_tg[p], 1)

            steps = {f.__name__: f for f in (tanh_z, conv_in, tanh_x, tanh_bc, squares, yt, relu, score, kv, exps,
                                             prt, tanh_gate)}
            halves(act, dict(steps, exp_a=decays(0), exp_b=decays(1)))

        @block.tensor
        def _(pe):
            pe.wait_ge(s_w2, 1)
            def in_proj(p, j):
                n = j + 1
                pe.wait_ge(s_yg[p], n)
                rhs = k.XNT[:, bass.ds((8 * p + j) * T, T)]
                for i, ct in enumerate((0, 1)):
                    last = nc.tensor.matmul(bank(p, 2, i * T, i * T + T), k.w("inw")[:, ct * P:ct * P + P], rhs,
                                            start=True, stop=True)
                last.then_inc(s_inz[p], 1)
                for i, ct in enumerate((2, 3)):
                    last = nc.tensor.matmul(bank(p, 0, i * T, i * T + T), k.w("inw")[:, ct * P:ct * P + P],
                                            rhs, start=True, stop=True)
                last.then_inc(s_in[p], 1)
                for i in range(2):
                    for back in range(TAPS):
                        w = k.w("tapbc")[:, 2 * P * (TAPS - 1 - back) + i * P:2 * P * (TAPS - 1 - back) + i * P + P]
                        last = nc.tensor.matmul(bank(p, 1, i * T + back, i * T + T), w,
                                                k.XNT[:, bass.ds((8 * p + j) * T, T - back)], start=(back == 0),
                                                stop=(back == TAPS - 1))
                last.then_inc(s_inbc[p], 1)

            def x_tokens(p, j):
                n = j + 1
                pe.wait_ge(s_xs[p], n)
                for t in range(TT):
                    for ct in range(2):
                        last = nc.tensor.transpose(bank(p, 0, (2 * t + ct) * P, (2 * t + ct) * P + P),
                                                   XS[:, p, ct, t * P:t * P + P], k.c("ident"))
                last.then_inc(s_xt[p], 1)

            def b_c(p, j):
                n = j + 1
                pe.wait_ge(s_bc[p], n)
                pe.wait_ge(s_zz[p], n)
                nc.tensor.matmul(bank(p, 2, 0, T), XS[:, p, 2, 0:P], XS[:, p, 3], start=True, stop=True)
                nc.tensor.matmul(bank(p, 2, T, T + P), XS[:, p, 2, P:T], XS[:, p, 3, P:T], start=True,
                                 stop=True).then_inc(s_g[p], 1)

            def decay(i):
                def step(p, j):
                    n = j + 1
                    if i == 0:
                        pe.wait_ge(s_dtx[p], n)
                        pe.wait_ge(s_thb[p], n)
                    else:
                        pe.wait_ge(s_ex[p], 2 * j + 1)
                    for h in (0, 1):
                        one = k.SEL[:, bass.ds(MH * j + 2 * i + h, 1), :].rearrange("p a c -> p (a c)")
                        for s in range(TT):
                            w = T - s * P
                            o = bank(p, h, s * T, s * T + w)
                            nc.tensor.matmul(o, one[:, 0:P], k.CUMT[:, p, s:].rearrange("p t c -> p (t c)"),
                                             start=True, stop=False)
                            nc.tensor.matmul(o, k.NCUMT[:, p, s], one[:, 0:w], start=False, stop=False)
                            last = nc.tensor.matmul(o[:, 0:P], k.IDB[:], k.LATER[:], start=False, stop=True)
                    last.then_inc(s_dec[p], 1)
                return step

            def scan(p, j):
                n = j + 1
                pe.wait_ge(s_m[p], n)
                pe.wait_ge(s_dtx[p], n)
                for h in range(MH):
                    o = bank(p, 0, h // 2 * T, h // 2 * T + T)[MP * (h % 2):MP * (h % 2) + MP]
                    nc.tensor.matmul(o, DTX[:, p, h], EX[:, p, h, 0:T], start=True, stop=False)
                    last = nc.tensor.matmul(o[:, P:T], DTX[:, p, MH + h], EX[:, p, h, T:T + P], start=False, stop=True)
                last.then_inc(s_y[p], 1)

            def out_proj(p, j):
                n = j + 1
                pe.wait_ge(s_sq[p], n)
                pe.wait_ge(s_gr[p], n)
                for t in range(TT):
                    for ct in range(2):
                        nc.tensor.matmul(bank(p, 3, t * D, t * D + D), YG[:, p, ct, t * P:t * P + P],
                                         k.w("outw")[:, ct * D:ct * D + D], start=(ct == 0), stop=(ct == 1))
                for t in range(TT):
                    for ct in range(2):
                        last = nc.tensor.matmul(bank(p, 3, T + t, T + t + 1), YSQ[:, p, ct, t * P:t * P + P],
                                                k.c("ones")[:, 0:1], start=(ct == 0), stop=(ct == 1))
                last.then_inc(s_yo[p], 1)

            def y_turn(p, j):
                n = j + 1
                pe.wait_ge(s_yoc[p], n)
                for t in range(TT):
                    last = nc.tensor.transpose(bank(p, 3, t * P, t * P + P), YO[:, p, t], k.c("ident"))
                last.then_inc(s_ytp[p], 1)

            def hidden(p, j):
                n = j + 1
                pe.wait_ge(s_yt[p], n)
                nc.tensor.matmul(bank(p, 3, 0, T)[0:32], k.w("w1"), YT[:, p], start=True, stop=True).then_inc(s_hp[p], 1)

            def score(p, j):
                n = j + 1
                pe.wait_ge(s_ht[p], n)
                nc.tensor.matmul(bank(p, 3, 0, T), W2[:], HT[:, p], start=True, stop=True).then_inc(s_zsp[p], 1)

            def score_turn(p, j):
                n = j + 1
                pe.wait_ge(s_sc[p], n)
                alone(pe)
                for t in range(TT):
                    last = nc.tensor.transpose(bank(p, 3, T + t, T + t + 1), SC[0:1, p, t * P:t * P + P],
                                               k.c("ident")[0:1, 0:1])
                last.then_inc(s_sct[p], 1)

            def select(p, j):
                n = j + 1
                pe.wait_ge(s_pick[p], n)
                for t in range(TT):
                    nc.tensor.matmul(bank(p, 3, 0, POOL), YO[:, p, t], PICK[:, p, t], start=(t == 0), stop=(t == TT - 1))
                for t in range(TT):
                    last = nc.tensor.matmul(bank(p, 3, 64, 64 + POOL)[0:1], k.c("ones")[:, 0:1], PICK[:, p, t],
                                            start=(t == 0), stop=(t == TT - 1))
                last.then_inc(s_self[p], 1)

            def keys_values(p, j):
                n = j + 1
                pe.wait_ge(s_ysel[p], n)
                nc.tensor.matmul(bank(p, 3, 256, 256 + POOL), k.AT[:], YSEL[:, p], start=True, stop=True)
                nc.tensor.matmul(bank(p, 3, 0, 256)[0:POOL], YSEL[:, p], k.VV[:], start=True,
                                 stop=True).then_inc(s_kv[p], 1)

            def logits(p, j):
                n = j + 1
                pe.wait_ge(s_vs[p], n)
                for t in range(TT):
                    o = bank(p, 3, t * POOL, t * POOL + POOL)
                    nc.tensor.matmul(o, YT[:, p, t * P:t * P + P], KA[:, p], start=True, stop=False)
                    last = nc.tensor.matmul(o, k.c("ones")[0:1], EMPTY[:, p], start=False, stop=True)
                last.then_inc(s_lg[p], 1)

            def probs_turn(p, j):
                n = j + 1
                pe.wait_ge(s_pr[p], n)
                alone(pe)
                for t in range(TT):
                    last = nc.tensor.transpose(bank(p, 3, t * P, t * P + P)[0:POOL], LG[:, p, t], k.c("ident"))
                last.then_inc(s_prt[p], 1)

            def retrieve(p, j):
                n = j + 1
                pe.wait_ge(s_prc[p], n)
                for t in range(TT):
                    o = bank(p, 3, t * 2 * D, (t + 1) * 2 * D)
                    nc.tensor.matmul(o, PRT[:, p, t * P:t * P + P], VSEL[:, p], start=True, stop=False)
                    last = nc.tensor.matmul(o[:, D:2 * D], YT[:, p, t * P:t * P + P], k.w("g1"), start=False, stop=True)
                last.then_inc(s_rg[p], 1)

            steps = {f.__name__: f for f in (in_proj, x_tokens, b_c, scan, out_proj, y_turn, hidden, score,
                                             score_turn, select, keys_values, logits, probs_turn, retrieve)}
            halves(pe, dict(steps, decay_a=decay(0), decay_b=decay(1)))


def ahead(engine, sems, by=1):
    for s in sems:
        engine.sem_inc(s, by)


def ffn_tokens(nc, sb, ps, sem, k, layer):
    norm = layer == 0
    X = k.X
    router = k.cf("router0" if norm else "router1")
    L = 4
    BN = sb("BN", [P, 8, 6])
    MV8 = sb("MV8", [P, 8, 2])
    MV = sb("MV", [P, NT, 2])
    XN = sb("XN", [P, L, 4, D])
    XS4 = sb("XS4", [P, L, 4, D])
    XFS = sb("XFS", [P, L, 4 * P])
    lanes, turns = range(L), UNITS // L

    def lane_sems(name):
        return [sem(f"{name}{p}") for p in lanes]

    s_link = sem("links")
    s_var, s_rstd = sem("variance"), sem("rstd")
    s_xf, s_tr, s_ev, s_kept, s_lg, s_lgc = (lane_sems(n) for n in (
        "tokens", "turned", "turned_in_slot", "all_kept", "logits", "logits_kept"))

    def tiles(p, j, t=0, n=4):
        return bass.ds((turns * p + j) * 4 + t, n)

    with nc.Block() as block:
        @block.gpsimd
        def _(pool):
            if norm:
                with pool.Fori(0, NT // 8) as j:
                    pool.wait_ge(s_var, j + 1)
                    v = MV[:, bass.ds(8 * j, 8), 1:2]
                    nc.gpsimd.tensor_tensor(v, v, k.POWER[:, 0:8].unsqueeze(2), ALU.pow).then_inc(s_rstd, 1)

        @block.vector
        def _(dve):
            done = 0
            if norm:
                with dve.Fori(0, NT // 8) as j:
                    link = Links(dve, s_link, 2, j)
                    for t in range(8):
                        last = nc.vector.bn_stats(BN[:, t], X[:, bass.ds(8 * j + t, 1), :].rearrange("p a d -> p (a d)"))
                    link(last)
                    alone(dve)
                    for t in range(8):
                        last = nc.vector.bn_aggr(MV8[:, t], BN[:, t])
                    link(last)
                    at = bass.ds(8 * j, 8)
                    nc.vector.tensor_copy(MV[:, at, 0:1], MV8[:, :, 0:1])
                    nc.vector.tensor_scalar(MV[:, at, 1:2], MV8[:, :, 1:2], EPS, None, ALU.add).then_inc(s_var, 1)
                    link.close()
                done = 2 * (NT // 8)
                dve.wait_ge(s_rstd, NT // 8)
            ahead(dve, s_lgc)
            with dve.Fori(0, turns) as j:
                link = Links(dve, s_link, L if norm else 0, j)
                link.base = link.base + done

                def normed(p):
                    for t in range(4):
                        at = tiles(p, j, t, 1)
                        last = nc.vector.scalar_tensor_tensor(
                            XN[:, p, t], X[:, at, :].rearrange("p a d -> p (a d)"),
                            MV[:, at, 0:1].rearrange("p a c -> p (a c)"), k.cf("lnw"), ALU.subtract, ALU.mult)
                    link(last)
                    dve.wait_ge(s_kept[p], j + 1)
                    for t in range(4):
                        last = nc.vector.scalar_tensor_tensor(
                            XS4[:, p, t], XN[:, p, t], MV[:, tiles(p, j, t, 1), 1:2].rearrange("p a c -> p (a c)"),
                            k.cf("lnb"), ALU.mult, ALU.add)
                    last.then_inc(s_xf[p], 1)

                def logits(p):
                    dve.wait_ge(s_lg[p], j + 1)
                    nc.vector.tensor_copy(k.LOG[:, :, tiles(p, j)],
                                          ps[:, 2048 + 512 * p:2080 + 512 * p].rearrange("p (n e) -> p e n", e=NE)
                                          ).then_inc(s_lgc[p], 1)

                for step in ((normed, logits) if norm else (logits,)):
                    for p in lanes:
                        step(p)
                link.close()

        @block.scalar
        def _(act):
            ahead(act, s_ev)
            ahead(act, s_kept)
            with act.Fori(0, turns) as j:
                if not norm:
                    for p in lanes:
                        act.wait_ge(s_kept[p], j + 1)
                        nc.scalar.activation(XS4[:, p], X[:, tiles(p, j), :], ACT.Copy).then_inc(s_xf[p], 1)
                for p in lanes:
                    act.wait_ge(s_tr[p], j + 1)
                    nc.scalar.activation(XFS[:, p], ps[:, 512 * p:512 * p + 512], ACT.Copy).then_inc(s_ev[p], 1)
                    last = nc.scalar.activation(k.XNT[:, bass.ds((turns * p + j) * 512, 512)],
                                                ps[:, 512 * p:512 * p + 512], ACT.Copy)
                    if norm:
                        last = nc.scalar.activation(k.XF[:, tiles(p, j), :], XS4[:, p], ACT.Copy)
                    last.then_inc(s_kept[p], 1)

        @block.tensor
        def _(pe):
            with pe.Fori(0, turns) as j:
                def logits(p):
                    pe.wait_ge(s_ev[p], j + 2)
                    pe.wait_ge(s_lgc[p], j + 1)
                    for t in range(4):
                        last = nc.tensor.matmul(ps[:, 2048 + 512 * p + NE * t:2048 + 512 * p + NE * t + NE],
                                                XFS[:, p, P * t:P * t + P], router, start=True, stop=True)
                    last.then_inc(s_lg[p], 1)

                for p in lanes:
                    pe.wait_ge(s_xf[p], j + 1)
                    pe.wait_ge(s_kept[p], j + 1)
                    for t in range(4):
                        last = nc.tensor.transpose(ps[:, 512 * p + P * t:512 * p + P * t + P], XS4[:, p, t], k.c("ident"))
                    last.then_inc(s_tr[p], 1)
                    if p:
                        logits(p - 1)
                logits(L - 1)


def route(nc, sb, ps, sem, k, layer, choices):
    OH = [sb(f"OH{c}", [P, NE, NT]) for c in range(choices)]
    EQ = sb("EQ", [P, NE, NT])
    MX = [sb(f"MXR{c}", [P, NT]) for c in range(choices)]
    FI = sb("FI", [P, NT])
    CI = sb("CI", [P, NE, NT])
    ENDS, NTL, START, OFF, ZERO = (sb(n, [P, NE]) for n in ("ENDS", "NTL", "START", "OFF", "ZERO"))
    GT = sb("GT", [P, NE, NT])
    POSF = sb("POSF", [P, NE, NT])
    POS1 = sb("POS1", [P, NT])
    TE = sb("TE", [1, TILES, NE - 1])
    TEF = sb("TEF", [1, TILES])
    TED = sb("TED", [1, TILES // FLOW])
    s_link, s_mx, s_sig, s_oh, s_cnt, s_done = (sem(n) for n in (
        "route_links", "best_logit", "route_tanh", "experts_marked", "counted", "routed"))
    with nc.Block() as block:
        @block.vector
        def _(dve):
            link = Links(dve, s_link)
            link(nc.vector.memset(ZERO[:], 0.0))
            rev = k.c("eight").unsqueeze(2).broadcast_to((P, NE, NT))
            for c in range(choices):
                nc.vector.tensor_reduce(MX[c][:], k.LOG[:].rearrange("p e n -> p n e"), AX_X, ALU.max).then_inc(s_mx, 1)
                dve.wait_ge(s_mx, c + 1)
                best = MX[c][:].unsqueeze(1).broadcast_to((P, NE, NT))
                link(nc.vector.tensor_tensor(EQ[:], k.LOG[:], best, ALU.is_equal))
                link(nc.vector.tensor_tensor(EQ[:], EQ[:], rev, ALU.mult))
                link(nc.vector.tensor_reduce(FI[:], EQ[:].rearrange("p e n -> p n e"), AX_X, ALU.max))
                nc.vector.tensor_tensor(OH[c][:], rev, FI[:].unsqueeze(1).broadcast_to((P, NE, NT)),
                                        ALU.is_equal).then_inc(s_oh, 1)
                if c + 1 < choices:
                    dve.wait_ge(s_oh, c + 1)
                    link(nc.vector.scalar_tensor_tensor(k.LOG[:], OH[c][:], -BIG, k.LOG[:], ALU.mult, ALU.add))
            for c in range(choices):
                dve.wait_ge(s_sig, c + 1)
                nc.vector.tensor_scalar(k.GATE[:, c], k.GATE[:, c], 0.5, 0.5, ALU.mult, ALU.add)
                dve.wait_ge(s_cnt, c + 1)
                within = ps[:, 1024 * c:1024 * c + 256].rearrange("p (e n) -> p e n", e=NE)
                total = ps[:, 1024 * c + 512:1024 * c + 768]
                link(nc.vector.tensor_tensor_scan(CI[:].rearrange("p e n -> p (e n)"), k.c("ones2"), total, 0.0,
                                                  ALU.mult, ALU.add))
                link(nc.vector.tensor_copy(ENDS[:], CI[:, :, NT - 1]))
                nc.vector.tensor_copy(OFF[:, 0:1], ZERO[:, 0:1])
                link(nc.vector.tensor_copy(OFF[:, 1:NE], ENDS[:, 0:NE - 1]))
                link(nc.vector.tensor_tensor(ENDS[:], ENDS[:], OFF[:], ALU.subtract))
                link(nc.vector.tensor_tensor(GT[:], ENDS[:].unsqueeze(2).broadcast_to((P, NE, NT)),
                                             k.c("m128").unsqueeze(1).broadcast_to((P, NE, NT)), ALU.is_gt))
                link(nc.vector.tensor_reduce(NTL[:], GT[:], AX_X, ALU.add))
                link(nc.vector.tensor_tensor_scan(START[:], k.c("ones2")[:, 0:NE], NTL[:], 0.0, ALU.mult, ALU.add))
                link(nc.vector.tensor_tensor(START[:], START[:], NTL[:], ALU.subtract))
                link(nc.vector.scalar_tensor_tensor(OFF[:], START[:], float(P), OFF[:], ALU.mult, ALU.subtract))
                link(nc.vector.tensor_tensor(CI[:].rearrange("p e n -> p (e n)"), CI[:].rearrange("p e n -> p (e n)"),
                                             total, ALU.subtract))
                link(nc.vector.tensor_tensor(POSF[:], CI[:], within, ALU.add))
                link(nc.vector.tensor_tensor(POSF[:], POSF[:], OFF[:].unsqueeze(2).broadcast_to((P, NE, NT)), ALU.add))
                link(nc.vector.tensor_tensor(POSF[:], POSF[:], OH[c][:], ALU.mult))
                link(nc.vector.tensor_reduce(POS1[:], POSF[:].rearrange("p e n -> p n e"), AX_X, ALU.add))
                nc.vector.tensor_copy(k.POS[:, c], POS1[:])
                link(nc.vector.tensor_tensor(TE[:], START[0:1, 1:NE].unsqueeze(1).broadcast_to((1, TILES, NE - 1)),
                                             k.c("tile")[0:1].unsqueeze(2).broadcast_to((1, TILES, NE - 1)), ALU.is_le))
                link(nc.vector.tensor_reduce(TEF[:], TE[:], AX_X, ALU.add))
                link(nc.vector.tensor_tensor(TEF[:], TEF[:], k.c("octal")[0:1], ALU.mult))
                link(nc.vector.tensor_reduce(TED[:], TEF[:].rearrange("p (n i) -> p n i", i=FLOW), AX_X, ALU.add))
                link(nc.vector.tensor_copy(k.TEX[:, c], TED[:]))

        @block.scalar
        def _(act):
            for c in range(choices):
                act.wait_ge(s_mx, c + 1)
                nc.scalar.activation(k.GATE[:, c], MX[c][:], ACT.Tanh, scale=0.5).then_inc(s_sig, 1)

        @block.tensor
        def _(pe):
            for c in range(choices):
                pe.wait_ge(s_oh, c + 1)
                oh = OH[c][:].rearrange("p e n -> p (e n)")
                nc.tensor.matmul(ps[:, 1024 * c:1024 * c + 256], k.c("ahead"), oh, start=True, stop=True)
                nc.tensor.matmul(ps[:, 1024 * c + 512:1024 * c + 768], k.c("ones"), oh, start=True,
                                 stop=True).then_inc(s_cnt, 1)


FLOW = 8
SENDS = 4


def experts(nc, sb, ps, sem, dram, k, layer, choices):
    W1, WD, X, ACC = k.W1, k.WD, k.X, k.ACC
    XF = k.XF if layer == 0 else k.X
    xs, ys = dram["sorted"], dram["expert_out"]
    ZS = sb("ZS", [P, SENDS, D])
    IX = sb("IX", [P, SENDS, 1], U32)
    XG = sb("XG", [P, FLOW, D])
    XGT = sb("XGT", [P, FLOW, P])
    SG = sb("SG", [P, FLOW, FF])
    HG = sb("HG", [P, FLOW, FF])
    HT = sb("HT", [P, FLOW, 2, P])
    OG = sb("OG", [P, FLOW, D])
    SS = sb("SS", [P, SLOTS, 2, 512])
    HS = sb("HS", [P, SLOTS, 2, 512])
    YB = sb("YB", [P, FLOW, D])
    IXB = sb("IXB", [P, FLOW, 1], U32)
    WX = sb("WX", [P, FLOW, D])
    BN = sb("BN", [P, FLOW, 6])
    MV = sb("MV", [P, FLOW, 2])
    slots, turns = range(SLOTS), UNITS // SLOTS
    sends, flow = NT // SENDS, TILES // FLOW

    def one(t, n):
        return t[:, bass.ds(n, 1), :].rearrange("p a d -> p (a d)")

    s_z, s_sc, s_free = ([sem(f"{n}{p}") for p in range(SENDS)] for n in ("row_scaled", "row_out", "row_slot_free"))
    s_gu, s_si, s_h, s_dn, s_acc = ([sem(f"{n}{p}") for p in slots] for n in (
        "gate_up", "silu", "shared_h", "shared_down", "accumulated"))
    with nc.Block() as block:
        @block.sync
        def _(sp):
            ahead(sp, s_free)
            with sp.Fori(0, sends) as j:
                for p in range(SENDS):
                    sp.wait_ge(s_sc[p], 16 * (j + 1))
                    sp.sem_inc(s_free[p], 1)

        @block.gpsimd
        def _(pool):
            with pool.Fori(0, sends) as j:
                for p in range(SENDS):
                    pool.wait_ge(s_z[p], j + 1)
                    alone(pool)
                    nc.gpsimd.indirect_dma_start(out=xs[0], out_offset=bass.IndirectOffsetOnAxis(ap=IX[:, p], axis=0),
                                                 in_=ZS[:, p], in_offset=None).then_inc(s_sc[p], 16)
            for p in range(SENDS):
                pool.wait_ge(s_sc[p], 16 * sends)

        @block.vector
        def _(dve):
            ahead(dve, s_acc)
            with dve.Fori(0, turns) as j:
                for p in slots:
                    dve.wait_ge(s_si[p], j + 1)
                    nc.vector.tensor_tensor(HS[:, p], SS[:, p], ps[:, 2048 * p + 1024:2048 * p + 2048].rearrange(
                        "p (c t) -> p c t", c=2), ALU.mult).then_inc(s_h[p], 1)
                for p in slots:
                    dve.wait_ge(s_dn[p], j + 1)
                    t = bass.ds((turns * p + j) * 4, 4)
                    nc.vector.scalar_tensor_tensor(
                        ACC[:, t, :], X[:, t, :], 2.0 if layer == 0 else 1.0,
                        ps[:, 2048 * p:2048 * p + 512].rearrange("p (t d) -> p t d", d=D), ALU.mult,
                        ALU.add).then_inc(s_acc[p], 1)

        @block.scalar
        def _(act):
            with act.Fori(0, turns) as j:
                for p in slots:
                    for i in range(SENDS):
                        n = SENDS * SLOTS * j + SENDS * p + i
                        act.wait_ge(s_free[i], SLOTS * j + p + 1)
                        nc.scalar.activation(IX[:, i], k.POS[:, 0, bass.ds(n, 1)], ACT.Copy)
                        nc.scalar.activation(ZS[:, i], one(XF, n), ACT.Copy,
                                             scale=k.GATE[:, 0, bass.ds(n, 1)]).then_inc(s_z[i], 1)
                    act.wait_ge(s_gu[p], j + 1)
                    act.wait_ge(s_acc[p], j + 1)
                    nc.scalar.activation(SS[:, p], ps[:, 2048 * p:2048 * p + 1024].rearrange("p (c t) -> p c t", c=2),
                                         ACT.Silu).then_inc(s_si[p], 1)

        @block.tensor
        def _(pe):
            pe.wait_ge(k.s_w[layer], 32)
            with pe.Fori(0, turns) as j:
                for p in slots:
                    pe.wait_ge(s_acc[p], j + 1)
                    for i in range(4):
                        last = nc.tensor.matmul(ps[:, 2048 * p + 512 * i:2048 * p + 512 * i + 512],
                                                W1[:, NE, i * P:i * P + P],
                                                k.XNT[:, bass.ds((turns * p + j) * 512, 512)], start=True, stop=True)
                    last.then_inc(s_gu[p], 1)
                for p in slots:
                    pe.wait_ge(s_h[p], j + 1)
                    for t in range(4):
                        for f in range(2):
                            last = nc.tensor.matmul(ps[:, 2048 * p + P * t:2048 * p + P * t + P],
                                                    HS[:, p, f, P * t:P * t + P], WD[:, NE, f], start=(f == 0),
                                                    stop=(f == 1))
                    last.then_inc(s_dn[p], 1)

    for c in range(choices):
        s_ld, s_xt, s_xc, s_gu, s_si, s_h, s_ht, s_hc, s_dn, s_og, s_st = ([sem(f"{n}{c}_{p}") for p in range(FLOW)] for n in (
            "rows_in", "rows_turned", "rows_kept", "e_gate_up", "e_silu", "e_h", "h_turned", "h_kept", "e_down",
            "e_out", "e_stored")) if c == 0 else k.flow_sems
        k.flow_sems = (s_ld, s_xt, s_xc, s_gu, s_si, s_h, s_ht, s_hc, s_dn, s_og, s_st)
        s_prep, s_out, s_back = sem(f"pool_links{c}"), sem(f"next_out{c}"), sem(f"first_back{c}")
        base = c * flow

        def bank(p, a=0, z=512):
            return ps[:, p * 512 + a:p * 512 + z]

        with nc.Block() as block:
            @block.sync
            def _(sp):
                def load(j, p):
                    sp.dma_start(XG[:, p], xs[c][bass.ds((j - base) * (FLOW * P) + p * P, P), :]).then_inc(s_ld[p], 16)

                def store(j, p):
                    sp.wait_ge(s_og[p], j + 2)
                    sp.dma_start(ys[c][bass.ds((j - base) * (FLOW * P) + p * P, P), :], OG[:, p]).then_inc(s_st[p], 16)

                for p in range(FLOW):
                    load(base, p)
                with sp.Fori(base, base + flow - 1) as j:
                    for p in range(FLOW):
                        sp.wait_ge(s_xt[p], j + 2)
                        load(j + 1, p)
                    for p in range(FLOW):
                        store(j, p)
                for p in range(FLOW):
                    store(base + flow - 1, p)
                for p in range(FLOW):
                    sp.wait_ge(s_st[p], 16 * (base + flow + 1))

            @block.gpsimd
            def _(pool):
                if c + 1 < choices:
                    with pool.Fori(0, sends) as n:
                        for i in range(SENDS):
                            t = n * SENDS + i
                            nc.gpsimd.tensor_tensor(ZS[:, i], one(XF, t), k.GATE[:, c + 1, bass.ds(t, 1)].broadcast_to((P, D)),
                                                    ALU.mult)
                            nc.gpsimd.tensor_copy(IX[:, i], k.POS[:, c + 1, bass.ds(t, 1)]).then_inc(s_prep, 1)
                        for i in range(SENDS):
                            pool.wait_ge(s_prep, SENDS * n + i + 1)
                            alone(pool)
                            nc.gpsimd.indirect_dma_start(out=xs[c + 1], out_offset=bass.IndirectOffsetOnAxis(ap=IX[:, i], axis=0),
                                                         in_=ZS[:, i], in_offset=None).then_inc(s_out, 16)
                        pool.wait_ge(s_out, 16 * SENDS * (n + 1))
                if c:
                    with pool.Fori(0, sends) as n:
                        for i in range(SENDS):
                            nc.gpsimd.tensor_copy(IX[:, i], k.POS[:, c - 1, bass.ds(n * SENDS + i, 1)]).then_inc(s_prep, 1)
                        for i in range(SENDS):
                            pool.wait_ge(s_prep, 2 * SENDS * n + i + 1)
                            alone(pool)
                            nc.gpsimd.indirect_dma_start(out=ZS[:, i], out_offset=None, in_=ys[c - 1],
                                                         in_offset=bass.IndirectOffsetOnAxis(ap=IX[:, i], axis=0)
                                                         ).then_inc(s_back, 16)
                        pool.wait_ge(s_back, 16 * SENDS * (n + 1))
                        for i in range(SENDS):
                            t = n * SENDS + i
                            nc.gpsimd.tensor_tensor(one(ACC, t), one(ACC, t), ZS[:, i], ALU.add).then_inc(s_prep, 1)
                        pool.wait_ge(s_prep, 2 * SENDS * (n + 1))

            @block.vector
            def _(dve):
                if c == 0:
                    ahead(dve, s_og)
                with dve.Fori(base, base + flow) as j:
                    for p in range(FLOW):
                        dve.wait_ge(s_xt[p], j + 2)
                        nc.vector.tensor_copy(XGT[:, p], bank(p, 0, P)).then_inc(s_xc[p], 1)
                    for p in range(FLOW):
                        dve.wait_ge(s_si[p], j + 1)
                        nc.vector.tensor_tensor(HG[:, p], SG[:, p], bank(p, FF, 2 * FF), ALU.mult).then_inc(s_h[p], 1)
                    for p in range(FLOW):
                        dve.wait_ge(s_dn[p], j + 1)
                        dve.wait_ge(s_st[p], 16 * (j + 1))
                        nc.vector.tensor_copy(OG[:, p], bank(p, 2 * P, 3 * P)).then_inc(s_og[p], 1)

            @block.scalar
            def _(act):
                if c == 0:
                    ahead(act, s_xt)
                    ahead(act, s_st, 16)
                with act.Fori(base, base + flow) as j:
                    for p in range(FLOW):
                        act.wait_ge(s_gu[p], j + 1)
                        nc.scalar.activation(SG[:, p], bank(p, 0, FF), ACT.Silu).then_inc(s_si[p], 1)
                    for p in range(FLOW):
                        act.wait_ge(s_ht[p], j + 1)
                        nc.scalar.activation(HT[:, p].rearrange("p c t -> p (c t)"), bank(p, 0, 2 * P),
                                             ACT.Copy).then_inc(s_hc[p], 1)

            @block.tensor
            def _(pe):
                with pe.Fori(base, base + flow) as j:
                    digits = nc.tensor.value_load(k.TEX[0:1, c, bass.ds(j - base, 1)], min_val=0,
                                                  max_val=NE ** FLOW - 1)
                    which = [(digits >> (3 * p)) & (NE - 1) for p in range(FLOW)]
                    for p in range(FLOW):
                        pe.wait_ge(s_ld[p], 16 * (j + 1))
                        pe.wait_ge(s_og[p], j + 1)
                        nc.tensor.transpose(bank(p, 0, P), XG[:, p], k.c("ident")).then_inc(s_xt[p], 1)
                    for p in range(FLOW):
                        pe.wait_ge(s_xc[p], j + 1)
                        nc.tensor.matmul(bank(p), XGT[:, p], W1[:, bass.ds(which[p], 1), :].rearrange("p a f -> p (a f)"),
                                         start=True, stop=True).then_inc(s_gu[p], 1)
                    for p in range(FLOW):
                        pe.wait_ge(s_h[p], j + 1)
                        for f in range(2):
                            last = nc.tensor.transpose(bank(p, f * P, P + f * P), HG[:, p, f * P:f * P + P], k.c("ident"))
                        last.then_inc(s_ht[p], 1)
                    for p in range(FLOW):
                        pe.wait_ge(s_hc[p], j + 1)
                        for f in range(2):
                            last = nc.tensor.matmul(bank(p, 2 * P, 3 * P), HT[:, p, f],
                                                    WD[:, bass.ds(which[p], 1), f].rearrange("p a f -> p (a f)"),
                                                    start=(f == 0), stop=(f == 1))
                        last.then_inc(s_dn[p], 1)

    s_ix, s_back, s_sum, s_x = ([sem(f"{n}{p}") for p in range(FLOW)] for n in ("places", "rows_back", "rows_added", "x_normed"))
    s_link, s_var, s_rstd = sem("back_links"), sem("x_variance"), sem("x_rstd")
    backs, c = NT // FLOW, choices - 1
    with nc.Block() as block:
        @block.gpsimd
        def _(pool):
            def rows(j, p):
                pool.wait_ge(s_ix[p], j + 1)
                pool.wait_ge(s_sum[p], j + 1)
                alone(pool)
                nc.gpsimd.indirect_dma_start(out=YB[:, p], out_offset=None, in_=ys[c],
                                             in_offset=bass.IndirectOffsetOnAxis(ap=IXB[:, p], axis=0)
                                             ).then_inc(s_back[p], 16)

            def rstd(j):
                pool.wait_ge(s_var, j + 1)
                nc.gpsimd.tensor_tensor(MV[:, :, 1], MV[:, :, 1], k.POWER[:, 0:FLOW], ALU.pow).then_inc(s_rstd, 1)

            for p in range(FLOW):
                rows(0, p)
            with pool.Fori(0, backs - 1) as j:
                for p in range(FLOW):
                    rows(j + 1, p)
                    if p == FLOW // 2 - 1:
                        rstd(j)
            rstd(backs - 1)

        @block.sync
        def _(sp):
            if layer == 1:
                out = dram["out"].rearrange("b (t p) d -> p (b t) d", p=P)
                with sp.Fori(0, backs) as j:
                    for p in range(FLOW):
                        sp.wait_ge(s_x[p], j + 1)
                    alone(sp)
                    at = bass.ds(FLOW * j, FLOW)
                    sp.dma_start(out[:, at, :], X[:, at, :]).then_inc(k.s_out, 16)
                sp.wait_ge(k.s_out, 16 * backs)

        @block.scalar
        def _(act):
            with act.Fori(0, backs) as j:
                for p in range(FLOW):
                    act.wait_ge(s_sum[p], j + 1)
                    nc.scalar.activation(IXB[:, p], k.POS[:, c, bass.ds(FLOW * j + p, 1)], ACT.Copy).then_inc(s_ix[p], 1)

        @block.vector
        def _(dve):
            ahead(dve, s_sum)
            with dve.Fori(0, backs) as j:
                link = Links(dve, s_link, 2, j)
                for p in range(FLOW):
                    dve.wait_ge(s_back[p], 16 * (j + 1))
                    nc.vector.tensor_tensor(WX[:, p], YB[:, p], one(ACC, FLOW * j + p), ALU.add).then_inc(s_sum[p], 1)
                for p in range(FLOW):
                    dve.wait_ge(s_sum[p], j + 2)
                    last = nc.vector.bn_stats(BN[:, p], WX[:, p])
                link(last)
                alone(dve)
                for p in range(FLOW):
                    last = nc.vector.bn_aggr(MV[:, p], BN[:, p])
                link(last)
                nc.vector.tensor_scalar(MV[:, :, 1], MV[:, :, 1], EPS, None, ALU.add).then_inc(s_var, 1)
                dve.wait_ge(s_rstd, j + 1)
                for p in range(FLOW):
                    nc.vector.tensor_scalar(one(X, FLOW * j + p), WX[:, p], MV[:, p, 0:1], MV[:, p, 1:2],
                                            ALU.subtract, ALU.mult).then_inc(s_x[p], 1)
                dve.wait_ge(s_x[FLOW - 1], j + 1)
                link.close()


AH, AD = 16, 8
PAIRS = [(0, 0), (0, 1), (0, 2), (1, 0), (1, 1), (2, 0)]
HROWS = AD * len(PAIRS) + 6
MROW = 2 * HROWS


def slope_parts(h):
    return 1 if h % 2 else 2


def slope_at(h):
    return h // 2 * 3 + (2 if h % 2 else 0)


def qkv(nc, sb, ps, sem, dram, k):
    XS4 = sb("AXS4", [P, SLOTS, 4, D])
    XTS = sb("XTS", [P, SLOTS, 512])
    QF = sb("QF", [P, SLOTS, 2, 512])
    WQ = sb("WQ", [P, 3 * D])
    BQ = sb("BQ", [P, 2])
    BV = sb("BV", [P, D])
    slots, turns = range(SLOTS), UNITS // SLOTS
    s_w, s_one, s_bq = sem("qkv_loaded"), sem("ones_set"), sem("bias_scaled")
    s_b = [sem(f"attn_consts_loaded{n}") for n in range(2)]
    s_link = sem("qkv_links")

    def two(name):
        return [sem(f"{name}{p}") for p in slots]

    s_x, s_tr, s_xt, s_qk, s_v, s_qf, s_vx, s_parts = (two(n) for n in (
        "a_tokens", "a_turned", "a_turned_kept", "qk_psum", "v_psum", "qk_kept", "v_kept", "qk_parts"))

    def bank(p, n, a=0, z=512):
        return ps[:, (4 * p + n) * 512 + a:(4 * p + n) * 512 + z]

    with nc.Block() as block:
        @block.sync
        def _(sp):
            sp.dma_start(WQ[:], dram["wqkv"]).then_inc(s_w, 16)
            sp.dma_start(BQ[:], dram["bqk"]).then_inc(s_w, 16)
            sp.dma_start(BV[:], dram["bv"]).then_inc(s_w, 16)
            for n in range(2):
                for p in slots:
                    sp.dma_start(k.QA[:, p, :, :, n * T:n * T + T], dram["qrows"]).then_inc(s_b[n], 16)
                    sp.dma_start(k.KA[:, p, :, n * T:n * T + T], dram["krows"]).then_inc(s_b[n], 16)
            sp.dma_start(k.SI[:], dram["slopes"]).then_inc(s_b[1], 16)
            sp.dma_start(k.DL[:], dram["ramps"]).then_inc(s_b[1], 16)
            sp.dma_start(k.WP[:], dram["wproj"]).then_inc(s_b[1], 16)
            sp.wait_ge(s_b[0], 16 * 2 * SLOTS)
            sp.wait_ge(s_parts[0], 2)
            for p in slots:
                copy_rows(sp, k, p, 0, range(len(PAIRS)), k.s_rows[p])
            load_experts(sp, dram, k, 1)
            sp.wait_ge(s_b[1], 16 * (2 * SLOTS + 3))

        @block.gpsimd
        def _(pool):
            nc.gpsimd.memset(k.VX[:], 1.0).then_inc(s_one, 1)
            with pool.Fori(0, turns) as j:
                for p in slots:
                    pool.wait_ge(s_tr[p], j + 1)
                    nc.gpsimd.tensor_copy(XS4[:, p], k.X[:, bass.ds((turns * p + j) * 4, 4), :]).then_inc(s_x[p], 1)

        @block.vector
        def _(dve):
            dve.wait_ge(s_w, 48)
            nc.vector.tensor_scalar(BQ[:, 0:1], BQ[:, 0:1], AD ** -0.5, None, ALU.mult).then_inc(s_bq, 1)
            dve.wait_ge(s_one, 1)
            ahead(dve, s_vx + s_parts)
            with dve.Fori(0, turns) as j:
                link = Links(dve, s_link, 2 * SLOTS, j)
                for p in slots:
                    dve.wait_ge(s_v[p], j + 2)
                    for t in range(4):
                        last = nc.vector.tensor_tensor(
                            k.VX[:, bass.ds((turns * p + j) * 4 + t, 1), :, 0:AD].rearrange("p a h d -> p (a h) d"),
                            bank(p, 3, t * P, t * P + P).rearrange("p (h d) -> p h d", h=AH),
                            BV[:].rearrange("p (h d) -> p h d", h=AH), ALU.add)
                    last.then_inc(s_vx[p], 1)
                    dve.wait_ge(s_qf[p], j + 2)
                    cols = bass.ds((turns * p + j) * 512, 512)
                    link(nc.vector.tensor_tensor(QF[:, p], QF[:, p], k.QK[:, :, 0, cols], ALU.subtract))
                    link(nc.vector.tensor_copy(k.QK[:, :, 1, cols], QF[:, p]))
                    nc.vector.tensor_tensor(k.QK[:, :, 2, cols], QF[:, p], k.QK[:, :, 1, cols],
                                            ALU.subtract).then_inc(s_parts[p], 1)
                link.close()

        @block.scalar
        def _(act):
            act.wait_ge(s_bq, 1)
            ahead(act, s_xt + s_qf)
            with act.Fori(0, turns) as j:
                for p in slots:
                    act.wait_ge(s_tr[p], j + 2)
                    act.wait_ge(s_v[p], j + 1)
                    nc.scalar.activation(XTS[:, p], bank(p, 0), ACT.Copy).then_inc(s_xt[p], 1)
                for p in slots:
                    act.wait_ge(s_qk[p], j + 1)
                    act.wait_ge(s_parts[p], j + 1)
                    for i, scale in enumerate((AD ** -0.5, 1.0)):
                        for o in (QF[:, p, i], k.QK[:, i, 0, bass.ds((turns * p + j) * 512, 512)]):
                            last = nc.scalar.activation(o, bank(p, 1 + i), ACT.Identity, bias=BQ[:, i:i + 1], scale=scale)
                    last.then_inc(s_qf[p], 1)

        @block.tensor
        def _(pe):
            pe.wait_ge(s_w, 48)
            ahead(pe, s_tr + s_v)
            with pe.Fori(0, turns) as j:
                for p in slots:
                    pe.wait_ge(s_x[p], j + 1)
                    pe.wait_ge(s_xt[p], j + 1)
                    for t in range(4):
                        last = nc.tensor.transpose(bank(p, 0, P * t, P * t + P), XS4[:, p, t], k.c("ident"))
                    last.then_inc(s_tr[p], 1)
                for p in slots:
                    pe.wait_ge(s_xt[p], j + 2)
                    pe.wait_ge(s_qf[p], j + 1)
                    pe.wait_ge(s_vx[p], j + 1)
                    for i in range(2):
                        last = nc.tensor.matmul(bank(p, 1 + i), WQ[:, i * D:i * D + D], XTS[:, p], start=True, stop=True)
                    last.then_inc(s_qk[p], 1)
                    for t in range(4):
                        last = nc.tensor.matmul(bank(p, 3, P * t, P * t + P), XTS[:, p, P * t:P * t + P], WQ[:, 2 * D:3 * D],
                                                start=True, stop=True)
                    last.then_inc(s_v[p], 1)


def copy_rows(engine, k, p, n, which, s):
    cols = bass.ds((2 * n + p) * T, T)
    for hh in range(2):
        for c in which:
            r = HROWS * hh + AD * c
            a, b = PAIRS[c]
            engine.dma_start(k.QA[r:r + AD, p, :, hh, bass.ds((n & 1) * T, T)],
                             k.QK[64 * hh:64 * hh + 64, 0, a, cols]).then_inc(s, 16)
            engine.dma_start(k.KA[r:r + AD, p, :, bass.ds((n & 1) * T, T)],
                             k.QK[64 * hh:64 * hh + 64, 1, b, cols]).then_inc(s, 16)


def attention(nc, sb, ps, sem, k):
    PR = k.XNT[:].rearrange("p (q h c) -> p q h c", q=2, h=4)
    MX = sb("MXA", [P, SLOTS, TT, AH])
    MR = sb("MRA", [P, SLOTS, TT, AH])
    MP = sb("MPA", [P, SLOTS, TT, 3, AH], BF16)
    MT = sb("MTA", [3 * AH, SLOTS, T], BF16)
    OS = sb("OSA", [P, SLOTS, 4 * T])
    RC = sb("RCA", [P, SLOTS, TT, AH])
    YA = sb("YAA", [P, SLOTS, TT, D])
    YAT = sb("YATA", [P, SLOTS, T])
    WX = sb("WXA", [P, SLOTS, TT, D])
    BN = sb("BNA", [P, SLOTS, TT, 6])
    MV = sb("MVA", [P, SLOTS, TT, 2])
    VS = sb("VSA", [P, SLOTS, TT, AH, AD + 1])
    X = k.X
    psb = ps[:].bitcast(BF16)
    slots, turns = range(SLOTS), B // SLOTS
    quads = AH // 4
    s_s1, s_mx, s_s2, s_ex = sem("scores"), sem("maxima"), sem("scores_turned"), sem("exps")

    def two(name):
        return [sem(f"{name}{p}") for p in slots]

    s_q, s_qs, s_mp, s_mt, s_mc, s_m, s_pv, s_vs = (two(n) for n in (
        "qk_rows", "qk_rows_too", "max_parts", "max_turned", "max_kept", "max_rows", "values_mixed", "v_slot"))
    s_os, s_ot, s_ya, s_yt, s_yc, s_pj, s_var, s_rs = (two(n) for n in (
        "mixed_kept", "mixed_turned", "y_heads", "yh_turned", "yh_kept", "projected", "a_variance", "a_rstd"))
    s_lm, s_lp, s_xb = two("max_links"), two("post_links"), two("x_biased")
    SP_PAIRS = len(PAIRS) - 2

    LEAD = 8
    TURN_MAX, LAST_MIX, TURNED, Y_TURNED, PROJECT = 2, LEAD, LEAD + 3, LEAD + 5, LEAD + 6

    def before(p, n):
        return (0, n) if p else (1, n - 1)

    def seq(p, n):
        return 2 * n + p

    def bank(which, h):
        at = 1024 * which + 512 * (h % 2)
        return ps[:, at:at + 512]

    def obank(p, a=0, z=1024):
        return ps[:, 2048 + 1024 * p + a:2048 + 1024 * p + z]

    def mixed(p, quad, n):
        return quads * n + quads + quad + 1

    on_sync, on_gpsimd = range(SP_PAIRS), range(SP_PAIRS, len(PAIRS))

    with nc.Block() as block:
        @block.sync
        def _(sp):
            def maxima(p, n):
                sp.wait_ge(s_mc[p], n + 1)
                alone(sp)
                sp.dma_start(k.QA[MROW:MROW + 3, p, :, :, bass.ds((n & 1) * T, T)],
                             MT[:, p]).then_inc(s_m[p], 16)

            for p in slots:
                copy_rows(sp, k, p, 1, on_sync, s_q[p])
            maxima(0, 0)
            with sp.Fori(0, turns - 2) as j:
                for p in slots:
                    maxima(*before(p, j + 1))
                    sp.wait_ge(s_s2, AH * (seq(p, j) + 1))
                    alone(sp)
                    copy_rows(sp, k, p, j + 2, on_sync, s_q[p])
            maxima(1, turns - 2)
            for p in slots:
                maxima(p, turns - 1)

        @block.gpsimd
        def _(pool):
            def values(p, n, first=False):
                if not first:
                    pool.wait_ge(s_pv[p], mixed(p, quads - 1, n - 1))
                nc.gpsimd.tensor_copy(VS[:, p], k.VX[:, bass.ds(seq(p, n) * TT, TT), :, :]).then_inc(s_vs[p], 1)
                xs = X[:, bass.ds(TT * seq(p, n), TT), :]
                nc.gpsimd.tensor_tensor(xs, xs, k.WP[:, D:2 * D].unsqueeze(1).broadcast_to((P, TT, D)),
                                        ALU.add).then_inc(s_xb[p], 1)

            def rstd(p, n):
                pool.wait_ge(s_var[p], n + 2)
                nc.gpsimd.tensor_tensor(MV[:, p, :, 1:2], MV[:, p, :, 1:2], k.POWER[:, 0:TT].unsqueeze(2),
                                        ALU.pow).then_inc(s_rs[p], 1)

            for p in slots:
                values(p, 0, first=True)
            for p in slots:
                copy_rows(pool, k, p, 1, on_gpsimd, s_qs[p])
            with pool.Fori(0, turns - 2) as j:
                for p in slots:
                    values(p, j + 1)
                    rstd(p, j)
                    pool.wait_ge(s_s2, AH * (seq(p, j) + 1))
                    alone(pool)
                    copy_rows(pool, k, p, j + 2, on_gpsimd, s_qs[p])
            for n in (turns - 2, turns - 1):
                for p in slots:
                    if n == turns - 2:
                        values(p, n + 1)
                    rstd(p, n)

        @block.vector
        def _(dve):
            def reduced(p, n, h):
                dve.wait_ge(s_s1, AH * seq(p, n) + h + 1)
                nc.vector.tensor_reduce(MX[:, p, :, h], bank(0, h).rearrange("p (t s) -> p t s", t=TT),
                                        AX_X, ALU.max).then_inc(s_mx, 1)

            def parts(p, n):
                link = Links(dve, s_lm[p], 3, n)
                dve.wait_ge(s_mx, AH * (seq(p, n) + 1))
                link(nc.vector.tensor_scalar(MP[:, p, :, 0], MX[:, p], -1.0, None, ALU.mult))
                link(nc.vector.scalar_tensor_tensor(MR[:, p], MX[:, p], -1.0, MP[:, p, :, 0], ALU.mult, ALU.subtract))
                link(nc.vector.tensor_copy(MP[:, p, :, 1], MR[:, p]))
                nc.vector.tensor_tensor(MP[:, p, :, 2], MR[:, p], MP[:, p, :, 1], ALU.subtract).then_inc(s_mp[p], 1)
                link.close()

            def heads(p, n, link):
                dve.wait_ge(s_ot[p], n + 1)
                o = obank(p).rearrange("p (t h c) -> p t h c", t=TT, h=AH)
                for t in range(TT):
                    last = nc.vector.reciprocal(RC[:, p, t], o[:, t, :, AD])
                link(last)
                for t in range(TT):
                    last = nc.vector.tensor_tensor(YA[:, p, t].rearrange("p (h d) -> p h d", h=AH), o[:, t, :, 0:AD],
                                                   spread(RC[:, p, t], AD), ALU.mult)
                last.then_inc(s_ya[p], 1)

            def sums(p, n, link):
                xs = X[:, bass.ds(TT * seq(p, n), TT), :]
                dve.wait_ge(s_xb[p], n + 1)
                dve.wait_ge(s_pj[p], n + 1)
                link(nc.vector.tensor_tensor(WX[:, p], xs, obank(p, 512, 768).rearrange("p (t d) -> p t d", d=D), ALU.add))
                for t in range(TT):
                    last = nc.vector.bn_stats(BN[:, p, t], WX[:, p, t])
                link(last)
                alone(dve)
                for t in range(TT):
                    last = nc.vector.bn_aggr(MV[:, p, t], BN[:, p, t])
                link(last)
                nc.vector.tensor_scalar(MV[:, p, :, 1:2], MV[:, p, :, 1:2], EPS, None, ALU.add).then_inc(s_var[p], 1)

            def normed(p, n):
                dve.wait_ge(s_rs[p], n + 1)
                for t in range(TT):
                    nc.vector.tensor_scalar(X[:, bass.ds(TT * seq(p, n) + t, 1), :].rearrange("p a d -> p (a d)"),
                                            WX[:, p, t], MV[:, p, t, 0:1], MV[:, p, t, 1:2], ALU.subtract, ALU.mult)

            def stage(p, n, maxima=True, turned=True, post=True, late=False):
                if turned:
                    parts(*before(p, n))
                link = Links(dve, s_lp[p], 4, n - 1)
                for h in range(AH):
                    if maxima:
                        reduced(p, n, h)
                    if h == 2 and late:
                        normed(*before(p, n - 1))
                    if post and h == TURNED:
                        heads(p, n - 1, link)
                    if post and h == PROJECT:
                        sums(p, n - 1, link)
                if post:
                    link.close()

            ahead(dve, s_var)
            for h in range(AH):
                reduced(0, 0, h)
            stage(1, 0, post=False)
            with dve.Fori(0, turns - 1) as j:
                stage(0, j + 1)
                stage(1, j + 1, late=True)
                normed(1, j)
            stage(0, turns, maxima=False)
            stage(1, turns, maxima=False, turned=False, late=True)
            normed(1, turns - 1)

        @block.scalar
        def _(act):
            def max_kept(p, n):
                act.wait_ge(s_mt[p], n + 1)
                nc.scalar.activation(MT[:, p], psb[0:3 * AH, 2 * (2048 + 1024 * p):2 * (2048 + 1024 * p) + T],
                                     ACT.Copy).then_inc(s_mc[p], 1)

            def exps(p, n, h):
                act.wait_ge(s_s2, AH * seq(p, n) + h + 1)
                if h >= 8:
                    act.wait_ge(s_pv[p], mixed(p, h // 4 - 2, n))
                else:
                    pb, nb = before(p, n)
                    act.wait_ge(s_pv[pb], mixed(pb, h // 4 + 2, nb))
                nc.scalar.activation(PR[:, h // 4 % 2, h % 4], bank(1, h), ACT.Exp).then_inc(s_ex, 1)

            def mixed_kept(p, n):
                act.wait_ge(s_pv[p], mixed(p, quads - 1, n))
                nc.scalar.activation(OS[:, p], obank(p), ACT.Copy).then_inc(s_os[p], 1)

            def y_kept(p, n):
                act.wait_ge(s_yt[p], n + 1)
                nc.scalar.activation(YAT[:, p], obank(p, 0, T), ACT.Copy).then_inc(s_yc[p], 1)

            def stage(p, n, tail=True, front=True):
                pb, nb = before(p, n)
                for i in range(AH):
                    if i < LEAD and tail:
                        exps(p, n - 1, AH - LEAD + i)
                    if i >= LEAD and front:
                        exps(pb, nb, i - LEAD)
                    if i == TURN_MAX + 1 and front:
                        max_kept(pb, nb)
                    if i == LAST_MIX + 1 and tail:
                        mixed_kept(p, n - 1)
                    if i == Y_TURNED and tail:
                        y_kept(p, n - 1)

            stage(1, 0, tail=False)
            with act.Fori(0, turns - 1) as j:
                stage(0, j + 1)
                stage(1, j + 1)
            stage(0, turns)
            stage(1, turns, front=False)

        @block.tensor
        def _(pe):
            def cols(n, a=0, z=T):
                return bass.ds((n & 1) * T + a, z - a)

            def pass1(p, n, h, first=False, wait=True):
                if h == 0 and first:
                    pe.wait_ge(k.s_rows[p], 16 * 4 * len(PAIRS))
                elif h == 0:
                    pe.wait_ge(s_q[p], 16 * 4 * len(on_sync) * n)
                    pe.wait_ge(s_qs[p], 16 * 4 * len(on_gpsimd) * n)
                if wait:
                    pe.wait_ge(s_mx, AH * seq(p, n) + h - 1)
                for t in range(TT):
                    o = bank(0, h)[:, T * t:T * t + T]
                    nc.tensor.matmul(o, k.QA[0:MROW, p, h // 2, h % 2, cols(n, t * P, t * P + P)],
                                     k.KA[0:MROW, p, h // 2, cols(n)], start=True, stop=False)
                    parts = slope_parts(h)
                    for a in range(parts):
                        last = nc.tensor.matmul(o[:, t * P:t * P + P], k.DL[:, 0], k.SI[:, slope_at(h) + a],
                                                start=False, stop=(a == parts - 1))
                last.then_inc(s_s1, 1)

            def pass2(p, n, h, wait=True):
                if h == 0:
                    pe.wait_ge(s_m[p], 16 * (n + 1))
                if wait:
                    pe.wait_ge(s_ex, AH * seq(p, n) + h - 1)
                for s in range(TT):
                    o = bank(1, h)[:, T * s:T * s + T]
                    nc.tensor.matmul(o, k.KA[0:MROW + 3, p, h // 2, cols(n, s * P, s * P + P)],
                                     k.QA[0:MROW + 3, p, h // 2, h % 2, cols(n)], start=True, stop=False)
                    parts = slope_parts(h)
                    for a in range(parts):
                        last = nc.tensor.matmul(o[:, s * P:s * P + P], k.DL[:, 1], k.SI[:, slope_at(h) + a],
                                                start=False, stop=(a == parts - 1))
                last.then_inc(s_s2, 1)

            def turn_max(p, n):
                pe.wait_ge(s_mp[p], n + 1)
                pe.wait_ge(s_var[p], n + 1)
                alone(pe)
                for t in range(TT):
                    at = 2 * (2048 + 1024 * p) + t * P
                    last = nc.tensor.transpose(psb[0:3 * AH, at:at + P], MP[:, p, t].rearrange("p a h -> p (a h)"), k.IDB[:])
                last.then_inc(s_mt[p], 1)

            def mix(p, n, quad):
                pe.wait_ge(s_ex, AH * seq(p, n) + 4 * quad + 4)
                if quad == 0:
                    pe.wait_ge(s_vs[p], n + 1)
                for s in range(TT):
                    for h in range(4):
                        last = nc.tensor.matmul(obank(p, quad * T, quad * T + T)[32 * h:32 * h + AD + 1],
                                                VS[:, p, s, 4 * quad + h], PR[:, quad % 2, h, s * T:s * T + T],
                                                start=(s == 0), stop=(s == TT - 1), tile_position=(0, 32 * h))
                last.then_inc(s_pv[p], 1)

            def turned(p, n):
                pe.wait_ge(s_os[p], n + 1)
                for t in range(TT):
                    for quad in range(quads):
                        last = nc.tensor.transpose(obank(p, t * 512 + quad * P, t * 512 + quad * P + P),
                                                   OS[:, p, quad * T + t * P:quad * T + t * P + P], k.c("ident"))
                last.then_inc(s_ot[p], 1)

            def y_turned(p, n):
                pe.wait_ge(s_ya[p], n + 1)
                for t in range(TT):
                    last = nc.tensor.transpose(obank(p, t * P, t * P + P), YA[:, p, t], k.c("ident"))
                last.then_inc(s_yt[p], 1)

            def project(p, n):
                pe.wait_ge(s_yc[p], n + 1)
                for t in range(TT):
                    o = obank(p, 512 + t * P, 512 + t * P + P)
                    last = nc.tensor.matmul(o, YAT[:, p, t * P:t * P + P], k.WP[:, 0:D], start=True, stop=True)
                last.then_inc(s_pj[p], 1)

            def stage(p, n, scores=True, tail=True, front=True):
                pb, nb = before(p, n)
                for i in range(AH):
                    if scores:
                        pass1(p, n, i, first=not tail)
                    if i < LEAD and tail:
                        h = AH - LEAD + i
                        pass2(p, n - 1, h)
                        if h % 4 == 1:
                            mix(p, n - 1, h // 4 - 1)
                    if i >= LEAD and front:
                        h = i - LEAD
                        pass2(pb, nb, h, wait=(tail or h >= 2))
                        if h % 4 == 1 and h > 1:
                            mix(pb, nb, h // 4 - 1)
                    if i == LAST_MIX and tail:
                        mix(p, n - 1, quads - 1)
                    if i == TURN_MAX and front:
                        turn_max(pb, nb)
                    if tail:
                        if i == TURNED:
                            turned(p, n - 1)
                        if i == Y_TURNED:
                            y_turned(p, n - 1)
                        if i == PROJECT:
                            project(p, n - 1)

            ahead(pe, s_pv, quads)
            for h in range(AH):
                pass1(0, 0, h, first=True, wait=h >= 2)
            stage(1, 0, tail=False)
            with pe.Fori(0, turns - 1) as j:
                stage(0, j + 1)
                stage(1, j + 1)
            stage(0, turns, scores=False)
            stage(1, turns, scores=False, front=False)


def staged(nc, tag, stage):
    with ExitStack() as ctx:
        sems = []

        def sem(name):
            sems.append(nc.alloc_semaphore(f"{tag}_{name}"))
            return sems[-1]

        stage(lambda name, shape, dtype=F32: ctx.enter_context(nc.sbuf_tensor(f"{tag}_{name}", shape, dtype)), sem)
        nc.all_engine_barrier()
        nc.clear_and_free_semaphores(sems)
        nc.all_engine_barrier()


def load_experts(sp, dram, k, layer):
    sp.dma_start(k.W1[:], dram["w1"][layer]).then_inc(k.s_w[layer], 16)
    sp.dma_start(k.WD[:].rearrange("p e f d -> p (e f d)"), dram["wd"][layer]).then_inc(k.s_w[layer], 16)


def attention_stage(nc, ps, dram, k):
    with ExitStack() as ctx:
        def sb(name, shape, dtype=F32):
            return ctx.enter_context(nc.sbuf_tensor(name, shape, dtype))

        k.QK = sb("QK", [P, 2, 3, NT * P], BF16)
        k.VX = sb("VX", [P, NT, AH, AD + 1])
        k.QA = sb("QA", [P, SLOTS, AH // 2, 2, 2 * T], BF16)
        k.KA = sb("KA_rows", [P, SLOTS, AH // 2, 2 * T], BF16)
        k.SI = sb("SI", [P, AH // 2 * 3, P], F16)
        k.DL = sb("DL", [P, 2, P], F16)
        k.WP = sb("WP", [P, 2 * D])
        staged(nc, "qkv", lambda sb, sem: qkv(nc, sb, ps, sem, dram, k))
        staged(nc, "attention", lambda sb, sem: attention(nc, sb, ps, sem, k))


def build(nc, dram):
    with ExitStack() as ctx:
        def sb(name, shape, dtype=F32):
            return ctx.enter_context(nc.sbuf_tensor(name, shape, dtype))

        def sem(name):
            return ctx.enter_context(nc.semaphore(name))

        k = Kept()
        ps = ctx.enter_context(nc.psum_tensor("ps", [P, 8 * 512], F32))
        k.X = sb("X", [P, NT, D])
        k.C = sb("C", [P, CONST_W])
        k.XNT = sb("XNT", [P, NT * P])
        k.POWER = sb("POWER", [P, 16])
        k.IDB = sb("IDB", [P, P], BF16)
        k.F = sb("F", [P, WF_W])
        k.s_w = [sem(f"experts_loaded{layer}") for layer in range(2)]
        k.s_out = sem("stored")
        k.s_rows = [sem(f"first_rows{p}") for p in range(SLOTS)]
        k.W1 = sb("W1", [P, NE + 1, 2 * FF])
        k.WD = sb("WD", [P, NE + 1, 2, D])
        with ExitStack() as inner:
            def own(name, shape, dtype=F32):
                return inner.enter_context(nc.sbuf_tensor(name, shape, dtype))

            k.W = own("W", [P, WA_W])
            k.LATER = own("LATER", [P, P], BF16)
            k.SEL = own("SEL", [96, TURNS * MH, T], BF16)
            k.CUMT = own("CUMT", [96, SLOTS, TT, P], BF16)
            k.NCUMT = own("NCUMT", [96, SLOTS, TT, P], BF16)
            k.DT = own("DT", [P, NT, MH])
            k.AT = own("AT", [P, P])
            k.VV = own("VV", [P, 2 * D])
            staged(nc, "prepare", lambda sb, sem: prepare(nc, sb, ps, sem, dram, k))
            staged(nc, "mamba", lambda sb, sem: mamba(nc, sb, ps, sem, k))
        for layer in range(2):
            choices = layer + 1
            if layer == 1:
                attention_stage(nc, ps, dram, k)
            with ExitStack() as inner:
                def own(name, shape, dtype=F32):
                    return inner.enter_context(nc.sbuf_tensor(f"{name}{layer}", shape, dtype))

                k.XF, k.ACC = own("XF", [P, NT, D]), own("ACC", [P, NT, D])
                k.LOG, k.GATE, k.POS = own("LOG", [P, NE, NT]), own("GATE", [P, 2, NT]), own("POS", [P, 2, NT], U32)
                k.TEX = own("TEX", [1, 2, TILES // FLOW], mybir.dt.int32)
                staged(nc, f"ffn_tokens{layer}", lambda sb, sem: ffn_tokens(nc, sb, ps, sem, k, layer))
                staged(nc, f"route{layer}", lambda sb, sem: route(nc, sb, ps, sem, k, layer, choices))
                staged(nc, f"experts{layer}", lambda sb, sem: experts(nc, sb, ps, sem, dram, k, layer, choices))


def constants(np):
    i, j = np.arange(P)[:, None], np.arange(P)[None]
    c = np.zeros((P, CONST_W), np.float32)

    def put(name, value):
        a, z = CONST[name]
        c[:value.shape[0], a:z] = value

    put("ident", np.eye(P))
    put("tri", (i <= j) * 1.0)
    put("ones", np.ones((P, P)))
    put("ones2", np.ones((P, NE * NT)))
    put("ahead", (i < j) * 1.0)
    put("eight", np.tile(NE - np.arange(NE), (P, 1)))
    put("m128", np.tile(P * np.arange(NT), (P, 1)))
    put("tile", np.tile(np.arange(TILES), (P, 1)))
    put("octal", np.tile(NE ** (np.arange(TILES) % FLOW), (P, 1)))
    put("later", (j < i) * -BIG)
    put("earlier", np.concatenate([(np.arange(T)[None] < i + P * t) * 1.0 for t in range(TT)], 1))
    put("slot", np.tile(np.arange(POOL), (P, 1)))
    r = np.arange(TURNS * 12)[:, None]
    put("sel", ((r // 12 == np.arange(TURNS * MH)[None] // MH) & (r % MH == np.arange(TURNS * MH)[None] % MH)) * 1.0)
    return c


def mamba_weights(np, g):
    def pad(a):
        return np.concatenate([a, np.zeros((P - a.shape[0], a.shape[1]), np.float32)]) if a.shape[0] < P else a

    w, f = {}, lambda n: np.asarray(g["L0_attn_" + n])
    w["inw"], w["dtw"] = f("in_w")[:768].T, f("in_w")[768:].T
    w["normw"] = f("norm_w")[:, None]
    w["convw"] = f("conv_w").reshape(4, P, TAPS).transpose(1, 0, 2).reshape(P, 16)
    w["convb"] = f("conv_b").reshape(4, P).T
    w["dtb"], w["alog"] = np.tile(f("dt_bias"), (P, 1)), np.tile(f("A_log"), (P, 1))
    w["dpar"] = np.repeat(f("D_param"), MP).reshape(2, P).T
    w["gnorm"] = f("gnorm_w").reshape(2, P).T
    w["outw"] = f("out_w").T.reshape(2, P, D).transpose(1, 0, 2).reshape(P, 2 * D)
    w["tapbc"] = np.broadcast_to(f("conv_w").reshape(4 * P, TAPS)[2 * P:].T.reshape(1, -1), (P, TAPS * 2 * P))
    w["w1"], w["w2"] = f("scorer_w1").T, f("scorer_w2").T
    w["summ"], w["qw"], w["kwt"], w["vwt"] = f("summ_w"), f("q_w"), f("k_w").T, f("v_w").T
    w["g1"], w["g2"] = f("gate_w")[:, :D].T, f("gate_w")[:, D:].T
    return np.ascontiguousarray(np.concatenate([pad(w[n]) for n in WA], 1))


def expert_weights(np, g):
    f = lambda n: np.asarray(g[n])
    g0 = np.concatenate([f("L0_ffn_gate_w"), f("L0_ffn_sh_gate")[None]])
    u0 = np.concatenate([f("L0_ffn_up_w"), f("L0_ffn_sh_up")[None]])
    d0 = np.concatenate([f("L0_ffn_down_w"), f("L0_ffn_sh_down")[None]])
    g1 = np.concatenate([f("L1_ffn_w_in_eDF"), f("L1_ffn_w_in_shared_FD").T[None]])
    u1 = np.concatenate([f("L1_ffn_w_swiglu_eDF"), f("L1_ffn_w_swiglu_FD").T[None]])
    d1 = np.concatenate([f("L1_ffn_w_out_eFD"), f("L1_ffn_w_out_shared_DF").T[None]])
    w1 = [np.concatenate([a, b], 2).transpose(1, 0, 2) for a, b in ((g0, u0), (g1, u1))]
    wd = [d.reshape(NE + 1, 2, P, D).transpose(2, 0, 1, 3).reshape(P, -1) for d in (d0, d1)]
    wf = np.concatenate([f("L0_ffn_router_w"), f("L1_ffn_router_DE"), np.tile(f("L0_ffn_ln_w"), (P, 1)),
                         np.tile(f("L0_ffn_ln_b"), (P, 1))], 1)
    return tuple(np.ascontiguousarray(a) for a in (np.stack(w1), np.stack(wd), wf))


def attention_constants(np, bf16):
    f32 = np.float32
    slope = np.array([2.0 ** (-0.5 * (h + 1)) for h in range(AH)]).astype(f32)
    s1 = slope.astype(bf16).astype(f32)
    s2 = (slope - s1).astype(bf16).astype(f32)
    s3 = slope - s1 - s2
    parts = np.stack([s1, s2, s3])
    at = np.arange(T, dtype=f32)
    last, first = (at >= P).astype(f32), (at < P).astype(f32)
    q = np.zeros((P, AH // 2, 2, T), f32)
    kk = np.zeros((P, AH // 2, T), f32)
    for h in range(AH):
        r = HROWS * (h % 2) + AD * len(PAIRS)
        for a in range(3):
            q[r + a, h // 2, h % 2], kk[r + a, h // 2] = -at * last, parts[a, h] * first
            q[r + 3 + a, h // 2, h % 2], kk[r + 3 + a, h // 2] = parts[a, h] * last, at * first
    kk[MROW:MROW + 3] = 1.0
    t1 = (slope * P).astype(np.float16)
    t2 = (slope * P - t1.astype(f32)).astype(np.float16)
    si = np.zeros((P, AH // 2 * 3, P), np.float16)
    for h in range(AH):
        for a in range(slope_parts(h)):
            si[:, slope_at(h) + a] = np.eye(P) * (t1, t2)[a][h]
    i, j = np.arange(P)[:, None], np.arange(P)[None]
    ramps = np.stack([np.minimum(i - j, 0), np.minimum(j - i, 0)], 1) / P
    return {"qrows": q.astype(bf16), "krows": kk.astype(bf16), "slopes": si, "ramps": ramps.astype(np.float16)}


def attention_weights(np, g):
    f = lambda n: np.asarray(g["L1_attn_" + n])
    order = np.arange(D).reshape(AH // 2, 2, AD).transpose(1, 2, 0).reshape(-1)
    w, b = f("W_qkv"), f("b_qkv")
    out = {"wqkv": np.concatenate([w[:, order], w[:, D + order], w[:, 2 * D:]], 1),
           "bqk": np.stack([b[order], b[D + order]], 1), "bv": np.tile(b[2 * D:], (P, 1)),
           "wproj": np.concatenate([f("W_proj"), np.tile(f("b_proj"), (P, 1))], 1)}
    return {n: np.ascontiguousarray(a) for n, a in out.items()}


def kernel(**inputs):
    import numpy as _np
    import concourse.bacc as _bacc
    from concourse import mybir as _mybir
    from concourse.bass_utils import run_bass_kernel_spmd as _run

    w1, wd, wf = expert_weights(_np, inputs)
    import ml_dtypes
    bf16 = ml_dtypes.bfloat16
    arrays = {"w1": w1, "wd": wd, "wf": wf, "x": _np.ascontiguousarray(inputs["L0_attn_x"]), "const": constants(_np), "wa": mamba_weights(_np, inputs)}
    arrays.update(attention_constants(_np, bf16))
    arrays.update(attention_weights(_np, inputs))
    nc = _bacc.Bacc("TRN2", target_bir_lowering=False, num_devices=1)
    dram = {n: nc.dram_tensor(n, a.shape, _mybir.dt.from_np(a.dtype), kind="ExternalInput").ap() for n, a in arrays.items()}
    for n in ("sorted", "expert_out"):
        dram[n] = [nc.dram_tensor(f"{n}{c}", (TILES * P, D), _mybir.dt.float32).ap() for c in range(2)]
    dram["out"] = nc.dram_tensor("out", (B, T, D), _mybir.dt.float32, kind="ExternalOutput").ap()
    build(nc, dram)
    r = _run(nc, [arrays], core_ids=[0])
    return r.results[0]["out"]
```
